# Optimizing a Trainium2 kernel written in Bass

```python
import numpy as np
import jax
import jax.numpy as jnp

def _softmax(x, axis=-1):
    return jax.nn.softmax(x, axis=axis)

def _gelu(x):
    return jax.nn.gelu(x, approximate=True)

def _silu(x):
    return jax.nn.silu(x)

def _sigmoid(x):
    return jax.nn.sigmoid(x)

def _layernorm(x, axis=-1, eps=1e-05):
    m = jnp.mean(x, axis=axis, keepdims=True)
    v = jnp.var(x, axis=axis, keepdims=True)
    return (x - m) / jnp.sqrt(v + eps)

def _scatter_add(tgt, idx, src, axis=0):
    return tgt.at[idx].add(src)

def _segment_sum(src, seg, n):
    return jax.ops.segment_sum(src, seg, n)
kernel_name = 'mk_xattn_ffn_d4_seqx_r4_c7e890'

def setup_inputs(seed: int=0):
    np.random.seed(seed)
    _w = jnp.asarray

    def _rec_inputs():
        import jax
        import jax.numpy as jnp
        _rk = jax.random.key(seed)
        x = -0.0002928 + 1 * jax.random.normal(jax.random.fold_in(_rk, 1), (2, 1024, 256), jnp.float32)
        _lenS = 1024 - jax.random.randint(jax.random.fold_in(_rk, 7), (2,), 0, max(1, 1024 // 4) + 1, jnp.int32)
        _lenS2 = 77 - jax.random.randint(jax.random.fold_in(_rk, 8), (2,), 0, max(1, 77 // 4) + 1, jnp.int32)
        _ctx_1024P = jax.random.normal(jax.random.fold_in(_rk, 11), (2, 16, 256), jnp.float32)
        _ctx_1024c = jax.random.dirichlet(jax.random.fold_in(_rk, 511), 0.3 * jnp.ones((16,), jnp.float32), (2, 77))
        _ctx_1024t = jnp.einsum('bsk,bkd->bsd', _ctx_1024c, _ctx_1024P)
        _ctx_1024t = _ctx_1024t * jax.lax.rsqrt(jnp.mean(jnp.square(_ctx_1024t)) + 1e-12) * 0.953939
        ctx_1024 = -1.39393e-06 + 0.999914 * (_ctx_1024t + 0.3 * jax.random.normal(jax.random.fold_in(_rk, 611), (2, 77, 256), jnp.float32))
        fside_Bx16xSxS2_0 = jax.random.uniform(jax.random.fold_in(_rk, 12), (2, 16, 1024, 77), jnp.float32, 0.0, 1)
        _validS = jnp.arange(1024)[None, :] < _lenS[:, None]
        _validS2 = jnp.arange(77)[None, :] < _lenS2[:, None]
        _causal = jnp.tril(jnp.ones((1024, 1024), dtype=bool))
        mask_Bx16xSxS2_bk1 = jnp.broadcast_to(_validS2[:, None, None, :], (2, 16, 1024, 77))
        mask_BxS_ff1 = jnp.where(jnp.ones((2, 1024), dtype=bool), 1.0, 0.0).astype(jnp.float32)
        mask_BxS2_ik0 = jnp.where(jnp.broadcast_to(_validS2[:, :], (2, 77)), 0, 1).astype(jnp.int32)
        mask_Bx1xSxS2_bk1 = jnp.broadcast_to(_validS2[:, None, None, :], (2, 1, 1024, 77))
        return (x, ctx_1024, fside_Bx16xSxS2_0, mask_Bx16xSxS2_bk1, mask_BxS_ff1, mask_BxS2_ik0, mask_Bx1xSxS2_bk1)
    x, ctx_1024, fside_Bx16xSxS2_0, mask_Bx16xSxS2_bk1, mask_BxS_ff1, mask_BxS2_ik0, mask_Bx1xSxS2_bk1 = _rec_inputs()

    def _L0_xattn_setup():
        import jax, jax.numpy as jnp
        import numpy as np
        D_MODEL, D_K, D_V, H = (256, 64, 64, 16)
        B, NQ, NK = (2, 512, 512)
        key = jax.random.key(seed)
        ks = jax.random.split(key, 14)
        xavier = lambda k, fan_in, fan_out: jax.random.uniform(k, (fan_in, fan_out), jnp.float32, -jnp.sqrt(6.0 / (fan_in + fan_out)), jnp.sqrt(6.0 / (fan_in + fan_out)))
        return {'queries': jax.random.normal(ks[0], (B, NQ, D_MODEL), jnp.float32), 'keys': jax.random.normal(ks[1], (B, NK, D_MODEL), jnp.float32), 'values': jax.random.normal(ks[2], (B, NK, D_MODEL), jnp.float32), 'attention_weights': jax.random.uniform(ks[3], (B, H, NQ, NK), jnp.float32), 'attention_mask': jax.random.randint(ks[4], (B, H, NQ, NK), 0, 2).astype(jnp.bool_), 'Wq': xavier(ks[5], D_MODEL, H * D_K), 'bq': jnp.zeros((H * D_K,), jnp.float32), 'Wk': xavier(ks[6], D_MODEL, H * D_K), 'bk': jnp.zeros((H * D_K,), jnp.float32), 'Wv': xavier(ks[7], D_MODEL, H * D_V), 'bv': jnp.zeros((H * D_V,), jnp.float32), 'Wo': xavier(ks[8], H * D_V, D_MODEL), 'bo': jnp.zeros((D_MODEL,), jnp.float32)}
    _L0_xattn_all = _L0_xattn_setup()
    _L0_xattn_in = {k: v for k, v in _L0_xattn_all.items() if k in ('Wq', 'bq', 'Wk', 'bk', 'Wv', 'bv', 'Wo', 'bo')}
    del _L0_xattn_all

    def _L0_ffn_setup():
        import jax, jax.numpy as jnp
        import numpy as np
        E = 16
        G = 4
        EPG = E // G
        K = 4
        TOPK_GROUP = 2
        PER_GROUP_K = K // TOPK_GROUP

        def _route(xf, router_w, correction_bias):
            S = xf.shape[0]
            logits = xf @ router_w.T
            scores = jax.nn.sigmoid(logits)
            sb = scores + correction_bias
            grp_top = jax.lax.top_k(sb.reshape(S, G, EPG), PER_GROUP_K)[0]
            group_scores = grp_top.sum(axis=-1)
            _, group_idx = jax.lax.top_k(group_scores, TOPK_GROUP)
            group_mask = jnp.zeros((S, G), sb.dtype).at[jnp.arange(S)[:, None], group_idx].set(1.0)
            score_mask = jnp.broadcast_to(group_mask[:, :, None], (S, G, EPG)).reshape(S, E)
            masked = jnp.where(score_mask > 0, sb, -jnp.inf)
            _, topk_idx = jax.lax.top_k(masked, K)
            w = jnp.take_along_axis(scores, topk_idx, axis=1)
            w = w / (w.sum(axis=-1, keepdims=True) + 1e-20)
            return (topk_idx, w, scores)
        key = jax.random.key(seed)
        ks = jax.random.split(key, 9)
        B, T, C, H, HS = (2, 256, 256, 64, 512)
        std = 0.02
        return {'x': jax.random.normal(ks[0], (B, T, C), jnp.float32), 'router_w': jax.random.normal(ks[1], (E, C), jnp.float32) * std, 'correction_bias': jnp.zeros((E,), jnp.float32), 'gate_w': jax.random.normal(ks[2], (E, C, H), jnp.float32) * std, 'up_w': jax.random.normal(ks[3], (E, C, H), jnp.float32) * std, 'down_w': jax.random.normal(ks[4], (E, H, C), jnp.float32) * std, 'shared_gate_w': jax.random.normal(ks[5], (HS, C), jnp.float32) * std, 'shared_up_w': jax.random.normal(ks[6], (HS, C), jnp.float32) * std, 'shared_down_w': jax.random.normal(ks[7], (C, HS), jnp.float32) * std}
    _L0_ffn_all = _L0_ffn_setup()
    _L0_ffn_in = {k: v for k, v in _L0_ffn_all.items() if k in ('router_w', 'correction_bias', 'gate_w', 'up_w', 'down_w', 'shared_gate_w', 'shared_up_w', 'shared_down_w')}
    del _L0_ffn_all

    def _L1_xattn_setup():
        import jax, jax.numpy as jnp
        import numpy as np
        key = jax.random.key(seed)
        ks = jax.random.split(key, 7)
        B, S, D, H, Dh = (4, 512, 256, 16, 64)
        return {'query_input': jax.random.normal(ks[0], (B, S, D), jnp.float32), 'key_input': jax.random.normal(ks[1], (B, S, D), jnp.float32), 'value_input': jax.random.normal(ks[2], (B, S, D), jnp.float32), 'Wq': jax.random.normal(ks[3], (D, H, Dh), jnp.float32) * 0.03, 'Wk': jax.random.normal(ks[4], (D, H, Dh), jnp.float32) * 0.03, 'Wv': jax.random.normal(ks[5], (D, H, Dh), jnp.float32) * 0.03, 'Wo': jax.random.normal(ks[6], (H, Dh, D), jnp.float32) * 0.03}
    _L1_xattn_all = _L1_xattn_setup()
    _L1_xattn_in = {k: v for k, v in _L1_xattn_all.items() if k in ('Wq', 'Wk', 'Wv', 'Wo')}
    del _L1_xattn_all

    def _L1_ffn_setup():
        import jax, jax.numpy as jnp
        import numpy as np
        HIDDEN = 256
        INTER = 1024
        key = jax.random.key(seed)
        k1, k2, k3, k4, k5 = jax.random.split(key, 5)
        hidden_states = jax.random.normal(k1, (4, 512, HIDDEN), dtype=jnp.float32)
        W1 = jax.random.normal(k2, (HIDDEN, INTER), dtype=jnp.float32) * (1.0 / np.sqrt(HIDDEN))
        b1 = jax.random.normal(k3, (INTER,), dtype=jnp.float32) * 0.02
        W2 = jax.random.normal(k4, (INTER, HIDDEN), dtype=jnp.float32) * (1.0 / np.sqrt(INTER))
        b2 = jax.random.normal(k5, (HIDDEN,), dtype=jnp.float32) * 0.02
        return {'hidden_states': hidden_states, 'W1': W1, 'b1': b1, 'W2': W2, 'b2': b2}
    _L1_ffn_all = _L1_ffn_setup()
    _L1_ffn_in = {k: v for k, v in _L1_ffn_all.items() if k in ('W1', 'b1', 'W2', 'b2')}
    del _L1_ffn_all

    def _L2_xattn_setup():
        import jax, jax.numpy as jnp
        import numpy as np
        B, F, T, D = (8, 64, 32, 256)
        NEG = -1e+30
        key = jax.random.key(seed)
        ks = jax.random.split(key, 10)
        s = 1.0 / np.sqrt(D)
        return {'features': jax.random.normal(ks[0], (B, F, D), jnp.float32), 'masks': jnp.ones((B, F), jnp.float32), 'textual_features': jax.random.normal(ks[1], (B, T, D), jnp.float32), 'q_masks': jax.random.randint(ks[2], (B, T), 0, 2, jnp.int32), 'Ws': jax.random.normal(ks[3], (D, D), jnp.float32) * s, 'W': jax.random.normal(ks[4], (D, D), jnp.float32) * s, 'w': jax.random.normal(ks[5], (D, 1), jnp.float32) * s, 'b': jax.random.normal(ks[6], (1, D), jnp.float32) * s, 'Wcw': jax.random.normal(ks[7], (1, D), jnp.float32) * s, 'bcw': jnp.zeros((1,), jnp.float32), 'Wcb': jax.random.normal(ks[8], (1, D), jnp.float32) * s, 'bcb': jnp.zeros((1,), jnp.float32)}
    _L2_xattn_all = _L2_xattn_setup()
    _L2_xattn_in = {k: v for k, v in _L2_xattn_all.items() if k in ('Ws', 'W', 'w', 'b', 'Wcw', 'bcw', 'Wcb', 'bcb')}
    del _L2_xattn_all

    def _L2_ffn_setup():
        import jax, jax.numpy as jnp
        import numpy as np
        import math
        GOLDEN_CENTER = 1.0 / math.e
        GOLDEN_LOWER = 0.5 - math.log(4.0 / 3.0)
        GOLDEN_UPPER = 0.5
        B, T, D = (4, 512, 256)
        E = 8
        I = 1024 // (E // 2)

        def _routing_weights(x, Wr, temperature):
            inh = jax.nn.sigmoid(x @ Wr / temperature)
            in_zone = (inh >= GOLDEN_LOWER) & (inh <= GOLDEN_UPPER)
            dist = jnp.abs(inh - GOLDEN_CENTER)
            w = jnp.exp(-dist / 0.1) * in_zone.astype(x.dtype)
            wsum = w.sum(axis=-1, keepdims=True)
            no_expert = wsum < 1e-08
            fb = jnp.exp(-dist / 0.3)
            _, top2 = jax.lax.top_k(fb, 2)
            fb_mask = jax.nn.one_hot(top2, E, dtype=x.dtype).sum(axis=-2)
            fb_w = fb * fb_mask
            fb_w = fb_w / jnp.clip(fb_w.sum(axis=-1, keepdims=True), 1e-08)
            w = jnp.where(no_expert, fb_w, w)
            wsum = w.sum(axis=-1, keepdims=True)
            return w / jnp.clip(wsum, 1e-08)
        key = jax.random.key(seed)
        k = jax.random.split(key, 6)
        s_d = 1.0 / math.sqrt(D)
        s_i = 1.0 / math.sqrt(I)
        return {'x': jax.random.normal(k[0], (B, T, D), jnp.float32), 'Wg': jax.random.normal(k[1], (E, D, I), jnp.float32) * s_d, 'Wu': jax.random.normal(k[2], (E, D, I), jnp.float32) * s_d, 'Wd': jax.random.normal(k[3], (E, I, D), jnp.float32) * s_i, 'Wr': jax.random.normal(k[4], (D, E), jnp.float32) * s_d, 'temperature': jnp.ones((1,), jnp.float32)}
    _L2_ffn_all = _L2_ffn_setup()
    _L2_ffn_in = {k: v for k, v in _L2_ffn_all.items() if k in ('Wg', 'Wu', 'Wd', 'Wr', 'temperature')}
    del _L2_ffn_all

    def _L3_xattn_setup():
        import jax, jax.numpy as jnp
        import numpy as np
        B, S, D, H = (4, 512, 256, 16)
        HD = D // H
        key = jax.random.key(seed)
        ks = jax.random.split(key, 12)
        scale = 1.0 / np.sqrt(D)
        inp = {'queries': jax.random.normal(ks[0], (B, S, D), jnp.float32), 'keys': jax.random.normal(ks[1], (B, S, D), jnp.float32), 'values': jax.random.normal(ks[2], (B, S, D), jnp.float32), 'mask': jax.random.randint(ks[3], (B, 1, S, S), 0, 2).astype(bool), 'Wq': jax.random.normal(ks[4], (D, D), jnp.float32) * scale, 'bq': jnp.zeros((D,), jnp.float32), 'Wk': jax.random.normal(ks[5], (D, D), jnp.float32) * scale, 'bk': jnp.zeros((D,), jnp.float32), 'Wv': jax.random.normal(ks[6], (D, D), jnp.float32) * scale, 'bv': jnp.zeros((D,), jnp.float32), 'Wo': jax.random.normal(ks[7], (D, D), jnp.float32) * scale, 'bo': jnp.zeros((D,), jnp.float32)}
        return inp
    _L3_xattn_all = _L3_xattn_setup()
    _L3_xattn_in = {k: v for k, v in _L3_xattn_all.items() if k in ('Wq', 'bq', 'Wk', 'bk', 'Wv', 'bv', 'Wo', 'bo')}
    del _L3_xattn_all

    def _L3_ffn_setup():
        import jax, jax.numpy as jnp
        import numpy as np
        EPS = 1e-08

        def _ste(x, q):
            return x + jax.lax.stop_gradient(q - x)

        def quant_act_uint8(x):
            s = jax.lax.stop_gradient(jnp.maximum(jnp.max(x), EPS)) / 255.0
            q = jnp.clip(jnp.round(x / s), 0.0, 255.0) * s
            return (_ste(x, q), s)

        def quant_weight_int8_perchannel(w):
            s = jax.lax.stop_gradient(jnp.maximum(jnp.max(jnp.abs(w), axis=1, keepdims=True), EPS)) / 127.0
            q = jnp.clip(jnp.round(w / s), -128.0, 127.0) * s
            return (_ste(w, q), s[:, 0])

        def quant_bias_int32(b, s_in, s_w):
            s = jax.lax.stop_gradient(s_in * s_w)
            q = jnp.round(b / s) * s
            return _ste(b, q)

        def quant_linear(x, w, b):
            xq, s_in = quant_act_uint8(x)
            wq, s_w = quant_weight_int8_perchannel(w)
            bq = quant_bias_int32(b, s_in, s_w)
            return jnp.einsum('btd,fd->btf', xq, wq) + bq
        key = jax.random.key(seed)
        k1, k2, k3, k4, k5 = jax.random.split(key, 5)
        B, S, D, F = (4, 512, 256, 1024)
        return {'x': jax.random.normal(k1, (B, S, D), dtype=jnp.float32), 'w1': jax.random.normal(k2, (F, D), dtype=jnp.float32) * (1.0 / np.sqrt(D)), 'b1': jax.random.normal(k3, (F,), dtype=jnp.float32) * 0.01, 'w2': jax.random.normal(k4, (D, F), dtype=jnp.float32) * (1.0 / np.sqrt(F)), 'b2': jax.random.normal(k5, (D,), dtype=jnp.float32) * 0.01}
    _L3_ffn_all = _L3_ffn_setup()
    _L3_ffn_in = {k: v for k, v in _L3_ffn_all.items() if k in ('w1', 'b1', 'w2', 'b2')}
    del _L3_ffn_all
    return {'x': x, 'ctx_1024': ctx_1024, 'fside_Bx16xSxS2_0': fside_Bx16xSxS2_0, 'mask_Bx16xSxS2_bk1': mask_Bx16xSxS2_bk1, 'mask_BxS_ff1': mask_BxS_ff1, 'mask_BxS2_ik0': mask_BxS2_ik0, 'mask_Bx1xSxS2_bk1': mask_Bx1xSxS2_bk1, 'L0_xattn_Wq': _L0_xattn_in['Wq'], 'L0_xattn_bq': _L0_xattn_in['bq'], 'L0_xattn_Wk': _L0_xattn_in['Wk'], 'L0_xattn_bk': _L0_xattn_in['bk'], 'L0_xattn_Wv': _L0_xattn_in['Wv'], 'L0_xattn_bv': _L0_xattn_in['bv'], 'L0_xattn_Wo': _L0_xattn_in['Wo'], 'L0_xattn_bo': _L0_xattn_in['bo'], 'L0_ffn_router_w': _L0_ffn_in['router_w'], 'L0_ffn_correction_bias': _L0_ffn_in['correction_bias'], 'L0_ffn_gate_w': _L0_ffn_in['gate_w'], 'L0_ffn_up_w': _L0_ffn_in['up_w'], 'L0_ffn_down_w': _L0_ffn_in['down_w'], 'L0_ffn_shared_gate_w': _L0_ffn_in['shared_gate_w'], 'L0_ffn_shared_up_w': _L0_ffn_in['shared_up_w'], 'L0_ffn_shared_down_w': _L0_ffn_in['shared_down_w'], 'L1_xattn_Wq': _L1_xattn_in['Wq'], 'L1_xattn_Wk': _L1_xattn_in['Wk'], 'L1_xattn_Wv': _L1_xattn_in['Wv'], 'L1_xattn_Wo': _L1_xattn_in['Wo'], 'L1_ffn_W1': _L1_ffn_in['W1'], 'L1_ffn_b1': _L1_ffn_in['b1'], 'L1_ffn_W2': _L1_ffn_in['W2'], 'L1_ffn_b2': _L1_ffn_in['b2'], 'L2_xattn_Ws': _L2_xattn_in['Ws'], 'L2_xattn_W': _L2_xattn_in['W'], 'L2_xattn_w': _L2_xattn_in['w'], 'L2_xattn_b': _L2_xattn_in['b'], 'L2_xattn_Wcw': _L2_xattn_in['Wcw'], 'L2_xattn_bcw': _L2_xattn_in['bcw'], 'L2_xattn_Wcb': _L2_xattn_in['Wcb'], 'L2_xattn_bcb': _L2_xattn_in['bcb'], 'L2_ffn_Wg': _L2_ffn_in['Wg'], 'L2_ffn_Wu': _L2_ffn_in['Wu'], 'L2_ffn_Wd': _L2_ffn_in['Wd'], 'L2_ffn_Wr': _L2_ffn_in['Wr'], 'L2_ffn_temperature': _L2_ffn_in['temperature'], 'L3_xattn_Wq': _L3_xattn_in['Wq'], 'L3_xattn_bq': _L3_xattn_in['bq'], 'L3_xattn_Wk': _L3_xattn_in['Wk'], 'L3_xattn_bk': _L3_xattn_in['bk'], 'L3_xattn_Wv': _L3_xattn_in['Wv'], 'L3_xattn_bv': _L3_xattn_in['bv'], 'L3_xattn_Wo': _L3_xattn_in['Wo'], 'L3_xattn_bo': _L3_xattn_in['bo'], 'L3_ffn_w1': _L3_ffn_in['w1'], 'L3_ffn_b1': _L3_ffn_in['b1'], 'L3_ffn_w2': _L3_ffn_in['w2'], 'L3_ffn_b2': _L3_ffn_in['b2']}

def reference(x, ctx_1024, fside_Bx16xSxS2_0, mask_Bx16xSxS2_bk1, mask_BxS_ff1, mask_BxS2_ik0, mask_Bx1xSxS2_bk1, L0_xattn_Wq, L0_xattn_bq, L0_xattn_Wk, L0_xattn_bk, L0_xattn_Wv, L0_xattn_bv, L0_xattn_Wo, L0_xattn_bo, L0_ffn_router_w, L0_ffn_correction_bias, L0_ffn_gate_w, L0_ffn_up_w, L0_ffn_down_w, L0_ffn_shared_gate_w, L0_ffn_shared_up_w, L0_ffn_shared_down_w, L1_xattn_Wq, L1_xattn_Wk, L1_xattn_Wv, L1_xattn_Wo, L1_ffn_W1, L1_ffn_b1, L1_ffn_W2, L1_ffn_b2, L2_xattn_Ws, L2_xattn_W, L2_xattn_w, L2_xattn_b, L2_xattn_Wcw, L2_xattn_bcw, L2_xattn_Wcb, L2_xattn_bcb, L2_ffn_Wg, L2_ffn_Wu, L2_ffn_Wd, L2_ffn_Wr, L2_ffn_temperature, L3_xattn_Wq, L3_xattn_bq, L3_xattn_Wk, L3_xattn_bk, L3_xattn_Wv, L3_xattn_bv, L3_xattn_Wo, L3_xattn_bo, L3_ffn_w1, L3_ffn_b1, L3_ffn_w2, L3_ffn_b2):
    import jax
    import jax.numpy as jnp

    def _L0_xattn_ref(queries, keys, values, attention_weights, attention_mask, Wq, bq, Wk, bk, Wv, bv, Wo, bo):
        import jax, jax.numpy as jnp
        import numpy as np
        D_MODEL, D_K, D_V, H = (256, 64, 64, 16)
        B, NQ, NK = (2, 512, 512)
        b_s, nq, _ = queries.shape
        nk = keys.shape[1]
        q = (queries @ Wq + bq).reshape(b_s, nq, H, D_K).transpose(0, 2, 1, 3)
        k = (keys @ Wk + bk).reshape(b_s, nk, H, D_K).transpose(0, 2, 1, 3)
        v = (values @ Wv + bv).reshape(b_s, nk, H, D_V).transpose(0, 2, 1, 3)
        att = jnp.einsum('bhqd,bhkd->bhqk', q, k) / jnp.sqrt(jnp.float32(D_K))
        att = att * attention_weights
        att = jnp.where(attention_mask, -jnp.inf, att)
        att = jax.nn.softmax(att, axis=-1)
        out = jnp.einsum('bhqk,bhkd->bhqd', att, v)
        out = out.transpose(0, 2, 1, 3).reshape(b_s, nq, H * D_V)
        return out @ Wo + bo

    def _L0_ffn_ref(x, router_w, correction_bias, gate_w, up_w, down_w, shared_gate_w, shared_up_w, shared_down_w):
        import jax, jax.numpy as jnp
        import numpy as np
        E = 16
        G = 4
        EPG = E // G
        K = 4
        TOPK_GROUP = 2
        PER_GROUP_K = K // TOPK_GROUP

        def _route(xf, router_w, correction_bias):
            S = xf.shape[0]
            logits = xf @ router_w.T
            scores = jax.nn.sigmoid(logits)
            sb = scores + correction_bias
            grp_top = jax.lax.top_k(sb.reshape(S, G, EPG), PER_GROUP_K)[0]
            group_scores = grp_top.sum(axis=-1)
            _, group_idx = jax.lax.top_k(group_scores, TOPK_GROUP)
            group_mask = jnp.zeros((S, G), sb.dtype).at[jnp.arange(S)[:, None], group_idx].set(1.0)
            score_mask = jnp.broadcast_to(group_mask[:, :, None], (S, G, EPG)).reshape(S, E)
            masked = jnp.where(score_mask > 0, sb, -jnp.inf)
            _, topk_idx = jax.lax.top_k(masked, K)
            w = jnp.take_along_axis(scores, topk_idx, axis=1)
            w = w / (w.sum(axis=-1, keepdims=True) + 1e-20)
            return (topk_idx, w, scores)
        B, T, C = x.shape
        S = B * T
        xf = x.reshape(S, C)
        sg = xf @ shared_gate_w.T
        su = xf @ shared_up_w.T
        shared_out = jax.nn.silu(sg) * su @ shared_down_w.T
        topk_idx, w, _scores = _route(xf, router_w, correction_bias)
        combine = jnp.zeros((S, E), xf.dtype).at[jnp.arange(S)[:, None], topk_idx].add(w)
        g = jnp.einsum('sc,ech->esh', xf, gate_w)
        u = jnp.einsum('sc,ech->esh', xf, up_w)
        h = jax.nn.silu(g) * u
        hw = h * combine.T[:, :, None]
        routed = jnp.einsum('esh,ehc->sc', hw, down_w)
        return (shared_out + routed).reshape(B, T, C)

    def _L1_xattn_ref(query_input, key_input, value_input, Wq, Wk, Wv, Wo):
        import jax, jax.numpy as jnp
        import numpy as np
        q = jnp.einsum('bsd,dhk->bshk', query_input, Wq)
        k = jnp.einsum('bsd,dhk->bshk', key_input, Wk)
        v = jnp.einsum('bsd,dhk->bshk', value_input, Wv)
        depth = Wq.shape[-1]
        q = q * depth ** (-0.5)
        logits = jnp.einsum('bthk,bfhk->bhft', k, q)
        weights = jax.nn.softmax(logits, axis=-1)
        ctx = jnp.einsum('bhft,bthk->bfhk', weights, v)
        return jnp.einsum('bfhk,hkd->bfd', ctx, Wo)

    def _L1_ffn_ref(hidden_states, W1, b1, W2, b2):
        import jax, jax.numpy as jnp
        import numpy as np
        HIDDEN = 256
        INTER = 1024
        h = jax.nn.relu(jnp.einsum('bsh,hi->bsi', hidden_states, W1) + b1)
        return jnp.einsum('bsi,ih->bsh', h, W2) + b2

    def _L2_xattn_ref(features, masks, textual_features, q_masks, Ws, W, w, b, Wcw, bcw, Wcb, bcb):
        import jax, jax.numpy as jnp
        import numpy as np
        B, F, T, D = (8, 64, 32, 256)
        NEG = -1e+30
        txt_proj = jnp.einsum('btd,de->bte', textual_features, Ws)
        feat_proj = jnp.einsum('bfd,de->bfe', features, W)
        h = jnp.tanh(txt_proj[:, None, :, :] + feat_proj[:, :, None, :] + b[None, None, :, :][..., 0, :])
        rho = jnp.einsum('bftd,d->bft', h, w[:, 0])
        qm = q_masks.astype(jnp.float32)
        rho = rho + (1.0 - qm)[:, None, :] * NEG
        att = jax.nn.softmax(rho, axis=-1)
        txt_h = jnp.einsum('bft,btd->bfd', att, textual_features)
        w_s = jnp.tanh(jnp.einsum('bfd,od->bfo', txt_h, Wcw) + bcw)
        b_s = jnp.tanh(jnp.einsum('bfd,od->bfo', txt_h, Wcb) + bcb)
        return w_s * features + b_s

    def _L2_ffn_ref(x, Wg, Wu, Wd, Wr, temperature):
        import jax, jax.numpy as jnp
        import numpy as np
        import math
        GOLDEN_CENTER = 1.0 / math.e
        GOLDEN_LOWER = 0.5 - math.log(4.0 / 3.0)
        GOLDEN_UPPER = 0.5
        B, T, D = (4, 512, 256)
        E = 8
        I = 1024 // (E // 2)

        def _routing_weights(x, Wr, temperature):
            inh = jax.nn.sigmoid(x @ Wr / temperature)
            in_zone = (inh >= GOLDEN_LOWER) & (inh <= GOLDEN_UPPER)
            dist = jnp.abs(inh - GOLDEN_CENTER)
            w = jnp.exp(-dist / 0.1) * in_zone.astype(x.dtype)
            wsum = w.sum(axis=-1, keepdims=True)
            no_expert = wsum < 1e-08
            fb = jnp.exp(-dist / 0.3)
            _, top2 = jax.lax.top_k(fb, 2)
            fb_mask = jax.nn.one_hot(top2, E, dtype=x.dtype).sum(axis=-2)
            fb_w = fb * fb_mask
            fb_w = fb_w / jnp.clip(fb_w.sum(axis=-1, keepdims=True), 1e-08)
            w = jnp.where(no_expert, fb_w, w)
            wsum = w.sum(axis=-1, keepdims=True)
            return w / jnp.clip(wsum, 1e-08)
        weights = _routing_weights(x, Wr, temperature)
        gate = jnp.einsum('btd,edi->beti', x, Wg)
        up = jnp.einsum('btd,edi->beti', x, Wu)
        h = jax.nn.silu(gate) * up
        e_out = jnp.einsum('beti,eid->betd', h, Wd)
        out = jnp.einsum('bte,betd->btd', weights, e_out)
        return out

    def _L3_xattn_ref(queries, keys, values, mask, Wq, bq, Wk, bk, Wv, bv, Wo, bo):
        import jax, jax.numpy as jnp
        import numpy as np
        B, S, D, H = (4, 512, 256, 16)
        HD = D // H
        b, sq, d = queries.shape

        def split_heads(x):
            return x.reshape(b, x.shape[1], H, HD).transpose(0, 2, 1, 3)
        q = split_heads(queries @ Wq + bq)
        k = split_heads(keys @ Wk + bk)
        v = split_heads(values @ Wv + bv)
        scores = jnp.einsum('bhqd,bhkd->bhqk', q, k) / jnp.sqrt(jnp.float32(HD))
        scores = jnp.where(mask, jnp.float32(-1000000000000000.0), scores)
        attn = jax.nn.softmax(scores, axis=-1)
        ctx = jnp.einsum('bhqk,bhkd->bhqd', attn, v)
        ctx = ctx.transpose(0, 2, 1, 3).reshape(b, sq, d)
        return ctx @ Wo + bo

    def _L3_ffn_ref(x, w1, b1, w2, b2):
        import jax, jax.numpy as jnp
        import numpy as np
        EPS = 1e-08

        def _ste(x, q):
            return x + jax.lax.stop_gradient(q - x)

        def quant_act_uint8(x):
            s = jax.lax.stop_gradient(jnp.maximum(jnp.max(x), EPS)) / 255.0
            q = jnp.clip(jnp.round(x / s), 0.0, 255.0) * s
            return (_ste(x, q), s)

        def quant_weight_int8_perchannel(w):
            s = jax.lax.stop_gradient(jnp.maximum(jnp.max(jnp.abs(w), axis=1, keepdims=True), EPS)) / 127.0
            q = jnp.clip(jnp.round(w / s), -128.0, 127.0) * s
            return (_ste(w, q), s[:, 0])

        def quant_bias_int32(b, s_in, s_w):
            s = jax.lax.stop_gradient(s_in * s_w)
            q = jnp.round(b / s) * s
            return _ste(b, q)

        def quant_linear(x, w, b):
            xq, s_in = quant_act_uint8(x)
            wq, s_w = quant_weight_int8_perchannel(w)
            bq = quant_bias_int32(b, s_in, s_w)
            return jnp.einsum('btd,fd->btf', xq, wq) + bq
        h = jax.nn.relu(quant_linear(x, w1, b1))
        return quant_linear(h, w2, b2)
    x = x + _L0_xattn_ref(_layernorm(x, axis=-1), ctx_1024, ctx_1024, fside_Bx16xSxS2_0, mask_Bx16xSxS2_bk1, L0_xattn_Wq, L0_xattn_bq, L0_xattn_Wk, L0_xattn_bk, L0_xattn_Wv, L0_xattn_bv, L0_xattn_Wo, L0_xattn_bo)
    x = x + _L0_ffn_ref(_layernorm(x, axis=-1), L0_ffn_router_w, L0_ffn_correction_bias, L0_ffn_gate_w, L0_ffn_up_w, L0_ffn_down_w, L0_ffn_shared_gate_w, L0_ffn_shared_up_w, L0_ffn_shared_down_w)
    x = x + _L1_xattn_ref(_layernorm(x, axis=-1), ctx_1024, ctx_1024, L1_xattn_Wq, L1_xattn_Wk, L1_xattn_Wv, L1_xattn_Wo)
    x = x + _L1_ffn_ref(_layernorm(x, axis=-1), L1_ffn_W1, L1_ffn_b1, L1_ffn_W2, L1_ffn_b2)
    x = x + _L2_xattn_ref(_layernorm(x, axis=-1), mask_BxS_ff1, ctx_1024, mask_BxS2_ik0, L2_xattn_Ws, L2_xattn_W, L2_xattn_w, L2_xattn_b, L2_xattn_Wcw, L2_xattn_bcw, L2_xattn_Wcb, L2_xattn_bcb)
    x = x + _L2_ffn_ref(_layernorm(x, axis=-1), L2_ffn_Wg, L2_ffn_Wu, L2_ffn_Wd, L2_ffn_Wr, L2_ffn_temperature)
    x = x + _L3_xattn_ref(_layernorm(x, axis=-1), ctx_1024, ctx_1024, mask_Bx1xSxS2_bk1, L3_xattn_Wq, L3_xattn_bq, L3_xattn_Wk, L3_xattn_bk, L3_xattn_Wv, L3_xattn_bv, L3_xattn_Wo, L3_xattn_bo)
    x = x + _L3_ffn_ref(_layernorm(x, axis=-1), L3_ffn_w1, L3_ffn_b1, L3_ffn_w2, L3_ffn_b2)
    return x

_drawn_inputs = setup_inputs


def setup_inputs(seed=0):
    import zlib

    import numpy as np

    out = dict(_drawn_inputs(seed))
    spreads = {'L0_xattn_bq': (0.0, 0.458),
     'L0_xattn_bk': (0.0, 0.691),
     'L0_xattn_bv': (0.0, 0.1),
     'L0_xattn_bo': (0.0, 0.1),
     'L0_ffn_correction_bias': (0.0, 0.8),
     'L3_xattn_bq': (0.0, 0.463),
     'L3_xattn_bk': (0.0, 2.0),
     'L3_xattn_bv': (0.0, 0.1),
     'L3_xattn_bo': (0.0, 0.1)}
    factors = {'L0_ffn_router_w': 6.158,
     'L0_ffn_gate_w': 5.307,
     'L0_ffn_up_w': 6.338,
     'L0_ffn_down_w': 5.311,
     'L1_ffn_b1': 3.359,
     'L2_xattn_b': 8.0,
     'L3_ffn_b1': 8.0,
     'L3_ffn_b2': 8.0,
     'L1_xattn_Wq': 2.728,
     'L1_xattn_Wk': 2.738,
     'L1_ffn_b2': 2.913}
    for name, (base, spread) in spreads.items():
        noise = np.random.default_rng([zlib.crc32(name.encode()), seed]).standard_normal(out[name].shape)
        drawn = base * np.exp(spread * noise) if base else spread * noise
        out[name] = jnp.asarray(drawn.astype(out[name].dtype))
    for name, factor in factors.items():
        out[name] = (out[name] * factor).astype(out[name].dtype)
    return out
```

```python
import math
from contextlib import ExitStack

import concourse.bass as bass
from concourse import mybir

F32 = mybir.dt.float32
BF16 = mybir.dt.bfloat16
U8 = mybir.dt.uint8
I32 = mybir.dt.int32
ALU = mybir.AluOpType
ACT = mybir.ActivationFunctionType
AX = mybir.AxisListType.X

P = 128
B, S, D = 2, 1024, 256
NT = B * S // P
TB = S // P
KT = D // P
H, S2 = 16, 77
HK = H * S2
HPB = 6
BANK = 512
NR = -(-HK // P)
RLAST = HK - (NR - 1) * P
CT = 4
NC = NT // CT
CN = CT * P
EPS = 1e-5
PGROUPS = [range(0, 4), range(4, 8), range(8, NR)]
BANKS = [(512 * g, 6 * g, min(H, 6 * g + 6)) for g in range(3)]


class Attention:

    def __init__(self, name, dims, biased, fside, mask_value):
        self.name, self.dims, self.biased, self.fside, self.mask_value = name, dims, biased, fside, mask_value
        self.hd = dims // H
        self.scale = float(self.hd) ** -0.5
        self.nm = dims // P
        self.g = P // self.hd
        self.seg = self.g * S2


def pipeline(eng, n, lead, step, body):
    for t in range(lead):
        body(t, t % step)
    with eng.Fori(0, (n - lead) // step) as i:
        for u in range(step):
            body(i * step + (lead + u), (lead + u) % step)
    for t in range(n, n + lead):
        body(t, t % step)


def live(t, lag, n):
    return not isinstance(t, int) or 0 <= t - lag < n


def has_before(t, k):
    return not isinstance(t, int) or t >= k


def build(nc, d, only=range(8)):
    ctx = ExitStack()
    with ctx:
        def sem(name):
            return ctx.enter_context(nc.semaphore(name))

        base = -(-nc.sbuf_base // 32) * 32
        limit = nc.sbuf_usable_end

        class Region:

            def __init__(self, start):
                self.at = start

            def __call__(self, name, shape, dt=F32):
                n = 1
                for s in shape[1:]:
                    n *= s
                size = -(-n * {F32: 4, BF16: 2, U8: 1, I32: 4}[dt] // 32) * 32
                t = nc.alloc_sbuf_tensor_at(name, shape, dt, offset=self.at)
                self.at += size
                assert self.at <= limit, (name, self.at - limit)
                return t

        keep = Region(base)
        x = keep("x", [P, NT, D])
        ident = keep("ident", [P, P])
        identb = keep("identb", [P, P], BF16)
        row0 = keep("row0", [P, P])
        ones = keep("ones", [P, P])
        ctxT = keep("ctxT", [P, KT, B * S2])
        mhalf = keep("mhalf", [P, 8])
        stats = keep("stats", [P, 8, 6])
        mv = keep("mv", [P, 8, 2])
        ve = keep("ve", [P, 8])
        rstd = keep("rstd", [P, 8])
        spare = keep("spare", [P, 1])
        start = keep.at

        psum = ctx.enter_context(nc.psum_tensor("psum", [P, 8 * BANK], F32))

        def bank(i, a=0, n=BANK):
            return psum[:, i * BANK + a:i * BANK + a + n]

        x_loaded = sem("x_loaded")
        const_loaded = sem("const_loaded")
        const_made = sem("const_made")
        layer_end = sem("layer_end")
        stored = sem("stored")
        parts = {e: [] for e in ("sync", "tensor", "scalar", "vector", "gpsimd")}
        ends = [0]

        def barrier():
            ends[0] += 1
            k = ends[0]
            for e in ("tensor", "scalar", "vector", "gpsimd"):
                def stop(eng, k=k):
                    eng.drain().then_inc(layer_end, 1)
                    eng.wait_ge(layer_end, 4 * k)
                parts[e].append(stop)

            def hold(eng, k=k):
                eng.wait_ge(layer_end, 4 * k)
            parts["sync"].append(hold)

        def load_x(eng):
            eng.dma_start(ctxT[:], d["ctxT"]).then_inc(const_loaded, 16)
            eng.dma_start(ident[:], d["ident"]).then_inc(const_loaded, 16)
            for b in range(B):
                eng.dma_start(x[:, TB * b:TB * (b + 1), :], d["x"][b].rearrange("(p j) n -> p j n", p=P)).then_inc(x_loaded, 16)
        parts["sync"].append(load_x)

        def make_constants(eng):
            eng.memset(ones[:], 1.0).then_inc(const_made, 1)
            eng.memset(mhalf[:], -0.5).then_inc(const_made, 1)
            eng.memset(row0[:], 0.0).then_inc(const_made, 1)
            eng.wait_ge(const_made, 3)
            eng.memset(row0[0:1, :], 1.0).then_inc(const_made, 1)
            eng.wait_ge(const_loaded, 32)
            eng.tensor_copy(identb[:], ident[:]).then_inc(const_made, 1)
        parts["gpsimd"].append(make_constants)

        def await_constants(eng):
            eng.wait_ge(const_made, 5)
            eng.wait_ge(const_loaded, 32)
            eng.wait_ge(x_loaded, 16 * B)
        for e in ("tensor", "scalar", "vector", "gpsimd"):
            parts[e].append(await_constants)

        weights_loaded = sem("weights_loaded")
        loads_until = {"": 0}

        def loads(name, pairs):
            loads_until[name] = max(loads_until.values()) + 16 * len(pairs)

            def go(eng):
                for dst, src in pairs:
                    eng.dma_start(dst, src).then_inc(weights_loaded, 16)
            parts["sync"].append(go)

        def await_weights(name):
            for e in ("tensor", "scalar", "vector", "gpsimd"):
                parts[e].append(lambda eng: eng.wait_ge(weights_loaded, loads_until[name]))

        kv_ready = sem("kv_ready")
        kv_taken = sem("kv_taken")
        fold_ready = sem("fold_ready")
        fold_taken = sem("fold_taken")
        prep = sem("fold_prepared")
        folds = {"kv": 0, "fold": 0, "prep": 0}

        def attention(L):
            nm, seg, g, n = L.nm, L.seg, L.g, L.name
            lastrows = RLAST + (1 if L.biased else 0)
            R = Region(start)
            A = R(n + "A", [P, KT, B, HK])
            VO = R(n + "VO", [P, B, NR, D])
            if L.biased:
                Ab = R(n + "Ab", [P, B, HK])
            if L.fside:
                fs = R(n + "fs", [P, 2, H, CT * S2])
                mk = R(n + "mk", [P, 2, H, CT * S2], U8)

                def of_tile(side, T, h0, h1):
                    return side[:, bass.ds(T // CT % 2, 1), h0:h1, bass.ds(T % CT * S2, S2)].rearrange("p a h k -> p (a h) k")
            shared = R.at
            W = Region(shared)
            wqT = W(n + "wqT", [P, nm, D])
            wk = W(n + "wk", [P, KT, L.dims])
            wv = W(n + "wv", [P, KT, L.dims])
            wo = W(n + "wo", [P, nm, D])
            BDK = W(n + "BDK", [P, B, nm, seg])
            BDV = W(n + "BDV", [P, B, nm, P + seg + P])
            group = W(n + "group", [P, 2, g])
            kvb = W(n + "kvb", [P, 2, nm])
            bqB = W(n + "bqB", [P, nm, P])
            pairs = [(wqT[:], d[n + "WqT"]), (wk[:], d[n + "Wk"]), (wv[:], d[n + "Wv"]), (wo[:], d[n + "Wo"]),
                     (group[:, 0, :], d[n + "group"])]
            if L.biased:
                pairs += [(kvb[:, 0, :], d[n + "bk"]), (kvb[:, 1, :], d[n + "bv"]), (bqB[:], d[n + "bqB"]),
                          (VO[RLAST:RLAST + 1, :, NR - 1, :], d[n + "bo2"])]
            loads(n, pairs)
            await_weights(n)
            kv0, fold0, prep0 = folds["kv"], folds["fold"], folds["prep"]

            def pe_kv(eng):
                for i in range(2 * nm):
                    m, w = i // 2, (wk, wv)[i % 2]
                    if i >= 4:
                        eng.wait_ge(kv_taken, kv0 + i - 3)
                    for kt in range(KT):
                        ins = eng.matmul(bank(i % 4, 0, B * S2), w[:, kt, P * m:P * m + P], ctxT[:, kt, :],
                                         start=kt == 0, stop=kt == KT - 1)
                    ins.then_inc(kv_ready, 1)
            parts["tensor"].append(pe_kv)

            def dve_kv(eng):
                eng.memset(BDV[:], 0.0).then_inc(prep, 1)
                eng.tensor_scalar(group[:, 1, :], group[:, 0, :], L.scale, None, ALU.mult).then_inc(prep, 1)
                if not L.biased:
                    eng.memset(kvb[:], 0.0).then_inc(prep, 1)
                eng.wait_ge(prep, prep0 + (2 if L.biased else 3))
                for i in range(2 * nm):
                    m, v = i // 2, i % 2
                    eng.wait_ge(kv_ready, kv0 + i + 1)
                    for b in range(B):
                        src = bank(i % 4, b * S2, S2).unsqueeze(1).broadcast_to([P, g, S2])
                        dst = BDV[:, b, m, P:P + seg] if v else BDK[:, b, m, :]
                        ins = eng.scalar_tensor_tensor(
                            out=dst.rearrange("p (g k) -> p g k", k=S2), in0=src, scalar=kvb[:, v, m:m + 1],
                            in1=group[:, 1 - v, :].unsqueeze(2).broadcast_to([P, g, S2]), op0=ALU.add, op1=ALU.mult)
                    ins.then_inc(kv_taken, 1)
            parts["vector"].append(dve_kv)

            jobs = [("A", b, kt) for b in range(B) for kt in range(KT)]
            if L.biased:
                jobs += [("Ab", b, 0) for b in range(B)]
            jobs += [("VO", b, r) for b in range(B) for r in range(0, NR, 2)]

            def pe_fold(eng):
                eng.wait_ge(kv_taken, kv0 + 2 * nm)
                for i, (kind, b, k) in enumerate(jobs):
                    if i >= 2:
                        eng.wait_ge(fold_taken, fold0 + i - 1)
                    b0 = 3 * (i % 2)
                    if kind != "VO":
                        for off, h0, h1 in BANKS:
                            for m in range(nm):
                                lo, hi = max(h0 * S2, m * seg), min(h1 * S2, (m + 1) * seg)
                                if lo < hi:
                                    w = wqT[:, m, P * k:P * k + P] if kind == "A" else bqB[:, m, :]
                                    o = b0 * BANK + off + lo - h0 * S2
                                    ins = eng.matmul(psum[:, o:o + hi - lo], w, BDK[:, b, m, lo - m * seg:hi - m * seg],
                                                     start=True, stop=True)
                    else:
                        for r in (k, k + 1):
                            rows = P if r < NR - 1 else RLAST
                            ms = [m for m in range(nm) if m * seg < P * r + rows and (m + 1) * seg > P * r]
                            for m in ms:
                                c = P + P * r - m * seg
                                ins = eng.matmul(psum[0:rows, (b0 + r - k) * BANK:(b0 + r - k) * BANK + D],
                                                 BDV[:, b, m, c:c + rows], wo[:, m, :],
                                                 start=m == ms[0], stop=m == ms[-1])
                    ins.then_inc(fold_ready, 1)
            parts["tensor"].append(pe_fold)

            def act_fold(eng):
                for i, (kind, b, k) in enumerate(jobs):
                    eng.wait_ge(fold_ready, fold0 + i + 1)
                    b0 = 3 * (i % 2)
                    if kind != "VO":
                        for off, h0, h1 in BANKS:
                            dst = A[:, k, b, h0 * S2:h1 * S2] if kind == "A" else Ab[:, b, h0 * S2:h1 * S2]
                            ins = eng.activation(dst, psum[:, b0 * BANK + off:b0 * BANK + off + (h1 - h0) * S2], ACT.Copy)
                    else:
                        for r in (k, k + 1):
                            rows = P if r < NR - 1 else RLAST
                            ins = eng.activation(VO[0:rows, b, r, :], psum[0:rows, (b0 + r - k) * BANK:(b0 + r - k) * BANK + D], ACT.Copy)
                    ins.then_inc(fold_taken, 1)
            parts["scalar"].append(act_fold)
            folds["kv"] += 2 * nm
            folds["fold"] += len(jobs)
            folds["prep"] += 2 if L.biased else 3
            barrier()

            M = Region(shared)
            lnx = [M(n + f"lnx{i}", [P, D]) for i in range(2)]
            lnT = [M(n + f"lnT{i}", [P, KT, P]) for i in range(2)]
            sc = [M(n + f"sc{i}", [P, HK]) for i in range(2)]
            pr = [M(n + f"pr{i}", [P, HK + 1]) for i in range(2)]
            pT = [M(n + f"pT{i}", [P, NR, P]) for i in range(2)]
            mx = M(n + "mx", [P, 2, H])
            sm = M(n + "sm", [P, 2, H])
            rs = M(n + "rs", [P, 2, H])
            if not L.fside and L.mask_value:
                mk3 = M(n + "mk3", [P, NT, S2], U8)
                ma3 = M(n + "ma3", [P, NT, S2])

            s = {k: sem(n + k) for k in (
                "ln_stats",
                "ln_rstd",
                "ln_done",
                "lnT_ready",
                "lnT_taken",
                "sc_ready",
                "sc_freed",
                "sc_steps",
                "shifted",
                "exp_done",
                "sum_steps",
                "probs_done",
                "pT_ready",
                "pT_taken",
                "out_ready",
                "x_added",
                "side_loaded",
                "mask_added",
                "pr_ones",
            )}
            NSC = 2 if L.fside else 1

            def of_bank(g):
                o, h0, h1 = BANKS[g]
                return psum[:, o:o + (h1 - h0) * S2].rearrange("p (h k) -> p h k", k=S2)

            if L.fside:
                def sp_side(eng):
                    for c in range(NC):
                        b, j = c // 2, c % 2
                        if c >= 1:
                            eng.wait_ge(s["side_loaded"], 32 * c)
                        if c >= 2:
                            eng.wait_ge(s["sc_steps"], NSC * CT * (c - 1))
                        sl = slice(j * CT * S2, (j + 1) * CT * S2)
                        eng.dma_start(fs[:, c % 2], d["fside"][b].rearrange("h (p j) k -> p h (j k)", p=P)[:, :, sl]).then_inc(s["side_loaded"], 16)
                        eng.dma_start(mk[:, c % 2], d["mask16"][b].rearrange("h (p j) k -> p h (j k)", p=P)[:, :, sl]).then_inc(s["side_loaded"], 16)
                parts["sync"].append(sp_side)
            elif L.mask_value:
                def sp_mask(eng):
                    for b in range(B):
                        eng.dma_start(mk3[:, TB * b:TB * (b + 1), :], d["mask1"][b, 0].rearrange("(p j) k -> p j k", p=P)).then_inc(s["side_loaded"], 16)
                parts["sync"].append(sp_mask)

            def pe_main(eng):
                def body(t, u):
                    if live(t, 0, NT):
                        T, i = t, u
                        eng.wait_ge(s["ln_done"], T + 1)
                        if has_before(T, 1):
                            eng.wait_ge(s["lnT_taken"], T)
                        for kt in range(KT):
                            ins = eng.transpose(bank(7, P * kt, P), lnx[i][:, P * kt:P * kt + P], ident[:])
                        ins.then_inc(s["lnT_ready"], 1)
                    if live(t, 1, NT):
                        T, i = t - 1, 1 - u
                        b = T // TB
                        eng.wait_ge(s["lnT_taken"], T + 1)
                        for g, (o, h0, h1) in enumerate(BANKS):
                            if has_before(T, 1):
                                eng.wait_ge(s["sc_freed"], 3 * (T - 1) + g + 1)
                            w = (h1 - h0) * S2
                            for kt in range(KT):
                                ins = eng.matmul(psum[:, o:o + w], lnT[i][:, kt, :], A[:, kt, bass.ds(b, 1), h0 * S2:h1 * S2],
                                                 start=kt == 0, stop=kt == KT - 1 and not L.biased)
                            if L.biased:
                                ins = eng.matmul(psum[:, o:o + w], row0[:], Ab[:, bass.ds(b, 1), h0 * S2:h1 * S2], start=False, stop=True)
                            ins.then_inc(s["sc_ready"], 1)
                    if live(t, 3, NT):
                        T, i = t - 3, 1 - u
                        b = T // TB
                        eng.wait_ge(s["probs_done"], T + 1)

                        def turn(k):
                            if k >= 2 or has_before(T, 1):
                                eng.wait_ge(s["pT_taken"], 3 * T + k - 1)
                            for r in PGROUPS[k]:
                                rows = P if r < NR - 1 else lastrows
                                o = (3 + (i + k) % 2) * BANK + (r % 4) * P
                                ins = eng.transpose(psum[0:rows, o:o + P], pr[i][:, P * r:P * r + rows], ident[:])
                            ins.then_inc(s["pT_ready"], 1)

                        def product(k):
                            eng.wait_ge(s["pT_taken"], 3 * T + k + 1)
                            if k == 0 and has_before(T, 2):
                                eng.wait_ge(s["x_added"], T - 1)
                            for r in PGROUPS[k]:
                                rows = P if r < NR - 1 else lastrows
                                ins = eng.matmul(bank(5 + i, 0, D), pT[i][0:rows, r, :], VO[0:rows, bass.ds(b, 1), r, :],
                                                 start=r == 0, stop=r == NR - 1)
                            if k == 2:
                                ins.then_inc(s["out_ready"], 1)

                        turn(0)
                        turn(1)
                        product(0)
                        turn(2)
                        product(1)
                        product(2)
                pipeline(eng, NT, 6, 2, body)
            parts["tensor"].append(pe_main)

            def dve_main(eng):
                def body(t, u):
                    if live(t, 1, NT):
                        T, i = t - 1, 1 - u
                        eng.wait_ge(s["ln_rstd"], T + 1)
                        if has_before(T, 2):
                            eng.wait_ge(s["lnT_ready"], T - 1)
                        eng.tensor_scalar(lnx[i][:], x[:, bass.ds(T, 1), :].rearrange("p a n -> p (a n)"), mv[:, i, 0:1], rstd[:, i:i + 1],
                                          ALU.subtract, ALU.mult).then_inc(s["ln_done"], 1)
                    if live(t, 2, NT):
                        T, i = t - 2, u
                        v = sc[i][:].rearrange("p (h k) -> p h k", k=S2)
                        if has_before(T, 2):
                            eng.wait_ge(s["exp_done"], T - 1)
                        if L.fside:
                            eng.wait_ge(s["side_loaded"], 32 * (T // CT + 1))
                            for g, (o, h0, h1) in enumerate(BANKS):
                                eng.wait_ge(s["sc_ready"], 3 * T + g + 1)
                                eng.tensor_tensor(v[:, h0:h1, :], of_bank(g), of_tile(fs, T, h0, h1), ALU.mult).then_inc(s["sc_freed"], 1)
                            eng.wait_ge(s["sc_freed"], 3 * T + 3)
                            eng.scalar_tensor_tensor(out=v, in0=of_tile(mk, T, 0, H), scalar=L.mask_value, in1=v,
                                                     op0=ALU.mult, op1=ALU.add).then_inc(s["sc_steps"], 1)
                            eng.wait_ge(s["sc_steps"], NSC * T + 1)
                            eng.tensor_reduce(mx[:, i, :], v, AX, ALU.max).then_inc(s["sc_steps"], 1)
                        elif L.mask_value is not None:
                            for g, (o, h0, h1) in enumerate(BANKS):
                                eng.wait_ge(s["sc_ready"], 3 * T + g + 1)
                                eng.tensor_tensor(v[:, h0:h1, :], of_bank(g), ma3[:, bass.ds(T, 1), :].broadcast_to([P, h1 - h0, S2]),
                                                  ALU.add).then_inc(s["sc_freed"], 1)
                            eng.wait_ge(s["sc_freed"], 3 * T + 3)
                            eng.tensor_reduce(mx[:, i, :], v, AX, ALU.max).then_inc(s["sc_steps"], 1)
                        else:
                            for g, (o, h0, h1) in enumerate(BANKS):
                                eng.wait_ge(s["sc_ready"], 3 * T + g + 1)
                                ins = eng.tensor_reduce(mx[:, i, h0:h1], of_bank(g), AX, ALU.max)
                            ins.then_inc(s["sc_steps"], 1)
                            eng.wait_ge(s["sc_steps"], T + 1)
                            for g, (o, h0, h1) in enumerate(BANKS):
                                eng.tensor_tensor(v[:, h0:h1, :], of_bank(g), mx[:, i, h0:h1].unsqueeze(2).broadcast_to([P, h1 - h0, S2]),
                                                  ALU.subtract).then_inc(s["sc_freed"], 1)
                    if live(t, 0, NT):
                        T, i = t, u
                        if has_before(T, 2):
                            eng.wait_ge(s["ln_rstd"], T - 1)
                        eng.bn_stats(stats[:, i, :], x[:, bass.ds(T, 1), :].rearrange("p a n -> p (a n)")).then_inc(s["ln_stats"], 1)
                        eng.wait_ge(s["ln_stats"], 3 * T + 1)
                        eng.memset(spare[:], 0.0)
                        eng.bn_aggr(mv[:, i, :], stats[:, i, :]).then_inc(s["ln_stats"], 1)
                        eng.wait_ge(s["ln_stats"], 3 * T + 2)
                        eng.tensor_scalar(ve[:, i:i + 1], mv[:, i, 1:2], EPS, None, ALU.add).then_inc(s["ln_stats"], 1)
                    if live(t, 3, NT):
                        T, i = t - 3, 1 - u
                        eng.wait_ge(s["exp_done"], T + 1)
                        eng.tensor_reduce(sm[:, i, :], pr[i][:, 0:HK].rearrange("p (h k) -> p h k", k=S2), AX, ALU.add).then_inc(s["sum_steps"], 1)
                        eng.wait_ge(s["sum_steps"], 2 * T + 1)
                        if has_before(T, 2):
                            eng.wait_ge(s["probs_done"], T - 1)
                        eng.reciprocal(rs[:, i, :], sm[:, i, :]).then_inc(s["sum_steps"], 1)
                    if live(t, 4, NT):
                        T = t - 4
                        eng.wait_ge(s["out_ready"], T + 1)
                        xt = x[:, bass.ds(T, 1), :].rearrange("p a n -> p (a n)")
                        eng.tensor_tensor(xt, xt, bank(5 + u % 2, 0, D), ALU.add).then_inc(s["x_added"], 1)
                if not L.fside and L.mask_value:
                    eng.wait_ge(s["mask_added"], 1)
                pipeline(eng, NT, 6, 2, body)
            parts["vector"].append(dve_main)

            def act_main(eng):
                def body(t, u):
                    if live(t, 0, NT):
                        T, i = t, u
                        eng.wait_ge(s["lnT_ready"], T + 1)
                        if has_before(T, 2):
                            eng.wait_ge(s["sc_ready"], 3 * (T - 1))
                        eng.activation(lnT[i][:].rearrange("p a n -> p (a n)"), bank(7, 0, KT * P), ACT.Copy).then_inc(s["lnT_taken"], 1)
                    if live(t, 3, NT):
                        T, i = t - 3, 1 - u
                        if has_before(T, 2):
                            eng.wait_ge(s["out_ready"], T - 1)
                        for k in range(3):
                            eng.wait_ge(s["pT_ready"], 3 * T + k + 1)
                            o = (3 + (i + k) % 2) * BANK
                            full = [r for r in PGROUPS[k] if r < NR - 1]
                            ins = eng.activation(pT[i][:, full[0]:full[-1] + 1, :].rearrange("p a n -> p (a n)"), psum[:, o:o + len(full) * P], ACT.Copy)
                            if k == 2:
                                ins = eng.activation(pT[i][0:lastrows, NR - 1, :], psum[0:lastrows, o + P:o + 2 * P], ACT.Copy)
                            ins.then_inc(s["pT_taken"], 1)
                    if live(t, 1, NT):
                        T, i = t - 1, 1 - u
                        if L.mask_value is None:
                            eng.wait_ge(s["sc_freed"], 3 * T + 3)
                        else:
                            eng.wait_ge(s["shifted"], T + 1)
                        if has_before(T, 2):
                            eng.wait_ge(s["pT_ready"], 3 * (T - 1))
                        eng.activation(pr[i][:, 0:HK], sc[i][:], ACT.Exp).then_inc(s["exp_done"], 1)
                pipeline(eng, NT, 6, 2, body)
            parts["scalar"].append(act_main)

            def pool_main(eng):
                for i in range(2):
                    eng.memset(pr[i][:, HK:HK + 1], 1.0).then_inc(s["pr_ones"], 1)
                if not L.fside and L.mask_value:
                    eng.wait_ge(s["side_loaded"], 32)
                    eng.tensor_scalar(ma3[:], mk3[:], L.mask_value, 1.0, ALU.mult, ALU.mult).then_inc(s["mask_added"], 1)

                def body(t, u):
                    if live(t, 2, NT):
                        T, i = t - 2, u
                        if L.mask_value is not None:
                            v = sc[i][:].rearrange("p (h k) -> p h k", k=S2)
                            eng.wait_ge(s["sc_steps"], NSC * (T + 1))
                            eng.tensor_tensor(v, v, mx[:, i, :].unsqueeze(2).broadcast_to([P, H, S2]), ALU.subtract).then_inc(s["shifted"], 1)
                    if live(t, 0, NT):
                        T, i = t, u
                        eng.wait_ge(s["ln_stats"], 3 * T + 3)
                        if has_before(T, 2):
                            eng.wait_ge(s["ln_done"], T - 1)
                        eng.tensor_tensor(rstd[:, i:i + 1], ve[:, i:i + 1], mhalf[:, 0:1], ALU.pow).then_inc(s["ln_rstd"], 1)
                    if live(t, 3, NT):
                        T, i = t - 3, 1 - u
                        v = pr[i][:, 0:HK].rearrange("p (h k) -> p h k", k=S2)
                        eng.wait_ge(s["sum_steps"], 2 * T + 2)
                        eng.tensor_tensor(v, v, rs[:, i, :].unsqueeze(2).broadcast_to([P, H, S2]), ALU.mult).then_inc(s["probs_done"], 1)
                pipeline(eng, NT, 6, 2, body)
            parts["gpsimd"].append(pool_main)
            barrier()

        ln_stats = sem("ln_stats")
        ln_rstd = sem("ln_rstd")
        ln_done = sem("ln_done")
        lnT_ready = sem("lnT_ready")
        lnT_taken = sem("lnT_taken")
        EACH = 2 * CT + 1
        ln_calls = [0]

        def normalise(n, lnx, lnT=None, logits=None, take_logits=None):
            c0 = NC * ln_calls[0]
            ln_calls[0] += 1

            def dve_ln(eng):
                with eng.Fori(0, NC) as c:
                    for q in range(CT):
                        eng.bn_stats(stats[:, q, :], x[:, bass.ds(CT * c + q, 1), :].rearrange("p a n -> p (a n)")).then_inc(ln_stats, 1)
                    eng.wait_ge(ln_stats, EACH * (c + c0) + CT)
                    eng.memset(spare[:], 0.0)
                    for q in range(CT):
                        eng.bn_aggr(mv[:, q, :], stats[:, q, :]).then_inc(ln_stats, 1)
                    eng.wait_ge(ln_stats, EACH * (c + c0) + 2 * CT)
                    eng.tensor_scalar(ve[:, 0:CT], mv[:, 0:CT, 1], EPS, None, ALU.add).then_inc(ln_stats, 1)
                    eng.wait_ge(ln_rstd, c + (c0 + 1))
                    for q in range(CT):
                        ins = eng.tensor_scalar(lnx[:, bass.ds(CT * c + q, 1), :].rearrange("p a n -> p (a n)"),
                                                x[:, bass.ds(CT * c + q, 1), :].rearrange("p a n -> p (a n)"),
                                                mv[:, q, 0:1], rstd[:, q:q + 1], ALU.subtract, ALU.mult)
                    ins.then_inc(ln_done, 1)
            parts["vector"].append(dve_ln)

            def pool_ln(eng):
                with eng.Fori(0, NC) as c:
                    eng.wait_ge(ln_stats, EACH * (c + (c0 + 1)))
                    eng.tensor_tensor(rstd[:, 0:CT], ve[:, 0:CT], mhalf[:, 0:CT], ALU.pow).then_inc(ln_rstd, 1)
            parts["gpsimd"].append(pool_ln)
            if lnT is None:
                return c0

            def pe_ln(eng):
                for c in range(NC):
                    eng.wait_ge(ln_done, c0 + c + 1)
                    for kt in range(KT):
                        for q in range(CT):
                            ins = eng.transpose(bank(2 * c + kt, P * q, P), lnx[:, CT * c + q, P * kt:P * kt + P], ident[:])
                        ins.then_inc(lnT_ready, 1)
                    if logits:
                        eng.wait_ge(lnT_taken, 2 * (c0 + c + 1))
                        logits(eng, c)
                eng.wait_ge(lnT_taken, 2 * (c0 + NC))
            parts["tensor"].append(pe_ln)

            def act_ln(eng):
                for c in range(NC):
                    for kt in range(KT):
                        eng.wait_ge(lnT_ready, 2 * (c0 + c) + kt + 1)
                        eng.activation(lnT[:, kt, CN * c:CN * (c + 1)], bank(2 * c + kt), ACT.Copy).then_inc(lnT_taken, 1)
                    if take_logits:
                        take_logits(eng, c)
            parts["scalar"].append(act_ln)
            return c0

        def feed_forward(n, nf, first_routed=None, per_weight=1, experts=0, route=None, gated=True, biased=False):
            R = Region(start)
            lnT = R(n + "lnT", [P, KT, NC * CN])
            lnx = R(n + "lnx", [P, NT, D])
            wg = R(n + "wg", [P, KT, nf * P])
            wu = R(n + "wu", [P, KT, nf * P]) if gated else None
            wd = R(n + "wd", [P, nf, D])
            hT = [R(n + f"hT{i}", [P, CN]) for i in range(3)]
            th = [R(n + f"th{i}", [P, CN]) for i in range(2)]
            pairs = [(wg[:], d[n + "wg"]), (wd[:], d[n + "wd"])] + ([(wu[:], d[n + "wu"])] if gated else [])
            if experts:
                ns = (nf - first_routed) // per_weight
                wr = R(n + "wr", [P, KT, experts])
                sel = R(n + "sel", [experts, ns, P])
                cw = R(n + "cw", [P, CT, experts])
                tl = R(n + "tl", [P, NT, experts])
                cwT = R(n + "cwT", [experts, CN])
                pairs += [(wr[:], d[n + "wr"]), (sel[:], d[n + "sel"])]
            if biased:
                b1 = R(n + "b1", [P, nf])
                b2 = R(n + "b2", [P, D])
                pairs += [(b1[:], d[n + "b1"]), (b2[:], d[n + "b2"])]
            more = route(n, R, pairs, tl, cw) if experts else None
            loads(n, pairs)

            g_ready = sem(n + "g_ready")
            h_done = sem(n + "h_done")
            out_ready = sem(n + "out_ready")
            x_added = sem(n + "x_added")
            h_steps = sem(n + "h_steps")
            if gated:
                u_ready = sem(n + "u_ready")
                th_done = sem(n + "th_done")
            if experts:
                logits_ready = sem(n + "logits_ready")
                tl_done = sem(n + "tl_done")
                c_ready = sem(n + "c_ready")
                cw_done = sem(n + "cw_done")
                cwT_ready = sem(n + "cwT_ready")
                cwT_taken = sem(n + "cwT_taken")

            def logits(eng, c):
                for q in range(CT):
                    for kt in range(KT):
                        t = CT * c + q
                        ins = eng.matmul(bank(2 * c, experts * q, experts), lnT[:, kt, P * t:P * t + P], wr[:, kt, :],
                                         start=kt == 0, stop=kt == KT - 1)
                ins.then_inc(logits_ready, 1)

            def take_logits(eng, c):
                eng.wait_ge(logits_ready, c + 1)
                eng.activation(tl[:, CT * c:CT * (c + 1), :].rearrange("p q e -> p (q e)"), bank(2 * c, 0, CT * experts),
                               ACT.Tanh, scale=more.scale).then_inc(tl_done, 1)
            await_weights(n)
            if experts:
                more.first()
            normalise(n, lnx, lnT, logits if experts else None, take_logits if experts else None)
            if experts:
                more.then(tl_done, cw_done)

            routed = [m for m in range(nf) if experts and m >= first_routed]
            nr = len(routed)
            steps = (2 * nf + nr) if gated else 0
            n_sel = nr // per_weight

            def pe_ff(eng):
                if experts:
                    eng.wait_ge(tl_done, NC)
                with eng.Fori(0, NC) as c:
                    def down(m):
                        eng.wait_ge(h_done, nf * c + m + 1)
                        if m == 0:
                            eng.wait_ge(x_added, c + 1)
                        for q in range(CT):
                            ins = eng.matmul(bank(5 + q // 2, D * (q % 2), D), hT[m % 3][:, P * q:P * q + P], wd[:, m, :],
                                             start=m == 0 and q % 2 == 0, stop=m == nf - 1, skip_group_check=True)
                        if m == nf - 1:
                            ins.then_inc(out_ready, 1)

                    for m in range(nf):
                        for kt in range(KT):
                            ins = eng.matmul(bank(m % 2), wg[:, kt, P * m:P * m + P], lnT[:, kt, bass.ds(CN * c, CN)],
                                             start=kt == 0, stop=kt == KT - 1)
                        ins.then_inc(g_ready, 1)
                        if gated:
                            for kt in range(KT):
                                ins = eng.matmul(bank(2 + m % 2), wu[:, kt, P * m:P * m + P], lnT[:, kt, bass.ds(CN * c, CN)],
                                                 start=kt == 0, stop=kt == KT - 1)
                            ins.then_inc(u_ready, 1)
                        if m in routed and routed.index(m) % per_weight == 0:
                            r = routed.index(m) // per_weight
                            if r == 0:
                                eng.wait_ge(cw_done, c + 1)
                                for q in range(CT):
                                    ins = eng.transpose(bank(7, P * q, P)[0:experts], cw[:, q, :], ident[:])
                                ins.then_inc(cwT_ready, 1)
                                eng.wait_ge(cwT_taken, c + 1)
                            eng.matmul(bank((4, 7)[r % 2]), sel[:, r, :], cwT[:], start=True, stop=True).then_inc(c_ready, 1)
                        if m >= 1:
                            down(m - 1)
                    down(nf - 1)
            parts["tensor"].append(pe_ff)

            def act_ff(eng):
                with eng.Fori(0, NC) as c:
                    for m in range(nf):
                        eng.wait_ge(g_ready, nf * c + m + 1)
                        if gated:
                            if m >= 2:
                                eng.wait_ge(h_done, nf * c + m - 1)
                            eng.activation(th[m % 2][:], bank(m % 2), ACT.Tanh, scale=0.5).then_inc(th_done, 1)
                            if experts and m == routed[0]:
                                eng.wait_ge(cwT_ready, c + 1)
                                eng.activation(cwT[:], bank(7)[0:experts], ACT.Copy).then_inc(cwT_taken, 1)
                        else:
                            eng.activation(hT[m % 3][:], bank(m % 2), ACT.Relu, bias=b1[:, m:m + 1]).then_inc(h_done, 1)
            parts["scalar"].append(act_ff)

            def dve_ff(eng):
                eng.memset(spare[:], 0.0).then_inc(x_added, 1)
                with eng.Fori(0, NC) as c:
                    k = 0

                    def step(ins):
                        nonlocal k
                        k += 1
                        ins.then_inc(h_steps, 1)
                        eng.wait_ge(h_steps, c * inner + k)
                    if experts:
                        more.after(eng, c, -1)
                    for m in range(nf if gated else 0):
                        h = hT[m % 3][:]
                        eng.wait_ge(u_ready, nf * c + m + 1)
                        eng.wait_ge(th_done, nf * c + m + 1)
                        step(eng.scalar_tensor_tensor(out=h, in0=th[m % 2][:], scalar=1.0, in1=bank(2 + m % 2), op0=ALU.add, op1=ALU.mult))
                        last = eng.scalar_tensor_tensor(out=h, in0=h, scalar=0.5, in1=bank(m % 2), op0=ALU.mult, op1=ALU.mult)
                        if m in routed:
                            r = routed.index(m) // per_weight
                            step(last)
                            eng.wait_ge(c_ready, n_sel * c + r + 1)
                            last = eng.tensor_tensor(h, h, bank((4, 7)[r % 2]), ALU.mult)
                        last.then_inc(h_done, 1)
                        if experts:
                            more.after(eng, c, m)
                    eng.wait_ge(out_ready, c + 1)
                    for k2 in range(2):
                        xt = x[:, bass.ds(CT * c + 2 * k2, 2), :].rearrange("p a n -> p (a n)")
                        ins = eng.tensor_tensor(xt, xt, bank(5 + k2), ALU.add)
                        if biased:
                            step(ins)
                            xt3 = x[:, bass.ds(CT * c + 2 * k2, 2), :]
                            ins = eng.tensor_tensor(xt3, xt3, b2[:].unsqueeze(1).broadcast_to([P, 2, D]), ALU.add)
                    ins.then_inc(x_added, 1)
            inner = (nf + nr if gated else 0) + (2 if biased else 0)
            parts["vector"].append(dve_ff)
            barrier()

        def rank_below(step, eng, v, gt, eq, tri, cnt, sel, rows, n, k):
            a = v.unsqueeze(2).broadcast_to([P, rows, n, n])
            b = v.unsqueeze(3).broadcast_to([P, rows, n, n])
            step(eng.tensor_tensor(gt, a, b, ALU.is_gt))
            step(eng.tensor_tensor(eq, a, b, ALU.is_equal))
            step(eng.tensor_tensor(eq, eq, tri[:].unsqueeze(1).broadcast_to([P, rows, n, n]), ALU.mult))
            step(eng.tensor_tensor(gt, gt, eq, ALU.add))
            step(eng.tensor_reduce(cnt, gt, AX, ALU.add))
            step(eng.tensor_scalar(sel, cnt, float(k), None, ALU.is_lt))

        class GroupRoute:
            scale = 0.5
            E, G = 16, 4

            def __init__(self, n, R, pairs, tl, cw):
                self.n, self.tl, self.cw = n, tl, cw
                E, G = self.E, self.G
                self.bias = R(n + "bias", [P, E])
                self.tri4 = R(n + "tri4", [P, G, G])
                self.tri16 = R(n + "tri16", [P, E, E])
                self.score, self.sb, self.m1, self.sel = (R(n + k, [P, CT, E]) for k in ("score", "sb", "m1", "sel"))
                self.two = R(n + "two", [P, CT * G, 6])
                self.gs, self.gcnt, self.gsel = (R(n + k, [P, CT, G]) for k in ("gs", "gcnt", "gsel"))
                self.g4, self.e4 = (R(n + k, [P, CT, G, G]) for k in ("g4", "e4"))
                self.g16, self.e16 = (R(n + k, [P, CT, E, E]) for k in ("g16", "e16"))
                self.cnt = R(n + "cnt", [P, CT, E])
                self.total = R(n + "total", [P, CT])
                pairs += [(self.bias[:], d[n + "bias"]), (self.tri4[:], d["tri4"]), (self.tri16[:], d["tri16"])]

            def first(self):
                pass

            STEPS = 27

            def then(self, tl_done, cw_done):
                self.tl_done, self.cw_done = tl_done, cw_done
                self.route_steps = sem(self.n + "route_steps")

            def after(self, eng, c, m):
                E, G = self.E, self.G
                if m == -1:
                    self.k = 0

                def step(ins):
                    self.k += 1
                    ins.then_inc(self.route_steps, 1)
                    eng.wait_ge(self.route_steps, c * self.STEPS + self.k)
                every = lambda t: t.unsqueeze(3).broadcast_to([P, CT, G, E // G])
                if m == 0:
                    eng.wait_ge(self.tl_done, c + 1)
                    step(eng.tensor_scalar(self.score[:], self.tl[:, bass.ds(CT * c, CT), :], 0.5, 0.5, ALU.mult, ALU.add))
                    step(eng.tensor_tensor(self.sb[:], self.score[:], self.bias[:].unsqueeze(1).broadcast_to([P, CT, E]), ALU.add))
                    v = self.sb[:].rearrange("p q (g k) -> p (q g) k", g=G)
                    two = self.two[:]
                    step(eng.tensor_tensor(two[:, :, 0:2], v[:, :, 0:2], v[:, :, 2:4], ALU.add))
                    step(eng.tensor_tensor(two[:, :, 2:4], v[:, :, 0:4:2], v[:, :, 1:4:2], ALU.add))
                    step(eng.tensor_tensor(two[:, :, 4:5], v[:, :, 0:1], v[:, :, 3:4], ALU.add))
                    step(eng.tensor_tensor(two[:, :, 5:6], v[:, :, 1:2], v[:, :, 2:3], ALU.add))
                    step(eng.tensor_reduce(self.gs[:].rearrange("p q g -> p (q g)"), two, AX, ALU.max))
                    rank_below(step, eng, self.gs[:], self.g4[:], self.e4[:], self.tri4, self.gcnt[:], self.gsel[:], CT, G, 2)
                    step(eng.tensor_tensor(self.m1[:].rearrange("p q (g k) -> p q g k", g=G), self.sb[:].rearrange("p q (g k) -> p q g k", g=G),
                                           every(self.gsel[:]), ALU.mult))
                    step(eng.tensor_scalar(self.gcnt[:], self.gsel[:], -1.0, 1e30, ALU.add, ALU.mult))
                    step(eng.tensor_tensor(self.m1[:].rearrange("p q (g k) -> p q g k", g=G), self.m1[:].rearrange("p q (g k) -> p q g k", g=G),
                                           every(self.gcnt[:]), ALU.add))
                if m == 1:
                    rank_below(step, eng, self.m1[:], self.g16[:], self.e16[:], self.tri16, self.cnt[:], self.sel[:], CT, E, 4)
                if m == 2:
                    step(eng.tensor_tensor(self.sel[:], self.sel[:], self.score[:], ALU.mult))
                    step(eng.tensor_reduce(self.total[:], self.sel[:], AX, ALU.add))
                    step(eng.tensor_scalar(self.total[:], self.total[:], 1e-20, None, ALU.add))
                    step(eng.reciprocal(self.total[:], self.total[:]))
                    step(eng.tensor_tensor(self.cw[:], self.sel[:], self.total[:].unsqueeze(2).broadcast_to([P, CT, E]), ALU.mult))
                    eng.memset(spare[:], 0.0).then_inc(self.cw_done, 1)
                    assert self.k == self.STEPS

        class ZoneRoute:
            E = 8
            CENTER = math.exp(-1.0)
            LOWER, UPPER = 0.5 - math.log(4.0 / 3.0), 0.5

            def __init__(self, n, R, pairs, tl, cw):
                self.n, self.tl, self.cw = n, tl, cw
                E = self.E
                self.temp = R(n + "temp", [P, 1])
                self.half = R(n + "half", [P, 1])
                self.scale = self.half[:, 0:1]
                self.tri8 = R(n + "tri8", [P, E, E])
                self.inh, self.zone, self.low, self.dist, self.w, self.fb = (R(n + k, [P, NT, E]) for k in ("inh", "zone", "low", "dist", "w", "fb"))
                self.g8, self.e8 = (R(n + k, [P, NT, E, E]) for k in ("g8", "e8"))
                self.cnt, self.sel, self.dif = (R(n + k, [P, NT, E]) for k in ("cnt", "sel", "dif"))
                self.total, self.none = R(n + "total", [P, NT]), R(n + "none", [P, NT])
                pairs += [(self.temp[:], d[n + "temp"]), (self.tri8[:], d["tri8"])]
                self.half_done = sem(n + "half_done")

            def first(self):
                def dve_half(eng):
                    eng.reciprocal(self.half[:], self.temp[:]).then_inc(self.half_done, 1)
                    eng.wait_ge(self.half_done, 1)
                    eng.tensor_scalar(self.half[:], self.half[:], 0.5, None, ALU.mult).then_inc(self.half_done, 1)
                parts["vector"].append(dve_half)
                parts["scalar"].append(lambda eng: eng.wait_ge(self.half_done, 2))

            def then(self, tl_done, cw_done):
                self.cw_done = cw_done
                zone_steps = sem(self.n + "zone_steps")
                exps_done = sem(self.n + "exps_done")
                route_steps = sem(self.n + "route_steps")
                E = self.E

                def dve_zone(eng):
                    eng.wait_ge(tl_done, NC)
                    eng.tensor_scalar(self.inh[:], self.tl[:], 0.5, 0.5, ALU.mult, ALU.add).then_inc(zone_steps, 1)
                    eng.wait_ge(zone_steps, 1)
                    eng.tensor_scalar(self.low[:], self.inh[:], self.LOWER, None, ALU.is_ge).then_inc(zone_steps, 1)
                    eng.tensor_scalar(self.dist[:], self.inh[:], self.CENTER, None, ALU.subtract).then_inc(zone_steps, 1)
                    eng.wait_ge(zone_steps, 3)
                    eng.scalar_tensor_tensor(out=self.zone[:], in0=self.inh[:], scalar=self.UPPER, in1=self.low[:], op0=ALU.is_le, op1=ALU.mult).then_inc(zone_steps, 1)
                    eng.scalar_tensor_tensor(out=self.dist[:], in0=self.dist[:], scalar=-1.0, in1=self.dist[:], op0=ALU.mult, op1=ALU.max).then_inc(zone_steps, 1)
                parts["vector"].append(dve_zone)

                def act_exps(eng):
                    eng.wait_ge(zone_steps, 5)
                    eng.activation(self.w[:], self.dist[:], ACT.Exp, scale=-1 / 0.1).then_inc(exps_done, 1)
                    eng.activation(self.fb[:], self.dist[:], ACT.Exp, scale=-1 / 0.3).then_inc(exps_done, 1)
                parts["scalar"].append(act_exps)

                def dve_route(eng):
                    count = 0

                    def step(ins):
                        nonlocal count
                        count += 1
                        ins.then_inc(route_steps, 1)
                        eng.wait_ge(route_steps, count)
                    every = lambda t: t.unsqueeze(2).broadcast_to([P, NT, E])
                    w, fb, total, none, sel = self.w[:], self.fb[:], self.total[:], self.none[:], self.sel[:]
                    eng.wait_ge(exps_done, 2)
                    step(eng.tensor_tensor(w, w, self.zone[:], ALU.mult))
                    rank_below(step, eng, fb, self.g8[:], self.e8[:], self.tri8, self.cnt[:], sel, NT, E, 2)
                    step(eng.tensor_tensor(sel, sel, fb, ALU.mult))
                    step(eng.tensor_reduce(total, sel, AX, ALU.add))
                    step(eng.tensor_scalar(total, total, 1e-8, None, ALU.max))
                    step(eng.reciprocal(total, total))
                    step(eng.tensor_tensor(sel, sel, every(total), ALU.mult))
                    step(eng.tensor_reduce(total, w, AX, ALU.add))
                    step(eng.tensor_scalar(none, total, 1e-8, None, ALU.is_lt))
                    step(eng.tensor_tensor(self.dif[:], sel, every(none), ALU.mult))
                    step(eng.tensor_scalar(none, none, -1.0, 1.0, ALU.mult, ALU.add))
                    step(eng.tensor_tensor(sel, w, every(none), ALU.mult))
                    step(eng.tensor_tensor(sel, sel, self.dif[:], ALU.add))
                    step(eng.tensor_reduce(total, sel, AX, ALU.add))
                    step(eng.tensor_scalar(total, total, 1e-8, None, ALU.max))
                    step(eng.reciprocal(total, total))
                    step(eng.tensor_tensor(sel, sel, every(total), ALU.mult))
                parts["vector"].append(dve_route)

            def after(self, eng, c, m):
                if m == -1:
                    eng.tensor_copy(self.cw[:], self.sel[:, bass.ds(CT * c, CT), :]).then_inc(self.cw_done, 1)

        def gate_attention(n):
            R = Region(start)
            lnx = R(n + "lnx", [P, NT, D])
            lnT = R(n + "lnT", [P, KT, NC * CN])
            W = R(n + "W", [P, KT, D])
            Ws = R(n + "Ws", [P, KT, D])
            bcol = R(n + "bcol", [P, KT])
            wide = R(n + "wide", [P, KT, 63])
            cB = R(n + "cB", [P, 2, KT, P])
            bc = R(n + "bc", [P, 2])
            qm = R(n + "qm", [P, B, S2], I32)
            txt = R(n + "txt", [P, KT, B * S2])
            txtb = R(n + "txtb", [P, KT, S2])
            ctab = R(n + "ctab", [P, 2, B * S2])
            madd = R(n + "madd", [P, B, S2])
            fT = R(n + "fT", [P, KT, S])
            RING = 8
            ring = [R(n + f"ring{i}", [P, S]) for i in range(RING)]
            rhoT = R(n + "rhoT", [96, S])
            rho = R(n + "rho", [P, TB, S2])
            prod = R(n + "prod", [P, TB, S2])
            mx, sm, rs = (R(n + k, [P, TB]) for k in ("mx", "sm", "rs"))
            g = R(n + "g", [P, 2, TB])
            loads(n, [(W[:], d[n + "W"]), (Ws[:], d[n + "Ws"]), (bcol[:], d[n + "b"]), (wide[:], d[n + "wide"]),
                      (cB[:], d[n + "cB"]), (bc[:], d[n + "bc"]), (qm[:], d[n + "qm"])])
            await_weights(n)
            normalise(n, lnx, lnT)
            tab_ready = sem(n + "tab_ready")
            tab_steps = sem(n + "tab_steps")
            f_ready = sem(n + "f_ready")
            f_taken = sem(n + "f_taken")
            txt_moved = sem(n + "txt_moved")
            tanh_done = sem(n + "tanh_done")
            rho_added = sem(n + "rho_added")
            rhoT_taken = sem(n + "rhoT_taken")
            rho_ready = sem(n + "rho_ready")
            soft = sem(n + "soft")
            exp_done = sem(n + "exp_done")
            gates_done = sem(n + "gates_done")
            order = [(t, e) for r in range(32) for e in range(KT) for t in (r, r + 32, r + 64) if t < S2]
            n_ord = len(order)

            def pe_tables(eng):
                for e in range(KT):
                    for kt in range(KT):
                        ins = eng.matmul(bank(e, 0, B * S2), Ws[:, kt, P * e:P * e + P], ctxT[:, kt, :], start=kt == 0, stop=kt == KT - 1)
                    ins.then_inc(tab_ready, 1)
                for e in range(2):
                    for kt in range(KT):
                        ins = eng.matmul(bank(2 + e, 0, B * S2), cB[:, e, kt, :], ctxT[:, kt, :], start=kt == 0, stop=kt == KT - 1)
                    ins.then_inc(tab_ready, 1)
                eng.wait_ge(tab_steps, 5)
            parts["tensor"].append(pe_tables)

            def dve_tables(eng):
                for e in range(KT):
                    eng.wait_ge(tab_ready, e + 1)
                    eng.tensor_scalar(txt[:, e, :], bank(e, 0, B * S2), bcol[:, e:e + 1], None, ALU.add).then_inc(tab_steps, 1)
                for e in range(2):
                    eng.wait_ge(tab_ready, 3 + e)
                    eng.tensor_copy(ctab[:, e, :], bank(2 + e, 0, B * S2)).then_inc(tab_steps, 1)
                eng.tensor_scalar(madd[:], qm[:], 1.0, 1e30, ALU.subtract, ALU.mult).then_inc(tab_steps, 1)
                eng.wait_ge(tab_steps, 5)
            parts["vector"].append(dve_tables)

            def pe_gate(eng):
                with eng.Fori(0, B) as b:
                    for e in range(KT):
                        for half in range(2):
                            k = 2 * e + half
                            for kt in range(KT):
                                ins = eng.matmul(bank(2 + k), W[:, kt, P * e:P * e + P], lnT[:, kt, bass.ds(b * S + half * CN, CN)],
                                                 start=kt == 0, stop=kt == KT - 1)
                            ins.then_inc(f_ready, 1)
                    for k, (t, e) in enumerate(order):
                        eng.wait_ge(tanh_done, n_ord * b + k + 1)
                        q, r = t // 32, t % 32
                        for half in range(2):
                            ins = eng.matmul(bank(half)[32 * q:32 * q + 32], wide[:, e, 31 - r:63 - r], ring[k % RING][:, half * CN:(half + 1) * CN],
                                             start=r == 0 and e == 0, stop=(t, e) == (last_of[q], KT - 1))
                        ins.then_inc(rho_added, 1)
                    eng.wait_ge(rhoT_taken, 2 * b + 2)
                    for j in range(TB):
                        ins = eng.transpose(bank(6 + j // 4, S2 * (j % 4), S2), rhoT[0:S2, P * j:P * j + P], ident[0:S2, 0:S2])
                    ins.then_inc(rho_ready, 1)
                    eng.wait_ge(soft, SOFT * b + 1)
            last_of = [31, 63, S2 - 1]
            SOFT = 8
            parts["tensor"].append(pe_gate)

            def act_gate(eng):
                with eng.Fori(0, B) as b:
                    for k in range(4):
                        eng.wait_ge(f_ready, 4 * b + k + 1)
                        eng.activation(fT[:, k // 2, (k % 2) * CN:(k % 2 + 1) * CN], bank(2 + k), ACT.Copy).then_inc(f_taken, 1)
                    eng.wait_ge(f_taken, 4 * b + 4)
                    eng.wait_ge(txt_moved, b + 1)
                    for k, (t, e) in enumerate(order):
                        if k >= RING:
                            eng.wait_ge(rho_added, n_ord * b + k - RING + 1)
                        eng.activation(ring[k % RING][:], fT[:, e, :], ACT.Tanh, bias=txtb[:, e, t:t + 1]).then_inc(tanh_done, 1)
                    eng.wait_ge(soft, SOFT * b + 3)
                    eng.activation(rho[:], rho[:], ACT.Exp).then_inc(exp_done, 1)
                    for i in range(2):
                        eng.wait_ge(soft, SOFT * b + 7 + i)
                        eng.activation(g[:, i, :], g[:, i, :], ACT.Tanh, bias=bc[:, i:i + 1]).then_inc(gates_done, 1)
            parts["scalar"].append(act_gate)

            def dve_gate(eng):
                with eng.Fori(0, B) as b:
                    eng.tensor_copy(txtb[:], txt[:, :, bass.ds(b * S2, S2)]).then_inc(txt_moved, 1)
                    eng.wait_ge(rho_added, n_ord * (b + 1))
                    for half in range(2):
                        eng.tensor_copy(rhoT[:, half * CN:(half + 1) * CN], bank(half)[0:96]).then_inc(rhoT_taken, 1)
                    eng.wait_ge(rho_ready, b + 1)
                    for k in range(2):
                        ins = eng.tensor_tensor(rho[:, 4 * k:4 * k + 4, :], bank(6 + k, 0, 4 * S2).rearrange("p (j t) -> p j t", t=S2),
                                                madd[:, bass.ds(b, 1), :].broadcast_to([P, 4, S2]), ALU.add)
                    ins.then_inc(soft, 1)
                    eng.wait_ge(soft, SOFT * b + 1)
                    eng.tensor_reduce(mx[:], rho[:], AX, ALU.max).then_inc(soft, 1)
                    eng.wait_ge(soft, SOFT * b + 2)
                    eng.tensor_tensor(rho[:], rho[:], mx[:].unsqueeze(2).broadcast_to([P, TB, S2]), ALU.subtract).then_inc(soft, 1)
                    eng.wait_ge(exp_done, b + 1)
                    eng.tensor_reduce(sm[:], rho[:], AX, ALU.add).then_inc(soft, 1)
                    eng.wait_ge(soft, SOFT * b + 4)
                    eng.reciprocal(rs[:], sm[:]).then_inc(soft, 1)
                    for i in range(2):
                        if i:
                            eng.wait_ge(dots, 4 * b + 2)
                        eng.tensor_tensor(prod[:], rho[:], ctab[:, i, bass.ds(b * S2, S2)].unsqueeze(1).broadcast_to([P, TB, S2]), ALU.mult).then_inc(dots, 1)
                        eng.wait_ge(dots, 4 * b + 2 * i + 1)
                        eng.tensor_reduce(g[:, i, :], prod[:], AX, ALU.add).then_inc(dots, 1)
                    eng.wait_ge(dots, 4 * b + 4)
                    eng.wait_ge(soft, SOFT * b + 5)
                    eng.memset(spare[:], 0.0).then_inc(soft, 1)
                    eng.tensor_tensor(g[:, 0, :], g[:, 0, :], rs[:], ALU.mult).then_inc(soft, 1)
                    eng.tensor_tensor(g[:, 1, :], g[:, 1, :], rs[:], ALU.mult).then_inc(soft, 1)
                    eng.wait_ge(gates_done, 2 * b + 2)
                    for j in range(TB):
                        xt = x[:, bass.ds(TB * b + j, 1), :].rearrange("p a n -> p (a n)")
                        eng.scalar_tensor_tensor(out=xt, in0=lnx[:, bass.ds(TB * b + j, 1), :].rearrange("p a n -> p (a n)"), scalar=g[:, 0, j:j + 1],
                                                 in1=xt, op0=ALU.mult, op1=ALU.add).then_inc(scaled, 1)
                    for j in range(TB):
                        xt = x[:, bass.ds(TB * b + j, 1), :].rearrange("p a n -> p (a n)")
                        eng.wait_ge(scaled, TB * b + j + 1)
                        eng.tensor_scalar(xt, xt, g[:, 1, j:j + 1], None, ALU.add)
            dots = sem(n + "dots")
            scaled = sem(n + "scaled")
            parts["vector"].append(dve_gate)
            barrier()

        def quantised(n):
            NF, ROUND = 8, 1.5 * 2 ** 23
            R = Region(start)
            lnx = R(n + "lnx", [P, NT, D])
            w1 = R(n + "w1", [P, NF, D])
            w2 = R(n + "w2", [P, KT, NF * P])
            b1 = R(n + "b1", [P, NF])
            b2 = R(n + "b2", [P, KT])
            q1 = R(n + "q1", [P, NF, D], BF16)
            q2 = R(n + "q2", [P, KT, NF * P], BF16)
            q1T = R(n + "q1T", [P, KT, NF * P], BF16)
            q2T = R(n + "q2T", [P, NF, D], BF16)
            s1, i1, s2, i2 = (R(n + k, [P, w]) for k, w in (("s1", NF), ("i1", NF), ("s2", KT), ("i2", KT)))
            qx = R(n + "qx", [P, CT, D])
            qxb = R(n + "qxb", [P, NT, D], BF16)
            qxT = R(n + "qxT", [P, KT, NC * CN], BF16)
            h = R(n + "h", [P, NF, NC * CN])
            hq = R(n + "hq", [P, CN])
            qh = [R(n + f"qh{i}", [P, CN], BF16) for i in range(3)]
            sc1, bi1, bi2 = R(n + "sc1", [P, NF]), R(n + "bi1", [P, NF]), R(n + "bi2", [P, KT])
            row = R(n + "row", [P, 2, D])
            diag = R(n + "diag", [P, 2, KT, P])
            mxx, mall, sx, ix = (R(n + k, [P, w]) for k, w in (("mxx", 1), ("mall", 2), ("sx", 2), ("ix", 2)))
            mh, mh1 = R(n + "mh", [P, NC * NF]), R(n + "mh1", [P, 1])
            tmp = R(n + "tmp", [P, NF])
            loads(n, [(w1[:], d[n + "w1"]), (w2[:], d[n + "w2"]), (b1[:], d[n + "b1"]), (b2[:], d[n + "b2"])])
            await_weights(n)
            c0 = normalise(n, lnx)
            st = sem(n + "st")
            maxed = sem(n + "maxed")
            wT_ready = sem(n + "wT_ready")
            wT_taken = sem(n + "wT_taken")
            qx_done = sem(n + "qx_done")
            qxT_ready = sem(n + "qxT_ready")
            qxT_taken = sem(n + "qxT_taken")
            p1_ready = sem(n + "p1_ready")
            h_done = sem(n + "h_done")
            h_maxed = sem(n + "h_maxed")
            hq_steps = sem(n + "hq_steps")
            qh_used = sem(n + "qh_used")
            row_ready = sem(n + "row_ready")
            out_ready = sem(n + "out_ready")
            qsteps = sem(n + "qsteps")
            osteps = sem(n + "osteps")

            def dve_weights(eng):
                k = 0

                def step(ins):
                    nonlocal k
                    k += 1
                    ins.then_inc(st, 1)
                    eng.wait_ge(st, k)
                for w, s, i, qf, nt, b in ((w1, s1, i1, q1, NF, b1), (w2, s2, i2, q2, KT, b2)):
                    step(eng.tensor_reduce(s[:], w[:], AX, ALU.max))
                    step(eng.tensor_reduce(i[:], w[:], AX, ALU.min))
                    step(eng.scalar_tensor_tensor(out=s[:], in0=i[:], scalar=-1.0, in1=s[:], op0=ALU.mult, op1=ALU.max))
                    step(eng.tensor_scalar(s[:], s[:], 1e-8, 1.0 / 127.0, ALU.max, ALU.mult))
                    step(eng.reciprocal(i[:], s[:]))
                    for t in range(nt):
                        ins = eng.tensor_scalar(w[:, t, :], w[:, t, :], i[:, t:t + 1], ROUND, ALU.mult, ALU.add)
                    step(ins)
                    step(eng.tensor_scalar(qf[:], w[:], ROUND, None, ALU.subtract))
                eng.wait_ge(ln_done, c0 + NC)
                step(eng.tensor_reduce(mxx[:], lnx[:].rearrange("p t n -> p (t n)"), AX, ALU.max))
                eng.wait_ge(maxed, 1)
                step(eng.tensor_scalar(sx[:, 0:1], mall[:, 0:1], 1e-8, 1.0 / 255.0, ALU.max, ALU.mult))
                step(eng.reciprocal(ix[:, 0:1], sx[:, 0:1]))
                step(eng.tensor_scalar(sc1[:], s1[:], sx[:, 0:1], None, ALU.mult))
                step(eng.reciprocal(tmp[:], sc1[:]))
                step(eng.tensor_tensor(tmp[:], tmp[:], b1[:], ALU.mult))
                step(eng.tensor_scalar(tmp[:], tmp[:], ROUND, None, ALU.add))
                step(eng.tensor_scalar(tmp[:], tmp[:], ROUND, None, ALU.subtract))
                step(eng.tensor_tensor(bi1[:], tmp[:], sc1[:], ALU.mult))
            N_WEIGHT = 7 * 2
            N_MAX = N_WEIGHT + 1
            N_ALL = N_MAX + 8
            parts["vector"].append(dve_weights)

            def pool_max(eng):
                eng.wait_ge(st, N_MAX)
                eng.partition_all_reduce(mall[:, 0:1], mxx[:], P, bass.bass_isa.ReduceOp.max).then_inc(maxed, 1)
            parts["gpsimd"].append(pool_max)

            def dve_qx(eng):
                with eng.Fori(0, NC) as c:
                    t4 = lnx[:, bass.ds(CT * c, CT), :]
                    eng.tensor_scalar(qx[:], t4, ix[:, 0:1], 0.0, ALU.mult, ALU.max).then_inc(qsteps, 1)
                    eng.wait_ge(qsteps, 3 * c + 1)
                    eng.tensor_scalar(qx[:], qx[:], 255.0, ROUND, ALU.min, ALU.add).then_inc(qsteps, 1)
                    eng.wait_ge(qsteps, 3 * c + 2)
                    eng.tensor_scalar(qxb[:, bass.ds(CT * c, CT), :], qx[:], ROUND, None, ALU.subtract).then_inc(qsteps, 1)
                    eng.wait_ge(qsteps, 3 * c + 3)
                    eng.memset(spare[:], 0.0).then_inc(qx_done, 1)
            parts["vector"].append(dve_qx)

            def bankb(i, a, w):
                return bank(i)[:, a // 2:(a + w) // 2].bitcast(BF16)

            def pe_wT(eng):
                eng.wait_ge(st, N_WEIGHT)
                for kt in range(KT):
                    for f in range(NF):
                        ins = eng.transpose(bankb(kt, P * f, P), q1[:, f, P * kt:P * kt + P], identb[:])
                    ins.then_inc(wT_ready, 1)
                for half in range(2):
                    for f4 in range(4):
                        f = 4 * half + f4
                        for kt in range(KT):
                            ins = eng.transpose(bankb(2 + half, D * f4 + P * kt, P), q2[:, kt, P * f:P * f + P], identb[:])
                    ins.then_inc(wT_ready, 1)
            parts["tensor"].append(pe_wT)

            def act_wT(eng):
                for i in range(4):
                    eng.wait_ge(wT_ready, i + 1)
                    dst = q1T[:, i, :] if i < 2 else q2T[:, 4 * (i - 2):4 * (i - 1), :].rearrange("p f n -> p (f n)")
                    eng.activation(dst, bankb(i, 0, 1024), ACT.Copy).then_inc(wT_taken, 1)
            parts["scalar"].append(act_wT)

            def pe_qxT(eng):
                for c in range(NC):
                    eng.wait_ge(qx_done, c + 1)
                    if c >= 2:
                        eng.wait_ge(qxT_taken, 2 * (c - 1))
                    for kt in range(KT):
                        for q in range(CT):
                            ins = eng.transpose(bankb(4 + 2 * (c % 2) + kt, P * q, P), qxb[:, CT * c + q, P * kt:P * kt + P], identb[:])
                        ins.then_inc(qxT_ready, 1)
                eng.wait_ge(qxT_taken, 2 * NC)
                eng.wait_ge(wT_taken, 4)
            parts["tensor"].append(pe_qxT)

            def act_qxT(eng):
                for c in range(NC):
                    for kt in range(KT):
                        eng.wait_ge(qxT_ready, 2 * c + kt + 1)
                        eng.activation(qxT[:, kt, CN * c:CN * (c + 1)], bankb(4 + 2 * (c % 2) + kt, 0, CN), ACT.Copy).then_inc(qxT_taken, 1)
            parts["scalar"].append(act_qxT)

            def pe_p1(eng):
                with eng.Fori(0, NC) as c:
                    for f in range(NF):
                        eng.wait_ge(h_done, NF * c + 1)
                        for kt in range(KT):
                            ins = eng.matmul(bank(f), q1T[:, kt, P * f:P * f + P], qxT[:, kt, bass.ds(CN * c, CN)], start=kt == 0, stop=kt == KT - 1)
                        ins.then_inc(p1_ready, 1)
            parts["tensor"].append(pe_p1)

            def act_p1(eng):
                eng.wait_ge(st, N_ALL)
                eng.activation(spare[:], spare[:], ACT.Copy).then_inc(h_done, 1)
                with eng.Fori(0, NC) as c:
                    for f in range(NF):
                        eng.wait_ge(p1_ready, NF * c + f + 1)
                        eng.activation(h[:, f, bass.ds(CN * c, CN)], bank(f), ACT.Relu, bias=bi1[:, f:f + 1], scale=sc1[:, f:f + 1]).then_inc(h_done, 1)
            parts["scalar"].append(act_p1)

            def dve_p1(eng):
                with eng.Fori(0, NC) as c:
                    for f in range(NF):
                        eng.wait_ge(h_done, NF * c + f + 2)
                        eng.tensor_reduce(mh[:, bass.ds(NF * c + f, 1)], h[:, f, bass.ds(CN * c, CN)], AX, ALU.max).then_inc(h_maxed, 1)
                k = N_ALL

                def step(ins):
                    nonlocal k
                    k += 1
                    ins.then_inc(st, 1)
                    eng.wait_ge(st, k)
                eng.wait_ge(h_maxed, NF * NC)
                step(eng.tensor_reduce(mh1[:], mh[:], AX, ALU.max))
                eng.wait_ge(maxed, 2)
                step(eng.tensor_scalar(sx[:, 1:2], mall[:, 1:2], 1e-8, 1.0 / 255.0, ALU.max, ALU.mult))
                step(eng.reciprocal(ix[:, 1:2], sx[:, 1:2]))
                step(eng.tensor_scalar(s2[:], s2[:], sx[:, 1:2], None, ALU.mult))
                step(eng.reciprocal(i2[:], s2[:]))
                step(eng.tensor_tensor(bi2[:], i2[:], b2[:], ALU.mult))
                step(eng.tensor_scalar(bi2[:], bi2[:], ROUND, None, ALU.add))
                step(eng.tensor_scalar(bi2[:], bi2[:], ROUND, None, ALU.subtract))
                step(eng.tensor_tensor(bi2[:], bi2[:], s2[:], ALU.mult))
                for kt in range(KT):
                    eng.tensor_scalar(diag[:, 0, kt, :], ident[:], s2[:, kt:kt + 1], None, ALU.mult)
                    ins = eng.tensor_scalar(diag[:, 1, kt, :], ident[:], bi2[:, kt:kt + 1], None, ALU.mult)
                step(ins)
            parts["vector"].append(dve_p1)

            def pool_max2(eng):
                eng.wait_ge(st, N_ALL + 1)
                eng.partition_all_reduce(mall[:, 1:2], mh1[:], P, bass.bass_isa.ReduceOp.max).then_inc(maxed, 1)
            parts["gpsimd"].append(pool_max2)

            def pe_row(eng):
                eng.wait_ge(st, N_ALL + 10)
                eng.wait_ge(h_done, NF * NC + 1)
                for i in range(2):
                    for kt in range(KT):
                        ins = eng.matmul(bank(6, D * i + P * kt, P), ones[:], diag[:, i, kt, :], start=True, stop=True)
                ins.then_inc(row_ready, 1)
            parts["tensor"].append(pe_row)
            parts["scalar"].append(lambda eng: (eng.wait_ge(row_ready, 1), eng.activation(row[:].rearrange("p i n -> p (i n)"), bank(6), ACT.Copy).then_inc(row_ready, 1)))

            def dve_p2(eng):
                eng.wait_ge(row_ready, 2)
                with eng.Fori(0, NC) as c:
                    for f in range(NF):
                        if f:
                            eng.wait_ge(hq_steps, NF * 2 * c + 2 * f)
                        eng.tensor_scalar(hq[:], h[:, f, bass.ds(CN * c, CN)], ix[:, 1:2], ROUND, ALU.mult, ALU.add).then_inc(hq_steps, 1)
                        eng.wait_ge(hq_steps, NF * 2 * c + 2 * f + 1)
                        if f >= 3:
                            eng.wait_ge(qh_used, NF * c + f - 2)
                        eng.tensor_scalar(qh[f % 3][:], hq[:], ROUND, None, ALU.subtract).then_inc(hq_steps, 1)
                    eng.wait_ge(qh_used, NF * (c + 1))
                    eng.wait_ge(hq_steps, NF * 2 * c + 2 * NF)
                    for k in range(2):
                        xt = x[:, bass.ds(CT * c + 2 * k, 2), :]
                        o = bank(2 * (k) + 0).rearrange("p (a n) -> p a n", a=2)
                        eng.tensor_tensor(ot[:, 2 * k:2 * k + 2, :], o, row[:, 0:1, :].broadcast_to([P, 2, D]), ALU.mult).then_inc(osteps, 1)
                        eng.wait_ge(osteps, 6 * c + 3 * k + 1)
                        eng.tensor_tensor(ot[:, 2 * k:2 * k + 2, :], ot[:, 2 * k:2 * k + 2, :], row[:, 1:2, :].broadcast_to([P, 2, D]), ALU.add).then_inc(osteps, 1)
                        eng.wait_ge(osteps, 6 * c + 3 * k + 2)
                        eng.tensor_tensor(xt, xt, ot[:, 2 * k:2 * k + 2, :], ALU.add).then_inc(osteps, 1)
            ot = R(n + "ot", [P, CT, D])
            parts["vector"].append(dve_p2)

            def pe_p2(eng):
                with eng.Fori(0, NC) as c:
                    for f in range(NF):
                        eng.wait_ge(hq_steps, NF * 2 * c + 2 * f + 2)
                        for q in range(CT):
                            ins = eng.matmul(bank(2 * (q // 2), D * (q % 2), D), qh[f % 3][:, P * q:P * q + P], q2T[:, f, :],
                                             start=f == 0 and q % 2 == 0, stop=f == NF - 1, skip_group_check=True)
                        ins.then_inc(qh_used, 1)
                    eng.wait_ge(osteps, 6 * c + 5)
            parts["tensor"].append(pe_p2)
            barrier()

        LAYERS = [lambda: attention(Attention("a0_", 1024, True, True, -1e30)),
                  lambda: feed_forward("f0_", 12, first_routed=4, experts=16, route=GroupRoute),
                  lambda: attention(Attention("a1_", 1024, False, False, None)),
                  lambda: feed_forward("f1_", 8, gated=False, biased=True),
                  lambda: gate_attention("a2_"),
                  lambda: feed_forward("f2_", 16, first_routed=0, per_weight=2, experts=8, route=ZoneRoute),
                  lambda: attention(Attention("a3_", 256, True, False, -1e15)),
                  lambda: quantised("f3_")]
        for i, make in enumerate(LAYERS):
            if make and i in only:
                make()

        def store_x(eng):
            for b in range(B):
                eng.dma_start(d["out"][b].rearrange("(p j) n -> p j n", p=P), x[:, TB * b:TB * (b + 1), :]).then_inc(stored, 16)
            eng.wait_ge(stored, 16 * B)
        parts["sync"].append(store_x)

        block = ctx.enter_context(nc.Block())

        @block.sync
        def _(eng):
            for part in parts["sync"]:
                part(eng)

        @block.tensor
        def _(eng):
            for part in parts["tensor"]:
                part(eng)

        @block.scalar
        def _(eng):
            for part in parts["scalar"]:
                part(eng)

        @block.vector
        def _(eng):
            for part in parts["vector"]:
                part(eng)

        @block.gpsimd
        def _(eng):
            for part in parts["gpsimd"]:
                part(eng)


def layouts(v):
    import numpy as np
    v = {k: np.asarray(a) for k, a in v.items()}
    rows = lambda a: np.ascontiguousarray(a.reshape(-1, P, a.shape[-1]).transpose(1, 0, 2))
    col = lambda a: np.ascontiguousarray(a.reshape(-1, P).T)
    every = lambda a: np.ascontiguousarray(np.broadcast_to(a, (P,) + a.shape))
    o = {"x": v["x"], "fside": v["fside_Bx16xSxS2_0"], "mask16": v["mask_Bx16xSxS2_bk1"], "mask1": v["mask_Bx1xSxS2_bk1"],
         "ident": np.eye(P, dtype=np.float32),
         "ctxT": rows(v["ctx_1024"].reshape(B * S2, D).T)}
    for n, l in (("a0_", "L0_xattn_"), ("a1_", "L1_xattn_"), ("a3_", "L3_xattn_")):
        w = {k: v[l + k] for k in ("Wq", "Wk", "Wv", "Wo")}
        dims = w["Wo"].size // D
        o[n + "WqT"] = rows(w["Wq"].reshape(D, dims).T)
        o[n + "Wk"] = rows(w["Wk"].reshape(D, dims))
        o[n + "Wv"] = rows(w["Wv"].reshape(D, dims))
        o[n + "Wo"] = rows(w["Wo"].reshape(dims, D))
        hd = dims // H
        o[n + "group"] = np.kron(np.eye(P // hd), np.ones((hd, 1))).astype(np.float32)
        if l + "bq" in v:
            o[n + "bk"], o[n + "bv"] = col(v[l + "bk"]), col(v[l + "bv"])
            o[n + "bqB"] = np.ascontiguousarray(np.broadcast_to(col(v[l + "bq"])[:, :, None], (P, dims // P, P)))
            o[n + "bo2"] = np.ascontiguousarray(np.broadcast_to(v[l + "bo"], (1, B, D)))
    inner = lambda a: a.transpose(1, 0, 2).reshape(D, -1)
    o["f0_wg"] = rows(np.concatenate([v["L0_ffn_shared_gate_w"].T, inner(v["L0_ffn_gate_w"])], 1))
    o["f0_wu"] = rows(np.concatenate([v["L0_ffn_shared_up_w"].T, inner(v["L0_ffn_up_w"])], 1))
    o["f0_wd"] = rows(np.concatenate([v["L0_ffn_shared_down_w"].T, v["L0_ffn_down_w"].reshape(-1, D)], 0))
    o["f0_wr"] = rows(v["L0_ffn_router_w"].T)
    o["f0_bias"] = every(v["L0_ffn_correction_bias"])
    o["f0_sel"] = np.kron(np.eye(16), np.ones((1, 64))).reshape(16, 8, P).astype(np.float32)
    o["f1_wg"], o["f1_wd"] = rows(v["L1_ffn_W1"]), rows(v["L1_ffn_W2"])
    o["f1_b1"], o["f1_b2"] = col(v["L1_ffn_b1"]), every(v["L1_ffn_b2"])
    o["a2_W"], o["a2_Ws"], o["a2_b"] = rows(v["L2_xattn_W"]), rows(v["L2_xattn_Ws"]), col(v["L2_xattn_b"].reshape(-1))
    wide = np.zeros((P, KT, 63), np.float32)
    wide[:, :, 31] = col(v["L2_xattn_w"].reshape(-1))
    o["a2_wide"] = wide
    o["a2_cB"] = np.ascontiguousarray(np.broadcast_to(
        np.stack([col(v["L2_xattn_Wcw"].reshape(-1)), col(v["L2_xattn_Wcb"].reshape(-1))], 1)[:, :, :, None], (P, 2, KT, P)))
    o["a2_bc"] = every(np.concatenate([v["L2_xattn_bcw"], v["L2_xattn_bcb"]]))
    o["a2_qm"] = every(v["mask_BxS2_ik0"])
    o["f2_wg"], o["f2_wu"] = rows(inner(v["L2_ffn_Wg"])), rows(inner(v["L2_ffn_Wu"]))
    o["f2_wd"], o["f2_wr"] = rows(v["L2_ffn_Wd"].reshape(-1, D)), rows(v["L2_ffn_Wr"])
    o["f2_temp"] = every(v["L2_ffn_temperature"])
    o["f2_sel"] = np.kron(np.eye(8), np.ones((1, P))).reshape(8, 8, P).astype(np.float32)
    o["f3_w1"], o["f3_w2"] = rows(v["L3_ffn_w1"]), rows(v["L3_ffn_w2"])
    o["f3_b1"], o["f3_b2"] = col(v["L3_ffn_b1"]), col(v["L3_ffn_b2"])
    for k in (4, 8, 16):
        o[f"tri{k}"] = every(np.tril(np.ones((k, k), np.float32), -1))
    return o


def kernel(**inputs):
    import numpy as np
    import concourse.bacc as bacc
    from concourse.bass_utils import run_bass_kernel_spmd as run

    nc = bacc.Bacc("TRN2", target_bir_lowering=False, num_devices=1)
    arrays, d = {}, {}
    for name, a in layouts(inputs).items():
        arrays[f"in_{name}"] = a
        d[name] = nc.dram_tensor(f"in_{name}", a.shape, mybir.dt.from_np(a.dtype), kind="ExternalInput").ap()
    d["out"] = nc.dram_tensor("out_x", (B, S, D), F32, kind="ExternalOutput").ap()
    build(nc, d)
    return run(nc, [arrays], core_ids=[0]).results[0]["out_x"]
```

```python
import math
from contextlib import ExitStack

import concourse.bass as bass
from concourse import mybir

F32 = mybir.dt.float32
F32R = mybir.dt.float32r
BF16 = mybir.dt.bfloat16
U8 = mybir.dt.uint8
I32 = mybir.dt.int32
ALU = mybir.AluOpType
ACT = mybir.ActivationFunctionType
AX = mybir.AxisListType.X

P = 128
B, S, D = 2, 1024, 256
NT = B * S // P
TB = S // P
KT = D // P
H, S2 = 16, 77
HK = H * S2
HPB = 6
BANK = 512
NR = -(-HK // P)
RLAST = HK - (NR - 1) * P
CT = 4
NC = NT // CT
CN = CT * P
EPS = 1e-5
PGROUPS = [range(0, 4), range(4, 8), range(8, NR)]
BANKS = [(512 * g, 6 * g, min(H, 6 * g + 6)) for g in range(3)]


class Attention:

    def __init__(self, name, dims, biased, fside, mask_value):
        self.name, self.dims, self.biased, self.fside, self.mask_value = name, dims, biased, fside, mask_value
        self.hd = dims // H
        self.scale = float(self.hd) ** -0.5
        self.nm = dims // P
        self.g = P // self.hd
        self.seg = self.g * S2


def pipeline(eng, n, lead, step, body):
    for t in range(lead):
        body(t, t % step)
    with eng.Fori(0, (n - lead) // step) as i:
        for u in range(step):
            body(i * step + (lead + u), (lead + u) % step)
    for t in range(n, n + lead):
        body(t, t % step)


def live(t, lag, n):
    return not isinstance(t, int) or 0 <= t - lag < n


def has_before(t, k):
    return not isinstance(t, int) or t >= k


def build(nc, d, only=range(8)):
    ctx = ExitStack()
    with ctx:
        def sem(name):
            return ctx.enter_context(nc.semaphore(name))

        base = -(-nc.sbuf_base // 32) * 32
        limit = nc.sbuf_usable_end

        class Region:

            def __init__(self, start, end=None):
                self.at, self.end = start, end or limit

            def __call__(self, name, shape, dt=F32):
                n = 1
                for s in shape[1:]:
                    n *= s
                size = -(-n * {F32: 4, F32R: 4, BF16: 2, U8: 1, I32: 4}[dt] // 32) * 32
                t = nc.alloc_sbuf_tensor_at(name, shape, dt, offset=self.at)
                self.at += size
                assert self.at <= self.end, (name, self.at - self.end)
                return t

        keep = Region(base)
        x = keep("x", [P, NT, D])
        ident = keep("ident", [P, P])
        identb = keep("identb", [P, P], BF16)
        ones = keep("ones", [P, P])
        ctxT = keep("ctxT", [P, KT, B * S2])
        mhalf = keep("mhalf", [P, NT])
        stats = keep("stats", [P, NT, 6])
        mv = keep("mv", [P, NT, 2])
        ve = keep("ve", [P, NT])
        rstd = keep("rstd", [P, NT])
        spare = keep("spare", [P, 1])
        start = keep.at

        psum = ctx.enter_context(nc.psum_tensor("psum", [P, 8 * BANK], F32))

        def bank(i, a=0, n=BANK):
            return psum[:, i * BANK + a:i * BANK + a + n]

        x_loaded = sem("x_loaded")
        const_loaded = sem("const_loaded")
        const_made = sem("const_made")
        layer_end = sem("layer_end")
        stored = sem("stored")
        parts = {e: [] for e in ("sync", "tensor", "scalar", "vector", "gpsimd")}
        ends = [0]

        def barrier():
            ends[0] += 1
            k = ends[0]
            for e in ("tensor", "scalar", "vector", "gpsimd"):
                def stop(eng, k=k):
                    eng.drain().then_inc(layer_end, 1)
                    eng.wait_ge(layer_end, 4 * k)
                parts[e].append(stop)

            def hold(eng, k=k):
                eng.wait_ge(layer_end, 4 * k)
            parts["sync"].append(hold)

        def load_constants(eng):
            eng.dma_start(ctxT[:], d["ctxT"]).then_inc(const_loaded, 16)
            eng.dma_start(ident[:], d["ident"]).then_inc(const_loaded, 16)
        parts["sync"].append(load_constants)

        def load_x(eng):
            for b in range(B):
                eng.dma_start(x[:, TB * b:TB * (b + 1), :], d["x"][b].rearrange("(p j) n -> p j n", p=P)).then_inc(x_loaded, 16)

        def make_constants(eng):
            eng.memset(ones[:], 1.0).then_inc(const_made, 1)
            eng.memset(mhalf[:], -0.5).then_inc(const_made, 1)
            eng.wait_ge(const_loaded, 32)
            eng.tensor_copy(identb[:], ident[:]).then_inc(const_made, 1)
        parts["gpsimd"].append(make_constants)

        def await_constants(eng):
            eng.wait_ge(const_made, 3)
            eng.wait_ge(const_loaded, 32)
        for e in ("tensor", "scalar", "vector", "gpsimd"):
            parts[e].append(await_constants)

        weights_loaded = sem("weights_loaded")
        kv_weights_loaded = sem("kv_weights_loaded")
        loads_until, kv_until = {"": 0}, {"": 0}
        load_weights = {}
        order_of_layers = [n for i, n in enumerate(("a0_", "f0_", "a1_", "f1_", "a2_", "f2_", "a3_", "f3_")) if i in only]

        def loads(name, pairs, kv_pairs=()):
            before = max(loads_until.values()), max(kv_until.values())
            loads_until[name] = before[0] + 16 * len(pairs)
            kv_until[name] = before[1] + 16 * len(kv_pairs)

            def go(eng):
                if before[0]:
                    eng.wait_ge(weights_loaded, before[0])
                if before[1] and kv_pairs:
                    eng.wait_ge(kv_weights_loaded, before[1])
                for dst, src in kv_pairs:
                    eng.dma_start(dst, src).then_inc(kv_weights_loaded, 16)
                for dst, src in pairs:
                    eng.dma_start(dst, src).then_inc(weights_loaded, 16)
            load_weights[name] = go
            if name == order_of_layers[0]:
                parts["sync"].append(go)
                parts["sync"].append(load_x)

        def load_weights_after(name, eng):
            k = order_of_layers.index(name) + 1
            if k < len(order_of_layers):
                load_weights[order_of_layers[k]](eng)

        def await_weights(name):
            for e in ("tensor", "scalar", "vector", "gpsimd"):
                parts[e].append(lambda eng: eng.wait_ge(weights_loaded, loads_until[name]))

        WEIGHTS = {"a0_": 33, "f0_": 43, "a1_": 33, "f1_": 22, "a2_": 12, "f2_": 53, "a3_": 9, "f3_": 17}
        weights_at, names = {}, list(WEIGHTS)
        for i, name in enumerate(names):
            top = limit if i % 2 == 0 else limit - 1024 * max(WEIGHTS[o] for o in names[i - 1:i + 2:2])
            weights_at[name] = (top // 32 * 32 - 1024 * WEIGHTS[name], top // 32 * 32)

        def region_end(n):
            k = names.index(n)
            return min(weights_at[o][0] for o in names[k:k + 2])

        kv_ready = sem("kv_ready")
        kv_taken = sem("kv_taken")
        fold_ready = sem("fold_ready")
        fold_taken = sem("fold_taken")
        prep = sem("fold_prepared")
        folds = {"kv": 0, "fold": 0, "prep": 0}
        attention_signals = {k: sem("tile_" + k) for k in (
        "ln_stats",
        "ln_rstd",
        "ln_done",
        "lnT_ready",
        "lnT_taken",
        "sc_ready",
        "sc_freed",
        "sc_steps",
        "shifted",
        "exp_done",
        "sum_steps",
        "probs_done",
        "pT_ready",
        "pT_taken",
        "out_ready",
        "x_added",
        )}
        attention_tiles = {"tiles": 0, "sc_steps": 0, "shifted": 0}

        def attention(L):
            nm, seg, g, n = L.nm, L.seg, L.g, L.name
            lastrows = RLAST + (1 if L.biased else 0)
            R = Region(start)
            A = R(n + "A", [P, KT, B, HK])
            VO = R(n + "VO", [P, B, NR, D])
            if L.fside:
                fs = R(n + "fs", [P, 2, H, CT * S2])
                mk = R(n + "mk", [P, 2, H, CT * S2], U8)

                def of_tile(side, T, h0, h1):
                    return side[:, bass.ds(T // CT % 2, 1), h0:h1, bass.ds(T % CT * S2, S2)].rearrange("p a h k -> p (a h) k")
            elif L.mask_value:
                mk3 = R(n + "mk3", [P, NT, S2], U8)
                ma3 = R(n + "ma3", [P, NT, S2])
            shared = R.at
            W = Region(*weights_at[n])
            wqT = W(n + "wqT", [P, nm, D])
            wk = W(n + "wk", [P, KT, L.dims])
            wv = W(n + "wv", [P, KT, L.dims])
            wo = W(n + "wo", [P, nm, D])
            F = Region(shared, weights_at[n][0])
            BDK = F(n + "BDK", [P, B, nm, seg])
            BDV = F(n + "BDV", [P, B, nm, P + seg + P])
            group = W(n + "group", [P, 2, g])
            kvb = W(n + "kvb", [P, 2, nm])
            if L.biased:
                bq = W(n + "bq", [P, nm])
            kv_pairs = [(wk[:], d[n + "Wk"]), (wv[:], d[n + "Wv"]), (group[:, 0, :], d[n + "group"])]
            pairs = [(wqT[:], d[n + "WqT"]), (wo[:], d[n + "Wo"])]
            if L.biased:
                kv_pairs += [(kvb[:, 0, :], d[n + "bk"]), (kvb[:, 1, :], d[n + "bv"])]
                pairs += [(bq[:], d[n + "bq"])]
            loads(n, pairs, kv_pairs)
            for e in ("tensor", "vector"):
                parts[e].append(lambda eng: eng.wait_ge(kv_weights_loaded, kv_until[n]))
            if L.biased:
                bo_loaded = sem(n + "bo_loaded")
                parts["sync"].append(lambda eng: eng.dma_start(VO[RLAST:RLAST + 1, :, NR - 1, :], d[n + "bo2"]).then_inc(bo_loaded, 16))
                parts["tensor"].append(lambda eng: eng.wait_ge(bo_loaded, 16))
            s = dict(attention_signals)
            if L.mask_value is not None:
                s["side_loaded"] = sem(n + "side_loaded")
                if not L.fside:
                    s["mask_added"] = sem(n + "mask_added")
            if L.biased:
                s["lnx_ones"] = sem(n + "lnx_ones")
            T0, SC0, SH0 = attention_tiles["tiles"], attention_tiles["sc_steps"], attention_tiles["shifted"]
            if L.fside:
                def load_side(eng, c):
                    if c >= 1:
                        eng.wait_ge(s["side_loaded"], 32 * c)
                    b, sl = c // 2, slice(c % 2 * CT * S2, (c % 2 + 1) * CT * S2)
                    eng.dma_start(fs[:, c % 2], d["fside"][b].rearrange("h (p j) k -> p h (j k)", p=P)[:, :, sl]).then_inc(s["side_loaded"], 16)
                    eng.dma_start(mk[:, c % 2], d["mask16"][b].rearrange("h (p j) k -> p h (j k)", p=P)[:, :, sl]).then_inc(s["side_loaded"], 16)

                def sp_side(eng):
                    for c in range(2):
                        load_side(eng, c)
                parts["sync"].append(sp_side)
            elif L.mask_value:
                def sp_mask(eng):
                    for b in range(B):
                        eng.dma_start(mk3[:, TB * b:TB * (b + 1), :], d["mask1"][b, 0].rearrange("(p j) k -> p j k", p=P)).then_inc(s["side_loaded"], 16)
                parts["sync"].append(sp_mask)

            kv0, fold0, prep0 = folds["kv"], folds["fold"], folds["prep"]

            def pe_kv(eng):
                for i in range(2 * nm):
                    m, w = i // 2, (wk, wv)[i % 2]
                    if i >= 4:
                        eng.wait_ge(kv_taken, kv0 + i - 3)
                    for kt in range(KT):
                        ins = eng.matmul(bank(i % 4, 0, B * S2), w[:, kt, P * m:P * m + P], ctxT[:, kt, :],
                                         start=kt == 0, stop=kt == KT - 1)
                    ins.then_inc(kv_ready, 1)
            parts["tensor"].append(pe_kv)

            def dve_kv(eng):
                eng.memset(BDV[:], 0.0).then_inc(prep, 1)
                eng.tensor_scalar(group[:, 1, :], group[:, 0, :], L.scale, None, ALU.mult).then_inc(prep, 1)
                if not L.biased:
                    eng.memset(kvb[:], 0.0).then_inc(prep, 1)
                eng.wait_ge(prep, prep0 + (2 if L.biased else 3))
                for i in range(2 * nm):
                    m, v = i // 2, i % 2
                    eng.wait_ge(kv_ready, kv0 + i + 1)
                    for b in range(B):
                        src = bank(i % 4, b * S2, S2).unsqueeze(1).broadcast_to([P, g, S2])
                        dst = BDV[:, b, m, P:P + seg] if v else BDK[:, b, m, :]
                        ins = eng.scalar_tensor_tensor(
                            out=dst.rearrange("p (g k) -> p g k", k=S2), in0=src, scalar=kvb[:, v, m:m + 1],
                            in1=group[:, 1 - v, :].unsqueeze(2).broadcast_to([P, g, S2]), op0=ALU.add, op1=ALU.mult)
                    ins.then_inc(kv_taken, 1)
                if L.biased:
                    eng.wait_ge(weights_loaded, loads_until[n])
                    for m in range(nm):
                        ins = eng.tensor_scalar(wqT[:, m, 1:D], wqT[:, m, 1:D], wqT[:, m, 0:1], None, ALU.subtract)
                    ins.then_inc(prep, 1)
                    eng.wait_ge(prep, prep0 + 3)
                    eng.tensor_copy(wqT[:, :, 0], bq[:]).then_inc(prep, 1)
            parts["vector"].append(dve_kv)

            jobs = [("A", b, kt) for b in range(B) for kt in range(KT)]
            jobs += [("VO", b, r) for b in range(B) for r in range(0, NR, 2)]

            def pe_fold(eng):
                eng.wait_ge(kv_taken, kv0 + 2 * nm)
                eng.wait_ge(weights_loaded, loads_until[n])
                if L.biased:
                    eng.wait_ge(prep, prep0 + 4)
                for i, (kind, b, k) in enumerate(jobs):
                    if i >= 2:
                        eng.wait_ge(fold_taken, fold0 + i - 1)
                    b0 = 3 * (i % 2)
                    if kind != "VO":
                        for off, h0, h1 in BANKS:
                            for m in range(nm):
                                lo, hi = max(h0 * S2, m * seg), min(h1 * S2, (m + 1) * seg)
                                if lo < hi:
                                    o = b0 * BANK + off + lo - h0 * S2
                                    ins = eng.matmul(psum[:, o:o + hi - lo], wqT[:, m, P * k:P * k + P], BDK[:, b, m, lo - m * seg:hi - m * seg],
                                                     start=True, stop=True)
                    else:
                        for r in (k, k + 1):
                            rows = P if r < NR - 1 else RLAST
                            ms = [m for m in range(nm) if m * seg < P * r + rows and (m + 1) * seg > P * r]
                            for m in ms:
                                c = P + P * r - m * seg
                                ins = eng.matmul(psum[0:rows, (b0 + r - k) * BANK:(b0 + r - k) * BANK + D],
                                                 BDV[:, b, m, c:c + rows], wo[:, m, :],
                                                 start=m == ms[0], stop=m == ms[-1])
                    ins.then_inc(fold_ready, 1)
            parts["tensor"].append(pe_fold)

            def act_fold(eng):
                for i, (kind, b, k) in enumerate(jobs):
                    eng.wait_ge(fold_ready, fold0 + i + 1)
                    b0 = 3 * (i % 2)
                    if kind != "VO":
                        for off, h0, h1 in BANKS:
                            ins = eng.activation(A[:, k, b, h0 * S2:h1 * S2], psum[:, b0 * BANK + off:b0 * BANK + off + (h1 - h0) * S2], ACT.Copy)
                    else:
                        for r in (k, k + 1):
                            rows = P if r < NR - 1 else RLAST
                            ins = eng.activation(VO[0:rows, b, r, :], psum[0:rows, (b0 + r - k) * BANK:(b0 + r - k) * BANK + D], ACT.Copy)
                    ins.then_inc(fold_taken, 1)
            parts["scalar"].append(act_fold)
            folds["kv"] += 2 * nm
            folds["fold"] += len(jobs)
            folds["prep"] += 4 if L.biased else 3
            barrier()

            M, M2 = Region(shared, weights_at[names[names.index(n) + 1]][0]), Region(*weights_at[n]) if L.fside else None
            lnx = [M(n + f"lnx{i}", [P, D]) for i in range(2)]
            lnT = [M(n + f"lnT{i}", [P, KT, P]) for i in range(2)]
            sc = [(M2 or M)(n + f"sc{i}", [P, HK]) for i in range(2)]
            pr = [(M2 or M)(n + f"pr{i}", [P, HK + 1]) for i in range(2)]
            pT = [M(n + f"pT{i}", [P, NR, P]) for i in range(2)]
            mx = M(n + "mx", [P, 2, H])
            sm = M(n + "sm", [P, 2, H])
            rs = M(n + "rs", [P, 2, H])

            NSC = 2 if L.fside else 1

            def of_bank(g):
                o, h0, h1 = BANKS[g]
                return psum[:, o:o + (h1 - h0) * S2].rearrange("p (h k) -> p h k", k=S2)

            if L.fside:
                def sp_side_late(eng):
                    load_weights_after(n, eng)
                    for c in range(2, NC):
                        eng.wait_ge(s["sc_steps"], SC0 + NSC * CT * (c - 1))
                        load_side(eng, c)
                parts["sync"].append(sp_side_late)
            else:
                parts["sync"].append(lambda eng: load_weights_after(n, eng))

            def pe_main(eng):
                if L.biased:
                    eng.wait_ge(s["lnx_ones"], 2)

                def body(t, u):
                    if live(t, 0, NT):
                        T, i = t, u
                        eng.wait_ge(s["ln_done"], T0 + T + 1)
                        if has_before(T, 1):
                            eng.wait_ge(s["lnT_taken"], T0 + T)
                        for kt in range(KT):
                            ins = eng.transpose(bank(7, P * kt, P), lnx[i][:, P * kt:P * kt + P], ident[:])
                        ins.then_inc(s["lnT_ready"], 1)
                    if live(t, 1, NT):
                        T, i = t - 1, 1 - u
                        b = T // TB
                        eng.wait_ge(s["lnT_taken"], T0 + T + 1)
                        for g, (o, h0, h1) in enumerate(BANKS):
                            if has_before(T, 1):
                                eng.wait_ge(s["sc_freed"], 3 * (T0 + T - 1) + g + 1)
                            w = (h1 - h0) * S2
                            for kt in range(KT):
                                ins = eng.matmul(psum[:, o:o + w], lnT[i][:, kt, :], A[:, kt, bass.ds(b, 1), h0 * S2:h1 * S2],
                                                 start=kt == 0, stop=kt == KT - 1)
                            ins.then_inc(s["sc_ready"], 1)
                    if live(t, 3, NT):
                        T, i = t - 3, 1 - u
                        b = T // TB
                        eng.wait_ge(s["probs_done"], T0 + T + 1)

                        def turn(k):
                            if k >= 2 or has_before(T, 1):
                                eng.wait_ge(s["pT_taken"], 3 * (T0 + T) + k - 1)
                            for r in PGROUPS[k]:
                                rows = P if r < NR - 1 else lastrows
                                o = (3 + (i + k) % 2) * BANK + (r % 4) * P
                                ins = eng.transpose(psum[0:rows, o:o + P], pr[i][:, P * r:P * r + rows], ident[:])
                            ins.then_inc(s["pT_ready"], 1)

                        def product(k):
                            eng.wait_ge(s["pT_taken"], 3 * (T0 + T) + k + 1)
                            if k == 0 and has_before(T, 2):
                                eng.wait_ge(s["x_added"], T0 + T - 1)
                            for r in PGROUPS[k]:
                                rows = P if r < NR - 1 else lastrows
                                ins = eng.matmul(bank(5 + i, 0, D), pT[i][0:rows, r, :], VO[0:rows, bass.ds(b, 1), r, :],
                                                 start=r == 0, stop=r == NR - 1)
                            if k == 2:
                                ins.then_inc(s["out_ready"], 1)

                        turn(0)
                        turn(1)
                        product(0)
                        turn(2)
                        product(1)
                        product(2)
                pipeline(eng, NT, 6, 2, body)
            parts["tensor"].append(pe_main)

            def dve_main(eng):
                eng.wait_ge(x_loaded, 16 * B)
                def body(t, u):
                    if live(t, 1, NT):
                        T, i = t - 1, 1 - u
                        eng.wait_ge(s["ln_rstd"], T0 + T + 1)
                        if has_before(T, 2):
                            eng.wait_ge(s["lnT_ready"], T0 + T - 1)
                        f0 = 1 if L.biased else 0
                        eng.tensor_scalar(lnx[i][:, f0:], x[:, bass.ds(T, 1), f0:].rearrange("p a n -> p (a n)"), mv[:, i, 0:1], rstd[:, i:i + 1],
                                          ALU.subtract, ALU.mult).then_inc(s["ln_done"], 1)
                    if live(t, 2, NT):
                        T, i = t - 2, u
                        v = sc[i][:].rearrange("p (h k) -> p h k", k=S2)
                        if has_before(T, 2):
                            eng.wait_ge(s["exp_done"], T0 + T - 1)
                        if L.fside:
                            eng.wait_ge(s["side_loaded"], 32 * (T // CT + 1))
                            for g, (o, h0, h1) in enumerate(BANKS):
                                eng.wait_ge(s["sc_ready"], 3 * (T0 + T) + g + 1)
                                eng.tensor_tensor(v[:, h0:h1, :], of_bank(g), of_tile(fs, T, h0, h1), ALU.mult).then_inc(s["sc_freed"], 1)
                            eng.wait_ge(s["sc_freed"], 3 * (T0 + T) + 3)
                            eng.scalar_tensor_tensor(out=v, in0=of_tile(mk, T, 0, H), scalar=L.mask_value, in1=v,
                                                     op0=ALU.mult, op1=ALU.add).then_inc(s["sc_steps"], 1)
                            eng.wait_ge(s["sc_steps"], SC0 + NSC * T + 1)
                            eng.tensor_reduce(mx[:, i, :], v, AX, ALU.max).then_inc(s["sc_steps"], 1)
                        elif L.mask_value is not None:
                            for g, (o, h0, h1) in enumerate(BANKS):
                                eng.wait_ge(s["sc_ready"], 3 * (T0 + T) + g + 1)
                                eng.tensor_tensor(v[:, h0:h1, :], of_bank(g), ma3[:, bass.ds(T, 1), :].broadcast_to([P, h1 - h0, S2]),
                                                  ALU.add).then_inc(s["sc_freed"], 1)
                            eng.wait_ge(s["sc_freed"], 3 * (T0 + T) + 3)
                            eng.tensor_reduce(mx[:, i, :], v, AX, ALU.max).then_inc(s["sc_steps"], 1)
                        else:
                            for g, (o, h0, h1) in enumerate(BANKS):
                                eng.wait_ge(s["sc_ready"], 3 * (T0 + T) + g + 1)
                                ins = eng.tensor_reduce(mx[:, i, h0:h1], of_bank(g), AX, ALU.max)
                            ins.then_inc(s["sc_steps"], 1)
                            eng.wait_ge(s["sc_steps"], SC0 + T + 1)
                            for g, (o, h0, h1) in enumerate(BANKS):
                                eng.tensor_tensor(v[:, h0:h1, :], of_bank(g), mx[:, i, h0:h1].unsqueeze(2).broadcast_to([P, h1 - h0, S2]),
                                                  ALU.subtract).then_inc(s["sc_freed"], 1)
                    if live(t, 0, NT):
                        T, i = t, u
                        if has_before(T, 2):
                            eng.wait_ge(s["ln_rstd"], T0 + T - 1)
                        eng.bn_stats(stats[:, i, :], x[:, bass.ds(T, 1), :].rearrange("p a n -> p (a n)")).then_inc(s["ln_stats"], 1)
                        eng.wait_ge(s["ln_stats"], 3 * (T0 + T) + 1)
                        eng.memset(spare[:], 0.0)
                        eng.bn_aggr(mv[:, i, :], stats[:, i, :]).then_inc(s["ln_stats"], 1)
                        eng.wait_ge(s["ln_stats"], 3 * (T0 + T) + 2)
                        eng.tensor_scalar(ve[:, i:i + 1], mv[:, i, 1:2], EPS, None, ALU.add).then_inc(s["ln_stats"], 1)
                    if live(t, 3, NT):
                        T, i = t - 3, 1 - u
                        eng.wait_ge(s["exp_done"], T0 + T + 1)
                        eng.tensor_reduce(sm[:, i, :], pr[i][:, 0:HK].rearrange("p (h k) -> p h k", k=S2), AX, ALU.add).then_inc(s["sum_steps"], 1)
                        eng.wait_ge(s["sum_steps"], 2 * (T0 + T) + 1)
                        if has_before(T, 2):
                            eng.wait_ge(s["probs_done"], T0 + T - 1)
                        eng.reciprocal(rs[:, i, :], sm[:, i, :]).then_inc(s["sum_steps"], 1)
                    if live(t, 4, NT):
                        T = t - 4
                        eng.wait_ge(s["out_ready"], T0 + T + 1)
                        xt = x[:, bass.ds(T, 1), :].rearrange("p a n -> p (a n)")
                        eng.tensor_tensor(xt, xt, bank(5 + u % 2, 0, D), ALU.add).then_inc(s["x_added"], 1)
                if not L.fside and L.mask_value:
                    eng.wait_ge(s["mask_added"], 1)
                pipeline(eng, NT, 6, 2, body)
            parts["vector"].append(dve_main)

            def act_main(eng):
                def body(t, u):
                    if live(t, 0, NT):
                        T, i = t, u
                        eng.wait_ge(s["lnT_ready"], T0 + T + 1)
                        if has_before(T, 2):
                            eng.wait_ge(s["sc_ready"], 3 * (T0 + T - 1))
                        eng.activation(lnT[i][:].rearrange("p a n -> p (a n)"), bank(7, 0, KT * P), ACT.Copy).then_inc(s["lnT_taken"], 1)
                    if live(t, 3, NT):
                        T, i = t - 3, 1 - u
                        if has_before(T, 2):
                            eng.wait_ge(s["out_ready"], T0 + T - 1)
                        for k in range(3):
                            eng.wait_ge(s["pT_ready"], 3 * (T0 + T) + k + 1)
                            o = (3 + (i + k) % 2) * BANK
                            full = [r for r in PGROUPS[k] if r < NR - 1]
                            ins = eng.activation(pT[i][:, full[0]:full[-1] + 1, :].rearrange("p a n -> p (a n)"), psum[:, o:o + len(full) * P], ACT.Copy)
                            if k == 2:
                                ins = eng.activation(pT[i][0:lastrows, NR - 1, :], psum[0:lastrows, o + P:o + 2 * P], ACT.Copy)
                            ins.then_inc(s["pT_taken"], 1)
                    if live(t, 1, NT):
                        T, i = t - 1, 1 - u
                        if L.mask_value is None:
                            eng.wait_ge(s["sc_freed"], 3 * (T0 + T) + 3)
                        else:
                            eng.wait_ge(s["shifted"], SH0 + T + 1)
                        if has_before(T, 2):
                            eng.wait_ge(s["pT_ready"], 3 * (T0 + T - 1))
                        eng.activation(pr[i][:, 0:HK], sc[i][:], ACT.Exp).then_inc(s["exp_done"], 1)
                pipeline(eng, NT, 6, 2, body)
            parts["scalar"].append(act_main)

            def pool_main(eng):
                for i in range(2):
                    eng.memset(pr[i][:, HK:HK + 1], 1.0)
                    if L.biased:
                        eng.memset(lnx[i][:, 0:1], 1.0).then_inc(s["lnx_ones"], 1)
                if not L.fside and L.mask_value:
                    eng.wait_ge(s["side_loaded"], 32)
                    eng.tensor_scalar(ma3[:], mk3[:], L.mask_value, 1.0, ALU.mult, ALU.mult).then_inc(s["mask_added"], 1)

                def body(t, u):
                    if live(t, 2, NT):
                        T, i = t - 2, u
                        if L.mask_value is not None:
                            v = sc[i][:].rearrange("p (h k) -> p h k", k=S2)
                            eng.wait_ge(s["sc_steps"], SC0 + NSC * (T + 1))
                            eng.tensor_tensor(v, v, mx[:, i, :].unsqueeze(2).broadcast_to([P, H, S2]), ALU.subtract).then_inc(s["shifted"], 1)
                    if live(t, 0, NT):
                        T, i = t, u
                        eng.wait_ge(s["ln_stats"], 3 * (T0 + T) + 3)
                        if has_before(T, 2):
                            eng.wait_ge(s["ln_done"], T0 + T - 1)
                        eng.tensor_tensor(rstd[:, i:i + 1], ve[:, i:i + 1], mhalf[:, 0:1], ALU.pow).then_inc(s["ln_rstd"], 1)
                    if live(t, 3, NT):
                        T, i = t - 3, 1 - u
                        v = pr[i][:, 0:HK].rearrange("p (h k) -> p h k", k=S2)
                        eng.wait_ge(s["sum_steps"], 2 * (T0 + T) + 2)
                        eng.tensor_tensor(v, v, rs[:, i, :].unsqueeze(2).broadcast_to([P, H, S2]), ALU.mult).then_inc(s["probs_done"], 1)
                pipeline(eng, NT, 6, 2, body)
            parts["gpsimd"].append(pool_main)
            attention_tiles["tiles"] += NT
            attention_tiles["sc_steps"] += NSC * NT
            attention_tiles["shifted"] += NT if L.mask_value is not None else 0
            barrier()

        def matmul_split(eng, out, w_hi, w_lo, v_hi, v_lo, start, stop):
            eng.matmul(out, w_hi, v_hi, start=start, stop=False, skip_group_check=True)
            eng.matmul(out, w_hi, v_lo, start=False, stop=False, skip_group_check=True)
            return eng.matmul(out, w_lo, v_hi, start=False, stop=stop, skip_group_check=True)

        ln_stats = sem("ln_stats")
        ln_rstd = sem("ln_rstd")
        ln_done = sem("ln_done")
        lnT_ready = sem("lnT_ready")
        lnT_taken = sem("lnT_taken")
        lnT_lo_taken = sem("lnT_lo_taken")
        EACH = 2 * NT + 1
        calls = {"ln": 0, "lo": 0}

        def normalise(n, lnx, lnT=None, lnT_lo=None, logits=None, take_logits=None, dve_meanwhile=None):
            n0 = calls["ln"]
            c0 = NC * n0
            l0 = NC * calls["lo"]
            calls["ln"] += 1
            if lnT_lo is not None:
                calls["lo"] += 1

            def dve_ln(eng):
                eng.wait_ge(x_loaded, 16 * B)
                with eng.Fori(0, NC) as c:
                    for q in range(CT):
                        eng.bn_stats(stats[:, bass.ds(CT * c + q, 1), :].rearrange("p a n -> p (a n)"),
                                     x[:, bass.ds(CT * c + q, 1), :].rearrange("p a n -> p (a n)")).then_inc(ln_stats, 1)
                eng.wait_ge(ln_stats, EACH * n0 + NT)
                eng.memset(spare[:], 0.0)
                for T in range(NT):
                    eng.bn_aggr(mv[:, T, :], stats[:, T, :]).then_inc(ln_stats, 1)
                eng.wait_ge(ln_stats, EACH * n0 + 2 * NT)
                eng.tensor_scalar(ve[:], mv[:, :, 1], EPS, None, ALU.add).then_inc(ln_stats, 1)
                if dve_meanwhile:
                    dve_meanwhile(eng)
                eng.wait_ge(ln_rstd, n0 + 1)

                def low(c):
                    for kt in range(KT):
                        eng.wait_ge(lnT_taken, 2 * (c0 + c) + kt + 1)
                        eng.tensor_tensor(lnT_lo[:, kt, CN * c:CN * (c + 1)], bank(2 * c + kt), lnT[:, kt, CN * c:CN * (c + 1)].bitcast(F32),
                                          ALU.subtract).then_inc(lnT_lo_taken, 1)
                for c in range(NC):
                    for T in range(CT * c, CT * c + CT):
                        ins = eng.tensor_scalar(lnx[:, T, :], x[:, T, :], mv[:, T, 0:1], rstd[:, T:T + 1], ALU.subtract, ALU.mult)
                    ins.then_inc(ln_done, 1)
                    if lnT_lo is not None and c >= 1:
                        low(c - 1)
                if lnT_lo is not None:
                    low(NC - 1)
            parts["vector"].append(dve_ln)

            def pool_ln(eng):
                eng.wait_ge(ln_stats, EACH * (n0 + 1))
                eng.tensor_tensor(rstd[:], ve[:], mhalf[:], ALU.pow).then_inc(ln_rstd, 1)
            parts["gpsimd"].append(pool_ln)
            if lnT is None:
                return c0

            def pe_ln(eng):
                for c in range(NC + 1):
                    if c < NC:
                        eng.wait_ge(ln_done, c0 + c + 1)
                        for kt in range(KT):
                            for q in range(CT):
                                ins = eng.transpose(bank(2 * c + kt, P * q, P), lnx[:, CT * c + q, P * kt:P * kt + P], ident[:])
                            ins.then_inc(lnT_ready, 1)
                    if c >= 1 and lnT_lo is not None:
                        eng.wait_ge(lnT_lo_taken, 2 * (l0 + c))
                        if logits:
                            logits(eng, c - 1)
                eng.wait_ge(lnT_taken, 2 * (c0 + NC))
            parts["tensor"].append(pe_ln)

            def act_ln(eng):
                for c in range(NC + 1):
                    for kt in range(KT if c < NC else 0):
                        eng.wait_ge(lnT_ready, 2 * (c0 + c) + kt + 1)
                        eng.activation(lnT[:, kt, CN * c:CN * (c + 1)], bank(2 * c + kt), ACT.Copy).then_inc(lnT_taken, 1)
                    if take_logits and c >= 1:
                        take_logits(eng, c - 1)
            parts["scalar"].append(act_ln)
            return c0

        def feed_forward(n, nf, first_routed=None, per_weight=1, experts=0, route=None, gated=True, biased=False):
            W = Region(*weights_at[n])
            wg = W(n + "wg", [P, KT, nf * P])
            wu = W(n + "wu", [P, KT, nf * P]) if gated else None
            wd = W(n + "wd", [P, nf, D])
            R = Region(start, region_end(n))
            lnT = R(n + "lnT", [P, KT, NC * CN], F32R)
            lnT_lo = R(n + "lnT_lo", [P, KT, NC * CN], F32R)
            wg_hi = R(n + "wg_hi", [P, KT, nf * P], F32R)
            wu_hi = R(n + "wu_hi", [P, KT, nf * P], F32R) if gated else None
            wd_hi = R(n + "wd_hi", [P, nf, D], F32R)
            W_lo = Region(*weights_at[n])
            wg_lo = W_lo(n + "wg_lo", [P, KT, nf * P], F32R)
            wu_lo = W_lo(n + "wu_lo", [P, KT, nf * P], F32R) if gated else None
            wd_lo = W_lo(n + "wd_lo", [P, nf, D], F32R)
            I = Region(R.at, region_end(n))
            before_I = Region(R.at, region_end(n))
            lnx = R(n + "lnx", [P, NT, D])
            h = [I(n + f"h{i}", [P, CN]) for i in range(2)]
            h_hi = [I(n + f"h_hi{i}", [P, CN], F32R) for i in range(4)]
            h_lo = [I(n + f"h_lo{i}", [P, CN], F32R) for i in range(4)]
            R.at = max(R.at, I.at)
            th = [R(n + f"th{i}", [P, CN]) for i in range(2)]
            WG = 4
            NG = nf // WG
            pairs = [(wg[:], d[n + "wg"]), (wd[:], d[n + "wd"])] + ([(wu[:], d[n + "wu"])] if gated else [])
            if experts:
                ns = (nf - first_routed) // per_weight
                wr = W(n + "wr", [P, KT, experts])
                wr_hi = R(n + "wr_hi", [P, KT, experts], F32R)
                wr_lo = R(n + "wr_lo", [P, KT, experts], F32R)
                sel = W(n + "sel", [experts, ns, P])
                cw = R(n + "cw", [P, CT, experts])
                tl = R(n + "tl", [P, NT, experts])
                cwT = R(n + "cwT", [experts, CN], F32R)
                cwT_lo = R(n + "cwT_lo", [experts, CN], F32R)
                sel_r = R(n + "sel_r", [experts, ns, P], F32R)
                pairs += [(wr[:], d[n + "wr"]), (sel[:], d[n + "sel"])]
            if biased:
                b1 = W(n + "b1", [P, nf])
                b2 = W(n + "b2", [P, D])
                pairs += [(b1[:], d[n + "b1"]), (b2[:], d[n + "b2"])]
            more = route(n, R, W, before_I, pairs, tl, cw) if experts else None
            loads(n, pairs)
            parts["sync"].append(lambda eng: load_weights_after(n, eng))

            w_hi_done = sem(n + "w_hi_done")
            w_lo_done = sem(n + "w_lo_done")
            w_lo_more = sem(n + "w_lo_more")
            wr_done = sem(n + "wr_done")
            g_ready = sem(n + "g_ready")
            h_full = sem(n + "h_full")
            hi_done = sem(n + "hi_done")
            lo_done = sem(n + "lo_done")
            out_ready = sem(n + "out_ready")
            x_added = sem(n + "x_added")
            h_steps = sem(n + "h_steps")
            if gated:
                u_ready = sem(n + "u_ready")
                th_done = sem(n + "th_done")
            if experts:
                logits_ready = sem(n + "logits_ready")
                tl_done = sem(n + "tl_done")
                c_ready = sem(n + "c_ready")
                cw_done = sem(n + "cw_done")
                cwT_ready = sem(n + "cwT_ready")
                cwT_taken = sem(n + "cwT_taken")
                cwT_lo_taken = sem(n + "cwT_lo_taken")
                sel_done = sem(n + "sel_done")

            def logits(eng, c):
                eng.wait_ge(wr_done, 2)
                for q in range(CT):
                    for kt in range(KT):
                        t = CT * c + q
                        cols = slice(P * t, P * t + P)
                        ins = matmul_split(eng, bank(2 * c, experts * q, experts), lnT[:, kt, cols], lnT_lo[:, kt, cols],
                                           wr_hi[:, kt, :], wr_lo[:, kt, :], kt == 0, kt == KT - 1)
                ins.then_inc(logits_ready, 1)

            def take_logits(eng, c):
                eng.wait_ge(logits_ready, c + 1)
                eng.activation(tl[:, CT * c:CT * (c + 1), :].rearrange("p q e -> p (q e)"), bank(2 * c, 0, CT * experts),
                               ACT.Tanh, scale=more.scale).then_inc(tl_done, 1)
            await_weights(n)

            def of_group(k):
                a, b = WG * k, WG * (k + 1)
                up = [(w[:, :, P * a:P * b], hi[:, :, P * a:P * b], lo[:, :, P * a:P * b])
                      for w, hi, lo in ((wg, wg_hi, wg_lo),) + (((wu, wu_hi, wu_lo),) if gated else ())]
                return up + [(wd[:, a:b, :], wd_hi[:, a:b, :], wd_lo[:, a:b, :])]

            def act_weights(eng):
                for k in range(NG):
                    for whole, upper, lower in of_group(k):
                        ins = eng.activation(upper, whole, ACT.Copy)
                    ins.then_inc(w_hi_done, 1)
                if experts:
                    eng.activation(sel_r[:], sel[:], ACT.Copy).then_inc(sel_done, 1)
            parts["scalar"].append(act_weights)

            def dve_weights(eng):
                if experts:
                    eng.tensor_copy(wr_hi[:], wr[:]).then_inc(wr_done, 1)
                eng.wait_ge(w_hi_done, 1)
                for whole, upper, lower in of_group(0):
                    ins = eng.tensor_tensor(lower, whole, upper.bitcast(F32), ALU.subtract)
                ins.then_inc(w_lo_done, 1)
                if experts:
                    eng.wait_ge(wr_done, 1)
                    eng.tensor_tensor(wr_lo[:], wr[:], wr_hi[:].bitcast(F32), ALU.subtract).then_inc(wr_done, 1)

            if experts:
                more.first()
            normalise(n, lnx, lnT, lnT_lo, logits if experts else None, take_logits if experts else None, dve_weights)

            def pool_weights(eng):
                for k in range(1, NG):
                    eng.wait_ge(w_hi_done, k + 1)
                    for whole, upper, lower in of_group(k):
                        ins = eng.tensor_tensor(lower, whole, upper.bitcast(F32), ALU.subtract)
                    ins.then_inc(w_lo_more, 1)
            parts["gpsimd"].append(pool_weights)
            if experts:
                more.then(tl_done, cw_done)

            routed = [m for m in range(nf) if experts and m >= first_routed]
            nr = len(routed)
            n_sel = nr // per_weight
            LAG = 2

            def chunks(eng, body):
                body(0)
                with eng.Fori(0, NC - 1) as i:
                    body(i + 1)

            def first(c):
                return isinstance(c, int) and c == 0

            def pe_ff(eng):
                if experts:
                    eng.wait_ge(tl_done, NC)

                def down(c, m):
                    eng.wait_ge(lo_done, nf * c + m + 1)
                    if m == 0 and not first(c):
                        eng.wait_ge(x_added, c)
                    for q in range(CT):
                        cols = slice(P * q, P * q + P)
                        ins = matmul_split(eng, bank(5 + q // 2, D * (q % 2), D), h_hi[m % 4][:, cols], h_lo[m % 4][:, cols],
                                           wd_hi[:, m, :], wd_lo[:, m, :], m == 0 and q % 2 == 0, m == nf - 1)
                    if m == nf - 1:
                        ins.then_inc(out_ready, 1)

                def body(c):
                    for m in range(nf):
                        if first(c) and m == 0:
                            eng.wait_ge(w_lo_done, 1)
                        elif first(c) and m % WG == 0:
                            eng.wait_ge(w_lo_more, m // WG)
                        if not first(c) or m >= 2:
                            eng.wait_ge(h_full, nf * c + m - 1)
                        if experts and m == first_routed:
                            eng.wait_ge(cw_done, c + 1)
                            for q in range(CT):
                                ins = eng.transpose(bank(4, P * q, P)[0:experts], cw[:, q, :], ident[:])
                            ins.then_inc(cwT_ready, 1)
                        for ready, b0, hi, lo in ((g_ready, 0, wg_hi, wg_lo),) + (((u_ready, 2, wu_hi, wu_lo),) if gated else ()):
                            for kt in range(KT):
                                ins = matmul_split(eng, bank(b0 + m % 2), hi[:, kt, P * m:P * m + P], lo[:, kt, P * m:P * m + P],
                                                   lnT[:, kt, bass.ds(CN * c, CN)], lnT_lo[:, kt, bass.ds(CN * c, CN)], kt == 0, kt == KT - 1)
                            ins.then_inc(ready, 1)
                        if m >= LAG:
                            down(c, m - LAG)
                        elif not first(c):
                            down(c - 1, nf + m - LAG)
                        if m in routed and routed.index(m) % per_weight == 0:
                            r = routed.index(m) // per_weight
                            if r == 0:
                                eng.wait_ge(cwT_lo_taken, c + 1)
                                if first(c):
                                    eng.wait_ge(sel_done, 1)
                            eng.matmul(bank((4, 7)[r % 2]), sel_r[:, r, :], cwT[:], start=True, stop=False)
                            eng.matmul(bank((4, 7)[r % 2]), sel_r[:, r, :], cwT_lo[:], start=False, stop=True).then_inc(c_ready, 1)
                chunks(eng, body)
                for m in range(nf - LAG, nf):
                    down(NC - 1, m)
            parts["tensor"].append(pe_ff)

            def act_ff(eng):
                def high(c, m):
                    eng.wait_ge(h_full, nf * c + m + 1)
                    eng.activation(h_hi[m % 4][:], h[m % 2][:], ACT.Copy).then_inc(hi_done, 1)

                def body(c):
                    for m in range(nf):
                        if experts and m == routed[0]:
                            eng.wait_ge(cwT_ready, c + 1)
                            eng.activation(cwT[:], bank(4)[0:experts], ACT.Copy).then_inc(cwT_taken, 1)
                        eng.wait_ge(g_ready, nf * c + m + 1)
                        if gated:
                            if not first(c) or m >= 2:
                                eng.wait_ge(h_full, nf * c + m - 1)
                            eng.activation(th[m % 2][:], bank(m % 2), ACT.Tanh, scale=0.5).then_inc(th_done, 1)
                            if m >= 1:
                                high(c, m - 1)
                            elif not first(c):
                                high(c - 1, nf - 1)
                        else:
                            if not first(c) or m >= 2:
                                eng.wait_ge(lo_done, nf * c + m - 1)
                            eng.activation(h[m % 2][:], bank(m % 2), ACT.Relu, bias=b1[:, m:m + 1]).then_inc(h_full, 1)
                chunks(eng, body)
                if gated:
                    high(NC - 1, nf - 1)
            parts["scalar"].append(act_ff)

            def pool_ff(eng):
                with eng.Fori(0, NC) as c:
                    for m in range(nf):
                        eng.wait_ge(hi_done, nf * c + m + 1)
                        eng.tensor_tensor(h_lo[m % 4][:], h[m % 2][:], h_hi[m % 4][:].bitcast(F32), ALU.subtract).then_inc(lo_done, 1)
            parts["gpsimd"].append(pool_ff)

            inner = nf + nr if gated else 0

            def dve_ff(eng):
                added = 2 if biased else 0

                def add(c):
                    eng.wait_ge(out_ready, c + 1)
                    for k2 in range(2):
                        xt = x[:, bass.ds(CT * c + 2 * k2, 2), :]
                        ins = eng.tensor_tensor(xt, xt, bank(5 + k2).rearrange("p (a n) -> p a n", a=2), ALU.add)
                        if biased:
                            ins.then_inc(h_steps, 1)
                            eng.wait_ge(h_steps, 2 * c + k2 + 1)
                            ins = eng.tensor_tensor(xt, xt, b2[:].unsqueeze(1).broadcast_to([P, 2, D]), ALU.add)
                    ins.then_inc(x_added, 1)

                def body(c):
                    k = 0

                    def step(ins):
                        nonlocal k
                        k += 1
                        ins.then_inc(h_steps, 1)
                        eng.wait_ge(h_steps, c * inner + k)
                    if experts:
                        more.after(eng, c, -1)
                    for m in range(nf):
                        if m == LAG and not first(c):
                            add(c - 1)
                        if not gated:
                            eng.wait_ge(h_full, nf * c + m + 1)
                            eng.tensor_copy(h_hi[m % 4][:], h[m % 2][:]).then_inc(hi_done, 1)
                            continue
                        hm = h[m % 2][:]
                        if experts and m == first_routed:
                            eng.wait_ge(cwT_taken, c + 1)
                            eng.tensor_tensor(cwT_lo[:], bank(4)[0:experts], cwT[:].bitcast(F32), ALU.subtract).then_inc(cwT_lo_taken, 1)
                        eng.wait_ge(u_ready, nf * c + m + 1)
                        eng.wait_ge(th_done, nf * c + m + 1)
                        if not first(c) or m >= 2:
                            eng.wait_ge(lo_done, nf * c + m - 1)
                        step(eng.scalar_tensor_tensor(out=hm, in0=th[m % 2][:], scalar=1.0, in1=bank(2 + m % 2), op0=ALU.add, op1=ALU.mult))
                        last = eng.scalar_tensor_tensor(out=hm, in0=hm, scalar=0.5, in1=bank(m % 2), op0=ALU.mult, op1=ALU.mult)
                        if m in routed:
                            r = routed.index(m) // per_weight
                            step(last)
                            eng.wait_ge(c_ready, n_sel * c + r + 1)
                            last = eng.tensor_tensor(hm, hm, bank((4, 7)[r % 2]), ALU.mult)
                        last.then_inc(h_full, 1)
                        if experts:
                            more.after(eng, c, m)
                chunks(eng, body)
                add(NC - 1)
            parts["vector"].append(dve_ff)
            barrier()

        def rank_below(step, eng, v, gt, eq, tri, cnt, sel, rows, n, k):
            a = v.unsqueeze(2).broadcast_to([P, rows, n, n])
            b = v.unsqueeze(3).broadcast_to([P, rows, n, n])
            yield from step(eng.tensor_tensor(gt, a, b, ALU.is_gt))
            yield from step(eng.tensor_tensor(eq, a, b, ALU.is_equal))
            yield from step(eng.tensor_tensor(eq, eq, tri[:].unsqueeze(1).broadcast_to([P, rows, n, n]), ALU.mult))
            yield from step(eng.tensor_tensor(gt, gt, eq, ALU.add))
            yield from step(eng.tensor_reduce(cnt, gt, AX, ALU.add))
            yield from step(eng.tensor_scalar(sel, cnt, float(k), None, ALU.is_lt))

        class GroupRoute:
            scale = 0.5
            E, G = 16, 4

            def __init__(self, n, R, W, scratch, pairs, tl, cw):
                self.n, self.tl, self.cw = n, tl, cw
                E, G = self.E, self.G
                self.bias = W(n + "bias", [P, E])
                self.tri4 = W(n + "tri4", [P, G, G])
                self.tri16 = W(n + "tri16", [P, E, E])
                self.score, self.sb, self.m1, self.sel = (R(n + k, [P, CT, E]) for k in ("score", "sb", "m1", "sel"))
                self.two = R(n + "two", [P, CT * G, 6])
                self.gs, self.gcnt, self.gsel = (R(n + k, [P, CT, G]) for k in ("gs", "gcnt", "gsel"))
                self.g4, self.e4 = (R(n + k, [P, CT, G, G]) for k in ("g4", "e4"))
                self.g16, self.e16 = (R(n + k, [P, CT, E, E]) for k in ("g16", "e16"))
                self.cnt = R(n + "cnt", [P, CT, E])
                self.total = R(n + "total", [P, CT])
                pairs += [(self.bias[:], d[n + "bias"]), (self.tri4[:], d["tri4"]), (self.tri16[:], d["tri16"])]

            def first(self):
                pass

            STEPS = 27

            def then(self, tl_done, cw_done):
                self.tl_done, self.cw_done = tl_done, cw_done
                self.route_steps = sem(self.n + "route_steps")

            def route(self, eng, c):
                E, G = self.E, self.G
                k = 0

                def step(ins):
                    nonlocal k
                    k += 1
                    ins.then_inc(self.route_steps, 1)
                    eng.wait_ge(self.route_steps, c * self.STEPS + k)
                    yield
                every = lambda t: t.unsqueeze(3).broadcast_to([P, CT, G, E // G])
                yield from step(eng.tensor_scalar(self.score[:], self.tl[:, bass.ds(CT * (c % NC), CT), :], 0.5, 0.5, ALU.mult, ALU.add))
                yield from step(eng.tensor_tensor(self.sb[:], self.score[:], self.bias[:].unsqueeze(1).broadcast_to([P, CT, E]), ALU.add))
                v = self.sb[:].rearrange("p q (g k) -> p (q g) k", g=G)
                two = self.two[:]
                yield from step(eng.tensor_tensor(two[:, :, 0:2], v[:, :, 0:2], v[:, :, 2:4], ALU.add))
                yield from step(eng.tensor_tensor(two[:, :, 2:4], v[:, :, 0:4:2], v[:, :, 1:4:2], ALU.add))
                yield from step(eng.tensor_tensor(two[:, :, 4:5], v[:, :, 0:1], v[:, :, 3:4], ALU.add))
                yield from step(eng.tensor_tensor(two[:, :, 5:6], v[:, :, 1:2], v[:, :, 2:3], ALU.add))
                yield from step(eng.tensor_reduce(self.gs[:].rearrange("p q g -> p (q g)"), two, AX, ALU.max))
                yield from rank_below(step, eng, self.gs[:], self.g4[:], self.e4[:], self.tri4, self.gcnt[:], self.gsel[:], CT, G, 2)
                yield from step(eng.tensor_tensor(self.m1[:].rearrange("p q (g k) -> p q g k", g=G), self.sb[:].rearrange("p q (g k) -> p q g k", g=G),
                                       every(self.gsel[:]), ALU.mult))
                yield from step(eng.tensor_scalar(self.gcnt[:], self.gsel[:], -1.0, 1e30, ALU.add, ALU.mult))
                yield from step(eng.tensor_tensor(self.m1[:].rearrange("p q (g k) -> p q g k", g=G), self.m1[:].rearrange("p q (g k) -> p q g k", g=G),
                                       every(self.gcnt[:]), ALU.add))
                yield from rank_below(step, eng, self.m1[:], self.g16[:], self.e16[:], self.tri16, self.cnt[:], self.sel[:], CT, E, 4)
                yield from step(eng.tensor_tensor(self.sel[:], self.sel[:], self.score[:], ALU.mult))
                yield from step(eng.tensor_reduce(self.total[:], self.sel[:], AX, ALU.add))
                yield from step(eng.tensor_scalar(self.total[:], self.total[:], 1e-20, None, ALU.add))
                yield from step(eng.reciprocal(self.total[:], self.total[:]))
                yield from step(eng.tensor_tensor(self.cw[:], self.sel[:], self.total[:].unsqueeze(2).broadcast_to([P, CT, E]), ALU.mult))
                eng.memset(spare[:], 0.0).then_inc(self.cw_done, 1)
                assert k == self.STEPS

            def after(self, eng, c, m):
                if m == -1:
                    if isinstance(c, int) and c == 0:
                        eng.wait_ge(self.tl_done, NC)
                        self.now = self.route(eng, 0)
                    self.next = self.route(eng, c + 1)
                if isinstance(c, int) and c == 0 and 0 <= m <= 2:
                    for _ in range(14 if m < 2 else self.STEPS):
                        next(self.now, None)
                if m > 4:
                    for _ in range(5):
                        next(self.next, None)

        class ZoneRoute:
            E = 8
            CENTER = math.exp(-1.0)
            LOWER, UPPER = 0.5 - math.log(4.0 / 3.0), 0.5

            def __init__(self, n, R, W, scratch, pairs, tl, cw):
                self.n, self.tl, self.cw = n, tl, cw
                E = self.E
                self.temp = W(n + "temp", [P, 1])
                self.half = R(n + "half", [P, 1])
                self.scale = self.half[:, 0:1]
                self.tri8 = W(n + "tri8", [P, E, E])
                self.inh, self.zone, self.low, self.dist, self.w, self.fb = (R(n + k, [P, NT, E]) for k in ("inh", "zone", "low", "dist", "w", "fb"))
                self.g8, self.e8 = (scratch(n + k, [P, NT, E, E]) for k in ("g8", "e8"))
                self.cnt, self.sel, self.dif = (R(n + k, [P, NT, E]) for k in ("cnt", "sel", "dif"))
                self.total, self.none = R(n + "total", [P, NT]), R(n + "none", [P, NT])
                pairs += [(self.temp[:], d[n + "temp"]), (self.tri8[:], d["tri8"])]
                self.half_done = sem(n + "half_done")

            def first(self):
                def dve_half(eng):
                    eng.reciprocal(self.half[:], self.temp[:]).then_inc(self.half_done, 1)
                    eng.wait_ge(self.half_done, 1)
                    eng.tensor_scalar(self.half[:], self.half[:], 0.5, None, ALU.mult).then_inc(self.half_done, 1)
                parts["vector"].append(dve_half)
                parts["scalar"].append(lambda eng: eng.wait_ge(self.half_done, 2))

            def then(self, tl_done, cw_done):
                self.cw_done = cw_done
                zone_steps = sem(self.n + "zone_steps")
                exps_done = sem(self.n + "exps_done")
                route_steps = sem(self.n + "route_steps")
                E = self.E

                def dve_zone(eng):
                    eng.wait_ge(tl_done, NC)
                    eng.tensor_scalar(self.inh[:], self.tl[:], 0.5, 0.5, ALU.mult, ALU.add).then_inc(zone_steps, 1)
                    eng.wait_ge(zone_steps, 1)
                    eng.tensor_scalar(self.low[:], self.inh[:], self.LOWER, None, ALU.is_ge).then_inc(zone_steps, 1)
                    eng.tensor_scalar(self.dist[:], self.inh[:], self.CENTER, None, ALU.subtract).then_inc(zone_steps, 1)
                    eng.wait_ge(zone_steps, 3)
                    eng.scalar_tensor_tensor(out=self.zone[:], in0=self.inh[:], scalar=self.UPPER, in1=self.low[:], op0=ALU.is_le, op1=ALU.mult).then_inc(zone_steps, 1)
                    eng.scalar_tensor_tensor(out=self.dist[:], in0=self.dist[:], scalar=-1.0, in1=self.dist[:], op0=ALU.mult, op1=ALU.max).then_inc(zone_steps, 1)
                parts["vector"].append(dve_zone)

                def act_exps(eng):
                    eng.wait_ge(zone_steps, 5)
                    eng.activation(self.w[:], self.dist[:], ACT.Exp, scale=-1 / 0.1).then_inc(exps_done, 1)
                    eng.activation(self.fb[:], self.dist[:], ACT.Exp, scale=-1 / 0.3).then_inc(exps_done, 1)
                parts["scalar"].append(act_exps)

                def dve_route(eng):
                    count = 0

                    def step(ins):
                        nonlocal count
                        count += 1
                        ins.then_inc(route_steps, 1)
                        eng.wait_ge(route_steps, count)
                        return ()
                    every = lambda t: t.unsqueeze(2).broadcast_to([P, NT, E])
                    w, fb, total, none, sel = self.w[:], self.fb[:], self.total[:], self.none[:], self.sel[:]
                    eng.wait_ge(exps_done, 2)
                    step(eng.tensor_tensor(w, w, self.zone[:], ALU.mult))
                    for _ in rank_below(step, eng, fb, self.g8[:], self.e8[:], self.tri8, self.cnt[:], sel, NT, E, 2):
                        pass
                    step(eng.tensor_tensor(sel, sel, fb, ALU.mult))
                    step(eng.tensor_reduce(total, sel, AX, ALU.add))
                    step(eng.tensor_scalar(total, total, 1e-8, None, ALU.max))
                    step(eng.reciprocal(total, total))
                    step(eng.tensor_tensor(sel, sel, every(total), ALU.mult))
                    step(eng.tensor_reduce(total, w, AX, ALU.add))
                    step(eng.tensor_scalar(none, total, 1e-8, None, ALU.is_lt))
                    step(eng.tensor_tensor(self.dif[:], sel, every(none), ALU.mult))
                    step(eng.tensor_scalar(none, none, -1.0, 1.0, ALU.mult, ALU.add))
                    step(eng.tensor_tensor(sel, w, every(none), ALU.mult))
                    step(eng.tensor_tensor(sel, sel, self.dif[:], ALU.add))
                    step(eng.tensor_reduce(total, sel, AX, ALU.add))
                    step(eng.tensor_scalar(total, total, 1e-8, None, ALU.max))
                    step(eng.reciprocal(total, total))
                    step(eng.tensor_tensor(sel, sel, every(total), ALU.mult))
                parts["vector"].append(dve_route)

            def after(self, eng, c, m):
                if m == -1 and isinstance(c, int) and c == 0:
                    eng.tensor_copy(self.cw[:], self.sel[:, 0:CT, :]).then_inc(self.cw_done, 1)
                if m == 2:
                    eng.tensor_copy(self.cw[:], self.sel[:, bass.ds(CT * ((c + 1) % NC), CT), :]).then_inc(self.cw_done, 1)

        def gate_attention(n):
            R = Region(start, region_end(n))
            RW = Region(*weights_at[n])
            lnx = R(n + "lnx", [P, NT, D])
            lnT = R(n + "lnT", [P, KT, NC * CN])
            W = RW(n + "W", [P, KT, D])
            Ws = RW(n + "Ws", [P, KT, D])
            bcol = RW(n + "bcol", [P, KT])
            wide = RW(n + "wide", [P, KT, 63])
            cB = RW(n + "cB", [P, 2, KT, P])
            bc = RW(n + "bc", [P, 2])
            qm = RW(n + "qm", [P, B, S2], I32)
            txt = R(n + "txt", [P, KT, B * S2])
            txtb = R(n + "txtb", [P, KT, S2])
            ctab = R(n + "ctab", [P, 2, B * S2])
            madd = R(n + "madd", [P, B, S2])
            fT = R(n + "fT", [P, KT, S])
            RING = 8
            ring = [R(n + f"ring{i}", [P, S]) for i in range(RING)]
            rhoT = R(n + "rhoT", [96, S])
            rho = R(n + "rho", [P, TB, S2])
            prod = R(n + "prod", [P, TB, S2])
            mx, sm, rs = (R(n + k, [P, TB]) for k in ("mx", "sm", "rs"))
            g = R(n + "g", [P, 2, TB])
            loads(n, [(W[:], d[n + "W"]), (Ws[:], d[n + "Ws"]), (bcol[:], d[n + "b"]), (wide[:], d[n + "wide"]),
                      (cB[:], d[n + "cB"]), (bc[:], d[n + "bc"]), (qm[:], d[n + "qm"])])
            parts["sync"].append(lambda eng: load_weights_after(n, eng))
            await_weights(n)
            normalise(n, lnx, lnT)
            tab_ready = sem(n + "tab_ready")
            tab_steps = sem(n + "tab_steps")
            f_ready = sem(n + "f_ready")
            f_taken = sem(n + "f_taken")
            txt_moved = sem(n + "txt_moved")
            tanh_done = sem(n + "tanh_done")
            rho_added = sem(n + "rho_added")
            rhoT_taken = sem(n + "rhoT_taken")
            rho_ready = sem(n + "rho_ready")
            soft = sem(n + "soft")
            exp_done = sem(n + "exp_done")
            gates_done = sem(n + "gates_done")
            order = [(t, e) for r in range(32) for e in range(KT) for t in (r, r + 32, r + 64) if t < S2]
            n_ord = len(order)

            def pe_tables(eng):
                for e in range(KT):
                    for kt in range(KT):
                        ins = eng.matmul(bank(e, 0, B * S2), Ws[:, kt, P * e:P * e + P], ctxT[:, kt, :], start=kt == 0, stop=kt == KT - 1)
                    ins.then_inc(tab_ready, 1)
                for e in range(2):
                    for kt in range(KT):
                        ins = eng.matmul(bank(2 + e, 0, B * S2), cB[:, e, kt, :], ctxT[:, kt, :], start=kt == 0, stop=kt == KT - 1)
                    ins.then_inc(tab_ready, 1)
                eng.wait_ge(tab_steps, 5)
            parts["tensor"].append(pe_tables)

            def dve_tables(eng):
                for e in range(KT):
                    eng.wait_ge(tab_ready, e + 1)
                    eng.tensor_scalar(txt[:, e, :], bank(e, 0, B * S2), bcol[:, e:e + 1], None, ALU.add).then_inc(tab_steps, 1)
                for e in range(2):
                    eng.wait_ge(tab_ready, 3 + e)
                    eng.tensor_copy(ctab[:, e, :], bank(2 + e, 0, B * S2)).then_inc(tab_steps, 1)
                eng.tensor_scalar(madd[:], qm[:], 1.0, 1e30, ALU.subtract, ALU.mult).then_inc(tab_steps, 1)
                eng.wait_ge(tab_steps, 5)
            parts["vector"].append(dve_tables)

            def pe_gate(eng):
                with eng.Fori(0, B) as b:
                    for e in range(KT):
                        for half in range(2):
                            k = 2 * e + half
                            for kt in range(KT):
                                ins = eng.matmul(bank(2 + k), W[:, kt, P * e:P * e + P], lnT[:, kt, bass.ds(b * S + half * CN, CN)],
                                                 start=kt == 0, stop=kt == KT - 1)
                            ins.then_inc(f_ready, 1)
                    for k, (t, e) in enumerate(order):
                        eng.wait_ge(tanh_done, n_ord * b + k + 1)
                        q, r = t // 32, t % 32
                        for half in range(2):
                            ins = eng.matmul(bank(half)[32 * q:32 * q + 32], wide[:, e, 31 - r:63 - r], ring[k % RING][:, half * CN:(half + 1) * CN],
                                             start=r == 0 and e == 0, stop=(t, e) == (last_of[q], KT - 1))
                        ins.then_inc(rho_added, 1)
                    eng.wait_ge(rhoT_taken, 2 * b + 2)
                    for j in range(TB):
                        ins = eng.transpose(bank(6 + j // 4, S2 * (j % 4), S2), rhoT[0:S2, P * j:P * j + P], ident[0:S2, 0:S2])
                    ins.then_inc(rho_ready, 1)
                    eng.wait_ge(soft, SOFT * b + 1)
            last_of = [31, 63, S2 - 1]
            SOFT = 8
            parts["tensor"].append(pe_gate)

            def act_gate(eng):
                with eng.Fori(0, B) as b:
                    for k in range(4):
                        eng.wait_ge(f_ready, 4 * b + k + 1)
                        eng.activation(fT[:, k // 2, (k % 2) * CN:(k % 2 + 1) * CN], bank(2 + k), ACT.Copy).then_inc(f_taken, 1)
                    eng.wait_ge(f_taken, 4 * b + 4)
                    eng.wait_ge(txt_moved, b + 1)
                    for k, (t, e) in enumerate(order):
                        if k >= RING:
                            eng.wait_ge(rho_added, n_ord * b + k - RING + 1)
                        eng.activation(ring[k % RING][:], fT[:, e, :], ACT.Tanh, bias=txtb[:, e, t:t + 1]).then_inc(tanh_done, 1)
                    eng.wait_ge(soft, SOFT * b + 3)
                    eng.activation(rho[:], rho[:], ACT.Exp).then_inc(exp_done, 1)
                    for i in range(2):
                        eng.wait_ge(soft, SOFT * b + 7 + i)
                        eng.activation(g[:, i, :], g[:, i, :], ACT.Tanh, bias=bc[:, i:i + 1]).then_inc(gates_done, 1)
            parts["scalar"].append(act_gate)

            def dve_gate(eng):
                with eng.Fori(0, B) as b:
                    eng.tensor_copy(txtb[:], txt[:, :, bass.ds(b * S2, S2)]).then_inc(txt_moved, 1)
                    eng.wait_ge(rho_added, n_ord * (b + 1))
                    for half in range(2):
                        eng.tensor_copy(rhoT[:, half * CN:(half + 1) * CN], bank(half)[0:96]).then_inc(rhoT_taken, 1)
                    eng.wait_ge(rho_ready, b + 1)
                    for k in range(2):
                        ins = eng.tensor_tensor(rho[:, 4 * k:4 * k + 4, :], bank(6 + k, 0, 4 * S2).rearrange("p (j t) -> p j t", t=S2),
                                                madd[:, bass.ds(b, 1), :].broadcast_to([P, 4, S2]), ALU.add)
                    ins.then_inc(soft, 1)
                    eng.wait_ge(soft, SOFT * b + 1)
                    eng.tensor_reduce(mx[:], rho[:], AX, ALU.max).then_inc(soft, 1)
                    eng.wait_ge(soft, SOFT * b + 2)
                    eng.tensor_tensor(rho[:], rho[:], mx[:].unsqueeze(2).broadcast_to([P, TB, S2]), ALU.subtract).then_inc(soft, 1)
                    eng.wait_ge(exp_done, b + 1)
                    eng.tensor_reduce(sm[:], rho[:], AX, ALU.add).then_inc(soft, 1)
                    eng.wait_ge(soft, SOFT * b + 4)
                    eng.reciprocal(rs[:], sm[:]).then_inc(soft, 1)
                    for i in range(2):
                        if i:
                            eng.wait_ge(dots, 4 * b + 2)
                        eng.tensor_tensor(prod[:], rho[:], ctab[:, i, bass.ds(b * S2, S2)].unsqueeze(1).broadcast_to([P, TB, S2]), ALU.mult).then_inc(dots, 1)
                        eng.wait_ge(dots, 4 * b + 2 * i + 1)
                        eng.tensor_reduce(g[:, i, :], prod[:], AX, ALU.add).then_inc(dots, 1)
                    eng.wait_ge(dots, 4 * b + 4)
                    eng.wait_ge(soft, SOFT * b + 5)
                    eng.memset(spare[:], 0.0).then_inc(soft, 1)
                    eng.tensor_tensor(g[:, 0, :], g[:, 0, :], rs[:], ALU.mult).then_inc(soft, 1)
                    eng.tensor_tensor(g[:, 1, :], g[:, 1, :], rs[:], ALU.mult).then_inc(soft, 1)
                    eng.wait_ge(gates_done, 2 * b + 2)
                    for j in range(TB):
                        xt = x[:, bass.ds(TB * b + j, 1), :].rearrange("p a n -> p (a n)")
                        eng.scalar_tensor_tensor(out=xt, in0=lnx[:, bass.ds(TB * b + j, 1), :].rearrange("p a n -> p (a n)"), scalar=g[:, 0, j:j + 1],
                                                 in1=xt, op0=ALU.mult, op1=ALU.add).then_inc(scaled, 1)
                    for j in range(TB):
                        xt = x[:, bass.ds(TB * b + j, 1), :].rearrange("p a n -> p (a n)")
                        eng.wait_ge(scaled, TB * b + j + 1)
                        eng.tensor_scalar(xt, xt, g[:, 1, j:j + 1], None, ALU.add)
            dots = sem(n + "dots")
            scaled = sem(n + "scaled")
            parts["vector"].append(dve_gate)
            barrier()

        def quantised(n):
            NF, ROUND = 8, 1.5 * 2 ** 23
            R = Region(start, region_end(n))
            W = Region(*weights_at[n])
            lnx = R(n + "lnx", [P, NT, D])
            w1 = W(n + "w1", [P, NF, D])
            w2 = W(n + "w2", [P, KT, NF * P])
            b1 = W(n + "b1", [P, NF])
            b2 = W(n + "b2", [P, KT])
            q1 = R(n + "q1", [P, NF, D], BF16)
            q2 = R(n + "q2", [P, KT, NF * P], BF16)
            q1T = R(n + "q1T", [P, KT, NF * P], BF16)
            q2T = R(n + "q2T", [P, NF, D], BF16)
            s1, i1, s2, i2 = (R(n + k, [P, w]) for k, w in (("s1", NF), ("i1", NF), ("s2", KT), ("i2", KT)))
            qx = R(n + "qx", [P, CT, D])
            qxb = R(n + "qxb", [P, NT, D], BF16)
            qxT = R(n + "qxT", [P, KT, NC * CN], BF16)
            h = R(n + "h", [P, NF, NC * CN])
            hq = R(n + "hq", [P, CN])
            qh = [R(n + f"qh{i}", [P, CN], BF16) for i in range(3)]
            sc1, bi1, bi2 = R(n + "sc1", [P, NF]), R(n + "bi1", [P, NF]), R(n + "bi2", [P, KT])
            row = R(n + "row", [P, 2, D])
            diag = R(n + "diag", [P, 2, KT, P])
            mxx, mall, sx, ix = (R(n + k, [P, w]) for k, w in (("mxx", 1), ("mall", 2), ("sx", 2), ("ix", 2)))
            mh, mh1 = R(n + "mh", [P, NC * NF]), R(n + "mh1", [P, 1])
            tmp = R(n + "tmp", [P, NF])
            loads(n, [(w1[:], d[n + "w1"]), (w2[:], d[n + "w2"]), (b1[:], d[n + "b1"]), (b2[:], d[n + "b2"])])
            await_weights(n)
            c0 = normalise(n, lnx)
            st = sem(n + "st")
            maxed = sem(n + "maxed")
            wT_ready = sem(n + "wT_ready")
            wT_taken = sem(n + "wT_taken")
            qx_done = sem(n + "qx_done")
            qxT_ready = sem(n + "qxT_ready")
            qxT_taken = sem(n + "qxT_taken")
            p1_ready = sem(n + "p1_ready")
            h_done = sem(n + "h_done")
            h_maxed = sem(n + "h_maxed")
            hq_steps = sem(n + "hq_steps")
            qh_used = sem(n + "qh_used")
            row_ready = sem(n + "row_ready")
            out_ready = sem(n + "out_ready")
            qsteps = sem(n + "qsteps")
            osteps = sem(n + "osteps")

            def dve_weights(eng):
                k = 0

                def step(ins):
                    nonlocal k
                    k += 1
                    ins.then_inc(st, 1)
                    eng.wait_ge(st, k)
                for w, s, i, qf, nt, b in ((w1, s1, i1, q1, NF, b1), (w2, s2, i2, q2, KT, b2)):
                    step(eng.tensor_reduce(s[:], w[:], AX, ALU.max))
                    step(eng.tensor_reduce(i[:], w[:], AX, ALU.min))
                    step(eng.scalar_tensor_tensor(out=s[:], in0=i[:], scalar=-1.0, in1=s[:], op0=ALU.mult, op1=ALU.max))
                    step(eng.tensor_scalar(s[:], s[:], 1e-8, 1.0 / 127.0, ALU.max, ALU.mult))
                    step(eng.reciprocal(i[:], s[:]))
                    for t in range(nt):
                        ins = eng.tensor_scalar(w[:, t, :], w[:, t, :], i[:, t:t + 1], ROUND, ALU.mult, ALU.add)
                    step(ins)
                    step(eng.tensor_scalar(qf[:], w[:], ROUND, None, ALU.subtract))
                eng.wait_ge(ln_done, c0 + NC)
                step(eng.tensor_reduce(mxx[:], lnx[:].rearrange("p t n -> p (t n)"), AX, ALU.max))
                eng.wait_ge(maxed, 1)
                step(eng.tensor_scalar(sx[:, 0:1], mall[:, 0:1], 1e-8, 1.0 / 255.0, ALU.max, ALU.mult))
                step(eng.reciprocal(ix[:, 0:1], sx[:, 0:1]))
                step(eng.tensor_scalar(sc1[:], s1[:], sx[:, 0:1], None, ALU.mult))
                step(eng.reciprocal(tmp[:], sc1[:]))
                step(eng.tensor_tensor(tmp[:], tmp[:], b1[:], ALU.mult))
                step(eng.tensor_scalar(tmp[:], tmp[:], ROUND, None, ALU.add))
                step(eng.tensor_scalar(tmp[:], tmp[:], ROUND, None, ALU.subtract))
                step(eng.tensor_tensor(bi1[:], tmp[:], sc1[:], ALU.mult))
            N_WEIGHT = 7 * 2
            N_MAX = N_WEIGHT + 1
            N_ALL = N_MAX + 8
            parts["vector"].append(dve_weights)

            def pool_max(eng):
                eng.wait_ge(st, N_MAX)
                eng.partition_all_reduce(mall[:, 0:1], mxx[:], P, bass.bass_isa.ReduceOp.max).then_inc(maxed, 1)
            parts["gpsimd"].append(pool_max)

            def dve_qx(eng):
                with eng.Fori(0, NC) as c:
                    t4 = lnx[:, bass.ds(CT * c, CT), :]
                    eng.tensor_scalar(qx[:], t4, ix[:, 0:1], 0.0, ALU.mult, ALU.max).then_inc(qsteps, 1)
                    eng.wait_ge(qsteps, 3 * c + 1)
                    eng.tensor_scalar(qx[:], qx[:], 255.0, ROUND, ALU.min, ALU.add).then_inc(qsteps, 1)
                    eng.wait_ge(qsteps, 3 * c + 2)
                    eng.tensor_scalar(qxb[:, bass.ds(CT * c, CT), :], qx[:], ROUND, None, ALU.subtract).then_inc(qsteps, 1)
                    eng.wait_ge(qsteps, 3 * c + 3)
                    eng.memset(spare[:], 0.0).then_inc(qx_done, 1)
            parts["vector"].append(dve_qx)

            def bankb(i, a, w):
                return bank(i)[:, a // 2:(a + w) // 2].bitcast(BF16)

            def pe_wT(eng):
                eng.wait_ge(st, N_WEIGHT)
                for kt in range(KT):
                    for f in range(NF):
                        ins = eng.transpose(bankb(kt, P * f, P), q1[:, f, P * kt:P * kt + P], identb[:])
                    ins.then_inc(wT_ready, 1)
                for half in range(2):
                    for f4 in range(4):
                        f = 4 * half + f4
                        for kt in range(KT):
                            ins = eng.transpose(bankb(2 + half, D * f4 + P * kt, P), q2[:, kt, P * f:P * f + P], identb[:])
                    ins.then_inc(wT_ready, 1)
            parts["tensor"].append(pe_wT)

            def act_wT(eng):
                for i in range(4):
                    eng.wait_ge(wT_ready, i + 1)
                    dst = q1T[:, i, :] if i < 2 else q2T[:, 4 * (i - 2):4 * (i - 1), :].rearrange("p f n -> p (f n)")
                    eng.activation(dst, bankb(i, 0, 1024), ACT.Copy).then_inc(wT_taken, 1)
            parts["scalar"].append(act_wT)

            def pe_qxT(eng):
                for c in range(NC):
                    eng.wait_ge(qx_done, c + 1)
                    if c >= 2:
                        eng.wait_ge(qxT_taken, 2 * (c - 1))
                    for kt in range(KT):
                        for q in range(CT):
                            ins = eng.transpose(bankb(4 + 2 * (c % 2) + kt, P * q, P), qxb[:, CT * c + q, P * kt:P * kt + P], identb[:])
                        ins.then_inc(qxT_ready, 1)
                eng.wait_ge(qxT_taken, 2 * NC)
                eng.wait_ge(wT_taken, 4)
            parts["tensor"].append(pe_qxT)

            def act_qxT(eng):
                for c in range(NC):
                    for kt in range(KT):
                        eng.wait_ge(qxT_ready, 2 * c + kt + 1)
                        eng.activation(qxT[:, kt, CN * c:CN * (c + 1)], bankb(4 + 2 * (c % 2) + kt, 0, CN), ACT.Copy).then_inc(qxT_taken, 1)
            parts["scalar"].append(act_qxT)

            def pe_p1(eng):
                with eng.Fori(0, NC) as c:
                    for f in range(NF):
                        eng.wait_ge(h_done, NF * c + 1)
                        for kt in range(KT):
                            ins = eng.matmul(bank(f), q1T[:, kt, P * f:P * f + P], qxT[:, kt, bass.ds(CN * c, CN)], start=kt == 0, stop=kt == KT - 1)
                        ins.then_inc(p1_ready, 1)
            parts["tensor"].append(pe_p1)

            def act_p1(eng):
                eng.wait_ge(st, N_ALL)
                eng.activation(spare[:], spare[:], ACT.Copy).then_inc(h_done, 1)
                with eng.Fori(0, NC) as c:
                    for f in range(NF):
                        eng.wait_ge(p1_ready, NF * c + f + 1)
                        eng.activation(h[:, f, bass.ds(CN * c, CN)], bank(f), ACT.Relu, bias=bi1[:, f:f + 1], scale=sc1[:, f:f + 1]).then_inc(h_done, 1)
            parts["scalar"].append(act_p1)

            def dve_p1(eng):
                with eng.Fori(0, NC) as c:
                    for f in range(NF):
                        eng.wait_ge(h_done, NF * c + f + 2)
                        eng.tensor_reduce(mh[:, bass.ds(NF * c + f, 1)], h[:, f, bass.ds(CN * c, CN)], AX, ALU.max).then_inc(h_maxed, 1)
                k = N_ALL

                def step(ins):
                    nonlocal k
                    k += 1
                    ins.then_inc(st, 1)
                    eng.wait_ge(st, k)
                eng.wait_ge(h_maxed, NF * NC)
                step(eng.tensor_reduce(mh1[:], mh[:], AX, ALU.max))
                eng.wait_ge(maxed, 2)
                step(eng.tensor_scalar(sx[:, 1:2], mall[:, 1:2], 1e-8, 1.0 / 255.0, ALU.max, ALU.mult))
                step(eng.reciprocal(ix[:, 1:2], sx[:, 1:2]))
                step(eng.tensor_scalar(s2[:], s2[:], sx[:, 1:2], None, ALU.mult))
                step(eng.reciprocal(i2[:], s2[:]))
                step(eng.tensor_tensor(bi2[:], i2[:], b2[:], ALU.mult))
                step(eng.tensor_scalar(bi2[:], bi2[:], ROUND, None, ALU.add))
                step(eng.tensor_scalar(bi2[:], bi2[:], ROUND, None, ALU.subtract))
                step(eng.tensor_tensor(bi2[:], bi2[:], s2[:], ALU.mult))
                for kt in range(KT):
                    eng.tensor_scalar(diag[:, 0, kt, :], ident[:], s2[:, kt:kt + 1], None, ALU.mult)
                    ins = eng.tensor_scalar(diag[:, 1, kt, :], ident[:], bi2[:, kt:kt + 1], None, ALU.mult)
                step(ins)
            parts["vector"].append(dve_p1)

            def pool_max2(eng):
                eng.wait_ge(st, N_ALL + 1)
                eng.partition_all_reduce(mall[:, 1:2], mh1[:], P, bass.bass_isa.ReduceOp.max).then_inc(maxed, 1)
            parts["gpsimd"].append(pool_max2)

            def pe_row(eng):
                eng.wait_ge(st, N_ALL + 10)
                eng.wait_ge(h_done, NF * NC + 1)
                for i in range(2):
                    for kt in range(KT):
                        ins = eng.matmul(bank(6, D * i + P * kt, P), ones[:], diag[:, i, kt, :], start=True, stop=True)
                ins.then_inc(row_ready, 1)
            parts["tensor"].append(pe_row)
            parts["scalar"].append(lambda eng: (eng.wait_ge(row_ready, 1), eng.activation(row[:].rearrange("p i n -> p (i n)"), bank(6), ACT.Copy).then_inc(row_ready, 1)))

            def dve_p2(eng):
                eng.wait_ge(row_ready, 2)
                with eng.Fori(0, NC) as c:
                    for f in range(NF):
                        if f:
                            eng.wait_ge(hq_steps, NF * 2 * c + 2 * f)
                        eng.tensor_scalar(hq[:], h[:, f, bass.ds(CN * c, CN)], ix[:, 1:2], ROUND, ALU.mult, ALU.add).then_inc(hq_steps, 1)
                        eng.wait_ge(hq_steps, NF * 2 * c + 2 * f + 1)
                        if f >= 3:
                            eng.wait_ge(qh_used, NF * c + f - 2)
                        eng.tensor_scalar(qh[f % 3][:], hq[:], ROUND, None, ALU.subtract).then_inc(hq_steps, 1)
                    eng.wait_ge(qh_used, NF * (c + 1))
                    eng.wait_ge(hq_steps, NF * 2 * c + 2 * NF)
                    for k in range(2):
                        xt = x[:, bass.ds(CT * c + 2 * k, 2), :]
                        o = bank(2 * (k) + 0).rearrange("p (a n) -> p a n", a=2)
                        eng.tensor_tensor(ot[:, 2 * k:2 * k + 2, :], o, row[:, 0:1, :].broadcast_to([P, 2, D]), ALU.mult).then_inc(osteps, 1)
                        eng.wait_ge(osteps, 6 * c + 3 * k + 1)
                        eng.tensor_tensor(ot[:, 2 * k:2 * k + 2, :], ot[:, 2 * k:2 * k + 2, :], row[:, 1:2, :].broadcast_to([P, 2, D]), ALU.add).then_inc(osteps, 1)
                        eng.wait_ge(osteps, 6 * c + 3 * k + 2)
                        eng.tensor_tensor(xt, xt, ot[:, 2 * k:2 * k + 2, :], ALU.add).then_inc(osteps, 1)
            ot = R(n + "ot", [P, CT, D])
            parts["vector"].append(dve_p2)

            def pe_p2(eng):
                with eng.Fori(0, NC) as c:
                    for f in range(NF):
                        eng.wait_ge(hq_steps, NF * 2 * c + 2 * f + 2)
                        for q in range(CT):
                            ins = eng.matmul(bank(2 * (q // 2), D * (q % 2), D), qh[f % 3][:, P * q:P * q + P], q2T[:, f, :],
                                             start=f == 0 and q % 2 == 0, stop=f == NF - 1, skip_group_check=True)
                        ins.then_inc(qh_used, 1)
                    eng.wait_ge(osteps, 6 * c + 5)
            parts["tensor"].append(pe_p2)
            barrier()

        LAYERS = [lambda: attention(Attention("a0_", 1024, True, True, -1e30)),
                  lambda: feed_forward("f0_", 12, first_routed=4, experts=16, route=GroupRoute),
                  lambda: attention(Attention("a1_", 1024, False, False, None)),
                  lambda: feed_forward("f1_", 8, gated=False, biased=True),
                  lambda: gate_attention("a2_"),
                  lambda: feed_forward("f2_", 16, first_routed=0, per_weight=2, experts=8, route=ZoneRoute),
                  lambda: attention(Attention("a3_", 256, True, False, -1e15)),
                  lambda: quantised("f3_")]
        for i, make in enumerate(LAYERS):
            if make and i in only:
                make()

        def store_x(eng):
            for b in range(B):
                eng.dma_start(d["out"][b].rearrange("(p j) n -> p j n", p=P), x[:, TB * b:TB * (b + 1), :]).then_inc(stored, 16)
            eng.wait_ge(stored, 16 * B)
        parts["sync"].append(store_x)

        block = ctx.enter_context(nc.Block())

        @block.sync
        def _(eng):
            for part in parts["sync"]:
                part(eng)

        @block.tensor
        def _(eng):
            for part in parts["tensor"]:
                part(eng)

        @block.scalar
        def _(eng):
            for part in parts["scalar"]:
                part(eng)

        @block.vector
        def _(eng):
            for part in parts["vector"]:
                part(eng)

        @block.gpsimd
        def _(eng):
            for part in parts["gpsimd"]:
                part(eng)


def layouts(v):
    import numpy as np
    v = {k: np.asarray(a) for k, a in v.items()}
    rows = lambda a: np.ascontiguousarray(a.reshape(-1, P, a.shape[-1]).transpose(1, 0, 2))
    col = lambda a: np.ascontiguousarray(a.reshape(-1, P).T)
    every = lambda a: np.ascontiguousarray(np.broadcast_to(a, (P,) + a.shape))
    o = {"x": v["x"], "fside": v["fside_Bx16xSxS2_0"], "mask16": v["mask_Bx16xSxS2_bk1"], "mask1": v["mask_Bx1xSxS2_bk1"],
         "ident": np.eye(P, dtype=np.float32),
         "ctxT": rows(v["ctx_1024"].reshape(B * S2, D).T)}
    for n, l in (("a0_", "L0_xattn_"), ("a1_", "L1_xattn_"), ("a3_", "L3_xattn_")):
        w = {k: v[l + k] for k in ("Wq", "Wk", "Wv", "Wo")}
        dims = w["Wo"].size // D
        o[n + "WqT"] = rows(w["Wq"].reshape(D, dims).T)
        o[n + "Wk"] = rows(w["Wk"].reshape(D, dims))
        o[n + "Wv"] = rows(w["Wv"].reshape(D, dims))
        o[n + "Wo"] = rows(w["Wo"].reshape(dims, D))
        hd = dims // H
        o[n + "group"] = np.kron(np.eye(P // hd), np.ones((hd, 1))).astype(np.float32)
        if l + "bq" in v:
            o[n + "bk"], o[n + "bv"] = col(v[l + "bk"]), col(v[l + "bv"])
            o[n + "bq"] = col(v[l + "bq"])
            o[n + "bo2"] = np.ascontiguousarray(np.broadcast_to(v[l + "bo"], (1, B, D)))
    inner = lambda a: a.transpose(1, 0, 2).reshape(D, -1)
    o["f0_wg"] = rows(np.concatenate([v["L0_ffn_shared_gate_w"].T, inner(v["L0_ffn_gate_w"])], 1))
    o["f0_wu"] = rows(np.concatenate([v["L0_ffn_shared_up_w"].T, inner(v["L0_ffn_up_w"])], 1))
    o["f0_wd"] = rows(np.concatenate([v["L0_ffn_shared_down_w"].T, v["L0_ffn_down_w"].reshape(-1, D)], 0))
    o["f0_wr"] = rows(v["L0_ffn_router_w"].T)
    o["f0_bias"] = every(v["L0_ffn_correction_bias"])
    o["f0_sel"] = np.kron(np.eye(16), np.ones((1, 64))).reshape(16, 8, P).astype(np.float32)
    o["f1_wg"], o["f1_wd"] = rows(v["L1_ffn_W1"]), rows(v["L1_ffn_W2"])
    o["f1_b1"], o["f1_b2"] = col(v["L1_ffn_b1"]), every(v["L1_ffn_b2"])
    o["a2_W"], o["a2_Ws"], o["a2_b"] = rows(v["L2_xattn_W"]), rows(v["L2_xattn_Ws"]), col(v["L2_xattn_b"].reshape(-1))
    wide = np.zeros((P, KT, 63), np.float32)
    wide[:, :, 31] = col(v["L2_xattn_w"].reshape(-1))
    o["a2_wide"] = wide
    o["a2_cB"] = np.ascontiguousarray(np.broadcast_to(
        np.stack([col(v["L2_xattn_Wcw"].reshape(-1)), col(v["L2_xattn_Wcb"].reshape(-1))], 1)[:, :, :, None], (P, 2, KT, P)))
    o["a2_bc"] = every(np.concatenate([v["L2_xattn_bcw"], v["L2_xattn_bcb"]]))
    o["a2_qm"] = every(v["mask_BxS2_ik0"])
    o["f2_wg"], o["f2_wu"] = rows(inner(v["L2_ffn_Wg"])), rows(inner(v["L2_ffn_Wu"]))
    o["f2_wd"], o["f2_wr"] = rows(v["L2_ffn_Wd"].reshape(-1, D)), rows(v["L2_ffn_Wr"])
    o["f2_temp"] = every(v["L2_ffn_temperature"])
    o["f2_sel"] = np.kron(np.eye(8), np.ones((1, P))).reshape(8, 8, P).astype(np.float32)
    o["f3_w1"], o["f3_w2"] = rows(v["L3_ffn_w1"]), rows(v["L3_ffn_w2"])
    o["f3_b1"], o["f3_b2"] = col(v["L3_ffn_b1"]), col(v["L3_ffn_b2"])
    for k in (4, 8, 16):
        o[f"tri{k}"] = every(np.tril(np.ones((k, k), np.float32), -1))
    return o


def kernel(**inputs):
    import numpy as np
    import concourse.bacc as bacc
    from concourse.bass_utils import run_bass_kernel_spmd as run

    nc = bacc.Bacc("TRN2", target_bir_lowering=False, num_devices=1)
    arrays, d = {}, {}
    for name, a in layouts(inputs).items():
        arrays[f"in_{name}"] = a
        d[name] = nc.dram_tensor(f"in_{name}", a.shape, mybir.dt.from_np(a.dtype), kind="ExternalInput").ap()
    d["out"] = nc.dram_tensor("out_x", (B, S, D), F32, kind="ExternalOutput").ap()
    build(nc, d)
    return run(nc, [arrays], core_ids=[0]).results[0]["out_x"]
```

```python
import math
from contextlib import ExitStack

import concourse.bass as bass
from concourse import mybir

F32 = mybir.dt.float32
F32R = mybir.dt.float32r
BF16 = mybir.dt.bfloat16
U8 = mybir.dt.uint8
I32 = mybir.dt.int32
ALU = mybir.AluOpType
ACT = mybir.ActivationFunctionType
AX = mybir.AxisListType.X

P = 128
B, S, D = 2, 1024, 256
NT = B * S // P
TB = S // P
KT = D // P
H, S2 = 16, 77
HK = H * S2
HPB = 6
BANK = 512
NR = -(-HK // P)
RLAST = HK - (NR - 1) * P
CT = 4
NC = NT // CT
CN = CT * P
EPS = 1e-5
ROUND = 1.5 * 2 ** 23
PGROUPS = [range(0, 4), range(4, 8), range(8, NR)]
BANKS = [(512 * g, 6 * g, min(H, 6 * g + 6)) for g in range(3)]


class Attention:

    def __init__(self, name, dims, biased, fside, mask_value, split_out):
        self.split_out = split_out
        self.name, self.dims, self.biased, self.fside, self.mask_value = name, dims, biased, fside, mask_value
        self.hd = dims // H
        self.scale = float(self.hd) ** -0.5
        self.nm = dims // P
        self.g = P // self.hd
        self.seg = self.g * S2


def pipeline(eng, n, lead, step, body):
    for t in range(lead):
        body(t, t % step)
    with eng.Fori(0, (n - lead) // step) as i:
        for u in range(step):
            body(i * step + (lead + u), (lead + u) % step)
    for t in range(n, n + lead):
        body(t, t % step)


def chunks(eng, body):
    body(0)
    with eng.Fori(0, NC - 1) as i:
        body(i + 1)


def first(c):
    return isinstance(c, int) and c == 0


def live(t, lag, n):
    return not isinstance(t, int) or 0 <= t - lag < n


def has_before(t, k):
    return not isinstance(t, int) or t >= k


def build(nc, d, only=range(8)):
    ctx = ExitStack()
    with ctx:
        def sem(name):
            return ctx.enter_context(nc.semaphore(name))

        base = -(-nc.sbuf_base // 32) * 32
        limit = nc.sbuf_usable_end

        class Region:

            def __init__(self, start, end=None):
                self.at, self.end = start, end or limit

            def __call__(self, name, shape, dt=F32):
                n = 1
                for s in shape[1:]:
                    n *= s
                size = -(-n * {F32: 4, F32R: 4, BF16: 2, U8: 1, I32: 4}[dt] // 32) * 32
                t = nc.alloc_sbuf_tensor_at(name, shape, dt, offset=self.at)
                self.at += size
                assert self.at <= self.end, (name, self.at - self.end)
                return t

        keep = Region(base)
        x = keep("x", [P, NT, D])
        ident = keep("ident", [P, P])
        identb = keep("identb", [P, P], BF16)
        ones = keep("ones", [P, P])
        ctxT = keep("ctxT", [P, KT, B * S2])
        mhalf = keep("mhalf", [P, NT])
        stats = keep("stats", [P, NT, 6])
        tile_stats = keep("tile_stats", [P, 2, 6])
        mv = keep("mv", [P, NT, 2])
        ve = keep("ve", [P, NT])
        rstd = keep("rstd", [P, NT])
        spare = keep("spare", [P, 1])
        rounder = keep("rounder", [P, 1])
        start = keep.at + 256

        psum = ctx.enter_context(nc.psum_tensor("psum", [P, 8 * BANK], F32))

        def bank(i, a=0, n=BANK):
            return psum[:, i * BANK + a:i * BANK + a + n]

        x_loaded = sem("x_loaded")
        const_loaded = sem("const_loaded")
        const_made = sem("const_made")
        layer_end = sem("layer_end")
        stored = sem("stored")
        parts = {e: [] for e in ("sync", "tensor", "scalar", "vector", "gpsimd")}
        ends = [0]

        def barrier():
            ends[0] += 1
            k = ends[0]
            for e in ("tensor", "scalar", "vector", "gpsimd"):
                def stop(eng, k=k):
                    eng.drain().then_inc(layer_end, 1)
                    eng.wait_ge(layer_end, 4 * k)
                parts[e].append(stop)

            def hold(eng, k=k):
                eng.wait_ge(layer_end, 4 * k)
            parts["sync"].append(hold)

        def load_constants(eng):
            eng.dma_start(ctxT[:], d["ctxT"]).then_inc(const_loaded, 16)
            eng.dma_start(ident[:], d["ident"]).then_inc(const_loaded, 16)
        parts["sync"].append(load_constants)

        def load_x(eng):
            for b in range(B):
                eng.dma_start(x[:, TB * b:TB * (b + 1), :], d["x"][b].rearrange("(p j) n -> p j n", p=P)).then_inc(x_loaded, 16)

        def make_constants(eng):
            eng.memset(ones[:], 1.0).then_inc(const_made, 1)
            eng.memset(mhalf[:], -0.5).then_inc(const_made, 1)
            eng.memset(rounder[:], ROUND).then_inc(const_made, 1)
            eng.wait_ge(const_loaded, 32)
            eng.tensor_copy(identb[:], ident[:]).then_inc(const_made, 1)
        parts["gpsimd"].append(make_constants)

        def await_constants(eng):
            eng.wait_ge(const_made, 4)
            eng.wait_ge(const_loaded, 32)
        for e in ("tensor", "scalar", "vector", "gpsimd"):
            parts[e].append(await_constants)

        weights_loaded = sem("weights_loaded")
        k_weights_loaded = sem("k_weights_loaded")
        v_weights_loaded = sem("v_weights_loaded")
        loads_until, k_until, v_until = {"": 0}, {"": 0}, {"": 0}
        load_weights = {}
        order_of_layers = [n for i, n in enumerate(("a0_", "f0_", "a1_", "f1_", "a2_", "f2_", "a3_", "f3_")) if i in only]

        def loads(name, pairs, k_pairs=(), v_pairs=()):
            before = max(loads_until.values()), max(k_until.values()), max(v_until.values())
            loads_until[name] = before[0] + 16 * len(pairs)
            k_until[name] = before[1] + 16 * len(k_pairs)
            v_until[name] = before[2] + 16 * len(v_pairs)

            def go(eng):
                if before[0]:
                    eng.wait_ge(weights_loaded, before[0])
                if before[1] and k_pairs:
                    eng.wait_ge(k_weights_loaded, before[1])
                    eng.wait_ge(v_weights_loaded, before[2])
                for dst, src in k_pairs:
                    eng.dma_start(dst, src).then_inc(k_weights_loaded, 16)
                for dst, src in v_pairs:
                    eng.dma_start(dst, src).then_inc(v_weights_loaded, 16)
                for dst, src in pairs:
                    eng.dma_start(dst, src).then_inc(weights_loaded, 16)
            load_weights[name] = go
            if name == order_of_layers[0]:
                parts["sync"].append(go)
                parts["sync"].append(load_x)

        def load_weights_after(name, eng):
            k = order_of_layers.index(name) + 1
            if k < len(order_of_layers):
                load_weights[order_of_layers[k]](eng)

        def await_weights(name):
            for e in ("tensor", "scalar", "vector", "gpsimd"):
                parts[e].append(lambda eng: eng.wait_ge(weights_loaded, loads_until[name]))

        WEIGHTS = {"a0_": 33, "f0_": 43, "a1_": 33, "f1_": 22, "a2_": 12, "f2_": 54, "a3_": 9, "f3_": 17}
        weights_at, names = {}, list(WEIGHTS)
        for i, name in enumerate(names):
            top = limit if i % 2 == 0 else limit - 1024 * max(WEIGHTS[o] for o in names[i - 1:i + 2:2])
            weights_at[name] = (top // 32 * 32 - 1024 * WEIGHTS[name], top // 32 * 32)

        x_stats = sem("x_stats")
        ALL_AT_ONCE = ("f0_", "f1_", "a2_", "f2_", "f3_")

        def statistics(eng, T):
            eng.bn_stats(stats[:, bass.ds(T, 1), :].rearrange("p a n -> p (a n)"), x[:, bass.ds(T, 1), :].rearrange("p a n -> p (a n)")).then_inc(x_stats, 1)

        def statistics_wanted(name):
            k = order_of_layers.index(name) + 1
            return k < len(order_of_layers) and order_of_layers[k] in ALL_AT_ONCE

        NF3 = 8
        W3 = Region(*weights_at["f3_"])
        w1 = W3("f3_w1", [P, NF3, D])
        w2 = W3("f3_w2", [P, KT, NF3 * P])
        s1, i1, s2, i2 = (keep(k, [P, w]) for k, w in (("s1", NF3), ("i1", NF3), ("s2", KT), ("i2", KT)))
        assert keep.at <= start
        extremes_taken = sem("extremes_taken")
        ahead = "a3_" in order_of_layers and "f3_" in order_of_layers

        def extremes(eng, k):
            w, out = (w1, w2)[k // 2], (s1, i1, s2, i2)[k]
            if k == 0:
                eng.wait_ge(weights_loaded, loads_until["f3_"])
            eng.tensor_reduce(out[:], w[:], AX, (ALU.max, ALU.min)[k % 2]).then_inc(extremes_taken, 1)

        def region_end(n):
            k = names.index(n)
            return min(weights_at[o][0] for o in names[k:k + 2])

        def matmul_split(eng, out, w_hi, w_lo, v_hi, v_lo, start, stop):
            eng.matmul(out, w_hi, v_hi, start=start, stop=False, skip_group_check=True)
            eng.matmul(out, w_hi, v_lo, start=False, stop=False, skip_group_check=True)
            return eng.matmul(out, w_lo, v_hi, start=False, stop=stop, skip_group_check=True)

        kv_ready = sem("kv_ready")
        kv_taken = sem("kv_taken")
        fold_ready = sem("fold_ready")
        fold_taken = sem("fold_taken")
        fold_lo_taken = sem("fold_lo_taken")
        zeros_made = sem("zeros_made")
        prep = sem("fold_prepared")
        folds = {"done": 0, "kv": 0, "ready": 0, "fold": 0, "lo": 0, "prep": 0}
        attention_signals = {k: sem("tile_" + k) for k in (
        "ln_stats",
        "ln_rstd",
        "ln_done",
        "lnT_ready",
        "lnT_taken",
        "lnT_lo_taken",
        "pT_lo_taken",
        "sc_ready",
        "sc_freed",
        "sc_steps",
        "shifted",
        "exp_done",
        "sum_steps",
        "probs_done",
        "pT_ready",
        "pT_taken",
        "out_ready",
        "x_added",
        )}
        attention_tiles = {"tiles": 0, "sc_steps": 0, "split": 0}

        def attention(L):
            nm, seg, g, n = L.nm, L.seg, L.g, L.name
            lastrows = RLAST + (1 if L.biased else 0)
            R = Region(start)
            A = R(n + "A", [P, KT, B, HK], F32R)
            A_lo = R(n + "A_lo", [P, KT, B, HK], F32R)
            if L.split_out:
                VO = R(n + "VO", [P, B, NR, D], F32R)
                VO_lo = R(n + "VO_lo", [P, B, NR, D], F32R)
                last_VO = R(n + "last_VO", [P, B, D])
            else:
                VO = R(n + "VO", [P, B, NR, D])
            if L.fside:
                FT = 2
                fs = R(n + "fs", [P, 2, H, FT * S2])
                mk = R(n + "mk", [P, 2, H, CT * S2], U8)

                def of_tile(side, T, h0, h1, per):
                    return side[:, bass.ds(T // per % 2, 1), h0:h1, bass.ds(T % per * S2, S2)].rearrange("p a h k -> p (a h) k")
            elif L.mask_value:
                mk3 = R(n + "mk3", [P, NT, S2], U8)
                ma3 = R(n + "ma3", [P, NT, S2])
            shared = R.at
            W = Region(*weights_at[n])
            wqT = W(n + "wqT", [P, nm, D])
            wk = W(n + "wk", [P, KT, L.dims])
            wv = W(n + "wv", [P, KT, L.dims])
            wo = W(n + "wo", [P, nm, D])
            F = Region(shared, weights_at[n][0])
            BDK = F(n + "BDK", [P, B, nm, seg])
            BDV = F(n + "BDV", [P, B, nm, P + seg + P])
            group = W(n + "group", [P, 2, g])
            kvb = W(n + "kvb", [P, 2, nm])
            if L.biased:
                bq = W(n + "bq", [P, nm])
            k_pairs = [(wk[:], d[n + "Wk"]), (group[:, 0, :], d[n + "group"])]
            v_pairs = [(wv[:], d[n + "Wv"])]
            pairs = [(wqT[:], d[n + "WqT"]), (wo[:], d[n + "Wo"])]
            if L.biased:
                k_pairs += [(kvb[:, 0, :], d[n + "bk"])]
                v_pairs += [(kvb[:, 1, :], d[n + "bv"])]
                pairs += [(bq[:], d[n + "bq"])]
            loads(n, pairs, k_pairs, v_pairs)
            for e in ("tensor", "vector"):
                parts[e].append(lambda eng: eng.wait_ge(k_weights_loaded, k_until[n]))
            if L.biased:
                bo_loaded = sem(n + "bo_loaded")
                bo_at = last_VO[RLAST:RLAST + 1, :, :] if L.split_out else VO[RLAST:RLAST + 1, :, NR - 1, :]
                parts["sync"].append(lambda eng: eng.dma_start(bo_at, d[n + "bo2"]).then_inc(bo_loaded, 16))
            s = dict(attention_signals)
            if L.mask_value is not None:
                s["side_loaded"] = sem(n + "side_loaded")
                if L.fside:
                    s["masks_loaded"] = sem(n + "masks_loaded")
                else:
                    s["mask_added"] = sem(n + "mask_added")
            if L.biased:
                s["lnx_ones"] = sem(n + "lnx_ones")
            LO0 = attention_tiles["split"]
            T0, SC0 = attention_tiles["tiles"], attention_tiles["sc_steps"]
            if L.fside:
                def load_factors(eng, c):
                    if c >= 1:
                        eng.wait_ge(s["side_loaded"], 16 * c)
                    b, j = c * FT // TB, c * FT % TB
                    eng.dma_start(fs[:, c % 2], d["fside"][b].rearrange("h (p j) k -> p h (j k)", p=P)[:, :, j * S2:(j + FT) * S2]).then_inc(s["side_loaded"], 16)

                def load_masks(eng, c):
                    if c >= 1:
                        eng.wait_ge(s["masks_loaded"], 16 * c)
                    b, j = c * CT // TB, c * CT % TB
                    eng.dma_start(mk[:, c % 2], d["mask16"][b].rearrange("h (p j) k -> p h (j k)", p=P)[:, :, j * S2:(j + CT) * S2]).then_inc(s["masks_loaded"], 16)

                def sp_side(eng):
                    for c in range(2):
                        load_factors(eng, c)
                        load_masks(eng, c)
                parts["sync"].append(sp_side)
            elif L.mask_value:
                def sp_mask(eng):
                    for b in range(B):
                        eng.dma_start(mk3[:, TB * b:TB * (b + 1), :], d["mask1"][b, 0].rearrange("(p j) k -> p j k", p=P)).then_inc(s["side_loaded"], 16)
                parts["sync"].append(sp_mask)

            early = n == "a3_" and ahead
            if early:
                parts["sync"].append(lambda eng: load_weights_after(n, eng))
                assert F.at <= weights_at["f3_"][0]

            done0 = folds["done"]
            folds["done"] += 1
            kv0, ready0, fold0, lo0, prep0 = (folds[k] for k in ("kv", "ready", "fold", "lo", "prep"))

            def pe_kv(eng):
                for i in range(2 * nm):
                    m, w = i % nm, (wk, wv)[i // nm]
                    if i == nm:
                        eng.wait_ge(v_weights_loaded, v_until[n])
                    if i >= 4:
                        eng.wait_ge(kv_taken, kv0 + i - 3)
                    for kt in range(KT):
                        ins = eng.matmul(bank(i % 4, 0, B * S2), w[:, kt, P * m:P * m + P], ctxT[:, kt, :],
                                         start=kt == 0, stop=kt == KT - 1)
                    ins.then_inc(kv_ready, 1)
            parts["tensor"].append(pe_kv)

            def pool_zeros(eng):
                eng.memset(BDV[:], 0.0).then_inc(zeros_made, 1)
            parts["gpsimd"].append(pool_zeros)

            def dve_kv(eng):
                eng.tensor_scalar(group[:, 1, :], group[:, 0, :], L.scale, None, ALU.mult).then_inc(prep, 1)
                if not L.biased:
                    eng.memset(kvb[:], 0.0).then_inc(prep, 1)
                eng.wait_ge(prep, prep0 + (1 if L.biased else 2))
                for i in range(2 * nm):
                    m, v = i % nm, i // nm
                    if i == nm:
                        eng.wait_ge(v_weights_loaded, v_until[n])
                        eng.wait_ge(zeros_made, done0 + 1)
                    eng.wait_ge(kv_ready, kv0 + i + 1)
                    for b in range(B):
                        src = bank(i % 4, b * S2, S2).unsqueeze(1).broadcast_to([P, g, S2])
                        dst = BDV[:, b, m, P:P + seg] if v else BDK[:, b, m, :]
                        ins = eng.scalar_tensor_tensor(
                            out=dst.rearrange("p (g k) -> p g k", k=S2), in0=src, scalar=kvb[:, v, m:m + 1],
                            in1=group[:, 1 - v, :].unsqueeze(2).broadcast_to([P, g, S2]), op0=ALU.add, op1=ALU.mult)
                    ins.then_inc(kv_taken, 1)
                if L.biased:
                    eng.wait_ge(weights_loaded, loads_until[n])
                    for m in range(nm):
                        ins = eng.tensor_scalar(wqT[:, m, 1:D], wqT[:, m, 1:D], wqT[:, m, 0:1], None, ALU.subtract)
                    ins.then_inc(prep, 1)
                    eng.wait_ge(prep, prep0 + 2)
                    eng.tensor_copy(wqT[:, :, 0], bq[:]).then_inc(prep, 1)
            parts["vector"].append(dve_kv)

            jobs = [("A", b, kt) for b in range(B) for kt in range(KT)]
            jobs += [("VO", b, r) for b in range(B) for r in range(0, NR, 2)]

            def is_split(kind):
                return kind == "A" or L.split_out

            def pe_fold(eng):
                eng.wait_ge(kv_taken, kv0 + 2 * nm)
                eng.wait_ge(weights_loaded, loads_until[n])
                if L.biased:
                    eng.wait_ge(prep, prep0 + 3)
                    eng.wait_ge(bo_loaded, 16)
                for i, (kind, b, k) in enumerate(jobs):
                    if i >= 2:
                        eng.wait_ge(fold_taken, fold0 + i - 1)
                        if is_split(jobs[i - 2][0]):
                            eng.wait_ge(fold_lo_taken, lo0 + sum(is_split(j[0]) for j in jobs[:i - 1]))
                    b0 = 3 * (i % 2)
                    if kind != "VO":
                        for off, h0, h1 in BANKS:
                            for m in range(nm):
                                lo, hi = max(h0 * S2, m * seg), min(h1 * S2, (m + 1) * seg)
                                if lo < hi:
                                    o = b0 * BANK + off + lo - h0 * S2
                                    ins = eng.matmul(psum[:, o:o + hi - lo], wqT[:, m, P * k:P * k + P], BDK[:, b, m, lo - m * seg:hi - m * seg],
                                                     start=True, stop=True)
                    else:
                        for r in (k, k + 1):
                            rows = P if r < NR - 1 else RLAST
                            ms = [m for m in range(nm) if m * seg < P * r + rows and (m + 1) * seg > P * r]
                            for m in ms:
                                c = P + P * r - m * seg
                                ins = eng.matmul(psum[0:rows, (b0 + r - k) * BANK:(b0 + r - k) * BANK + D],
                                                 BDV[:, b, m, c:c + rows], wo[:, m, :],
                                                 start=m == ms[0], stop=m == ms[-1])
                    ins.then_inc(fold_ready, 1)
            parts["tensor"].append(pe_fold)

            def act_fold(eng):
                if L.biased:
                    eng.wait_ge(bo_loaded, 16)
                for i, (kind, b, k) in enumerate(jobs):
                    eng.wait_ge(fold_ready, ready0 + i + 1)
                    b0 = 3 * (i % 2)
                    if kind != "VO":
                        for off, h0, h1 in BANKS:
                            ins = eng.activation(A[:, k, b, h0 * S2:h1 * S2], psum[:, b0 * BANK + off:b0 * BANK + off + (h1 - h0) * S2], ACT.Copy)
                    else:
                        for r in (k, k + 1):
                            rows = P if r < NR - 1 else RLAST
                            to = last_VO[0:rows, b, :] if L.split_out and r == NR - 1 else VO[0:rows, b, r, :]
                            ins = eng.activation(to, psum[0:rows, (b0 + r - k) * BANK:(b0 + r - k) * BANK + D], ACT.Copy)
                    ins.then_inc(fold_taken, 1)
                if L.split_out:
                    eng.wait_ge(fold_taken, fold0 + len(jobs))
                    eng.activation(VO[0:lastrows, :, NR - 1, :], last_VO[0:lastrows, :, :], ACT.Copy).then_inc(fold_taken, 1)
            parts["scalar"].append(act_fold)

            EXTREMES_AT = [len(jobs) - 9 + 2 * k for k in range(4)]

            def dve_fold(eng):
                for i, (kind, b, k) in enumerate(jobs):
                    if not is_split(kind):
                        continue
                    eng.wait_ge(fold_taken, fold0 + i + 1)
                    b0 = 3 * (i % 2)
                    if kind != "VO":
                        for off, h0, h1 in BANKS:
                            ins = eng.tensor_tensor(A_lo[:, k, b, h0 * S2:h1 * S2], psum[:, b0 * BANK + off:b0 * BANK + off + (h1 - h0) * S2],
                                                    A[:, k, b, h0 * S2:h1 * S2].bitcast(F32), ALU.subtract)
                    else:
                        for r in (k, k + 1):
                            if r < NR - 1:
                                ins = eng.tensor_tensor(VO_lo[:, b, r, :], psum[:, (b0 + r - k) * BANK:(b0 + r - k) * BANK + D],
                                                        VO[:, b, r, :].bitcast(F32), ALU.subtract)
                    ins.then_inc(fold_lo_taken, 1)
                    if early and i in EXTREMES_AT:
                        extremes(eng, EXTREMES_AT.index(i))
                if L.split_out:
                    eng.wait_ge(fold_taken, fold0 + len(jobs) + 1)
                    eng.tensor_tensor(VO_lo[0:lastrows, :, NR - 1, :], last_VO[0:lastrows, :, :], VO[0:lastrows, :, NR - 1, :].bitcast(F32), ALU.subtract)
            parts["vector"].append(dve_fold)
            folds["lo"] += sum(is_split(j[0]) for j in jobs)
            folds["kv"] += 2 * nm
            folds["ready"] += len(jobs)
            folds["fold"] += len(jobs) + (1 if L.split_out else 0)
            folds["prep"] += 3 if L.biased else 2
            barrier()

            M, M2 = Region(shared, weights_at[names[names.index(n) + 1]][0]), Region(*weights_at[n]) if L.fside else None
            lnx = [M(n + f"lnx{i}", [P, D]) for i in range(2)]
            lnT = [M(n + f"lnT{i}", [P, KT, P], F32R) for i in range(2)]
            lnT_lo = [M(n + f"lnT_lo{i}", [P, KT, P], F32R) for i in range(2)]
            sc = [(M2 or M)(n + f"sc{i}", [P, HK]) for i in range(2)]
            pr = [(M2 or M)(n + f"pr{i}", [P, HK + 1]) for i in range(2)]
            if L.split_out:
                pT = [M(n + f"pT{i}", [P, NR, P], F32R) for i in range(2)]
                pT_lo = [M(n + f"pT_lo{i}", [P, NR, P], F32R) for i in range(2)]
            else:
                pT = [M2(n + f"pT{i}", [P, NR, P]) for i in range(2)]
            mx = M(n + "mx", [P, 2, H])
            sm = M(n + "sm", [P, 2, H])
            rs = M(n + "rs", [P, 2, H])

            NSC = 2 if L.fside else 1

            def of_bank(g):
                o, h0, h1 = BANKS[g]
                return psum[:, o:o + (h1 - h0) * S2].rearrange("p (h k) -> p h k", k=S2)

            if L.fside:
                def sp_side_late(eng):
                    load_weights_after(n, eng)
                    for c in range(2, NT // FT):
                        eng.wait_ge(s["sc_steps"], SC0 + NSC * FT * (c - 1))
                        load_factors(eng, c)
                        if c * FT % CT == 0 and c * FT >= 2 * CT:
                            load_masks(eng, c * FT // CT)
                parts["sync"].append(sp_side_late)
            elif not early:
                parts["sync"].append(lambda eng: load_weights_after(n, eng))


            def pe_main(eng):
                if L.biased:
                    eng.wait_ge(s["lnx_ones"], 2)

                def body(t, u):
                    def turn_lnx():
                        if not live(t, 0, NT):
                            return
                        T, i = t, u
                        eng.wait_ge(s["ln_done"], T0 + T + 1)
                        if has_before(T, 1):
                            eng.wait_ge(s["lnT_lo_taken"], T0 + T)
                        for kt in range(KT):
                            ins = eng.transpose(bank(7, P * kt, P), lnx[i][:, P * kt:P * kt + P], ident[:])
                        ins.then_inc(s["lnT_ready"], 1)

                    def scores(g):
                        if not live(t, 1, NT):
                            return
                        T, i = t - 1, 1 - u
                        b = T // TB
                        if g == 0:
                            eng.wait_ge(s["lnT_lo_taken"], T0 + T + 1)
                        if has_before(T, 1):
                            eng.wait_ge(s["sc_freed"], 3 * (T0 + T - 1) + g + 1)
                        o, h0, h1 = BANKS[g]
                        w = (h1 - h0) * S2
                        for kt in range(KT):
                            ins = matmul_split(eng, psum[:, o:o + w], lnT[i][:, kt, :], lnT_lo[i][:, kt, :],
                                               A[:, kt, bass.ds(b, 1), h0 * S2:h1 * S2], A_lo[:, kt, bass.ds(b, 1), h0 * S2:h1 * S2],
                                               kt == 0, kt == KT - 1)
                        ins.then_inc(s["sc_ready"], 1)

                    def turn(k):
                        if not live(t, 3, NT):
                            return
                        T, i = t - 3, 1 - u
                        if k == 0:
                            eng.wait_ge(s["probs_done"], T0 + T + 1)
                        if k >= 2 or has_before(T, 1):
                            eng.wait_ge(pT_left, pT_base + 3 * T + k - 1)
                        for r in PGROUPS[k]:
                            rows = P if r < NR - 1 else lastrows
                            o = (3 + (i + k) % 2) * BANK + (r % 4) * P
                            ins = eng.transpose(psum[0:rows, o:o + P], pr[i][:, P * r:P * r + rows], ident[:])
                        ins.then_inc(s["pT_ready"], 1)

                    def product(k):
                        if not live(t, 3, NT):
                            return
                        T, i = t - 3, 1 - u
                        b = T // TB
                        eng.wait_ge(pT_left, pT_base + 3 * T + k + 1)
                        if k == 0 and has_before(T, 2):
                            eng.wait_ge(s["x_added"], T0 + T - 1)
                        for r in PGROUPS[k]:
                            rows = P if r < NR - 1 else lastrows
                            v = VO[0:rows, bass.ds(b, 1), r, :]
                            if L.split_out:
                                ins = matmul_split(eng, bank(5 + i, 0, D), pT[i][0:rows, r, :], pT_lo[i][0:rows, r, :],
                                                   v, VO_lo[0:rows, bass.ds(b, 1), r, :], r == 0, r == NR - 1)
                            else:
                                ins = eng.matmul(bank(5 + i, 0, D), pT[i][0:rows, r, :], v, start=r == 0, stop=r == NR - 1)
                        if k == 2:
                            ins.then_inc(s["out_ready"], 1)

                    scores(0)
                    turn(0)
                    turn(1)
                    scores(1)
                    turn_lnx()
                    product(0)
                    turn(2)
                    scores(2)
                    product(1)
                    product(2)
                pipeline(eng, NT, 6, 2, body)
            parts["tensor"].append(pe_main)
            pT_left, pT_base = (s["pT_lo_taken"], 3 * LO0) if L.split_out else (s["pT_taken"], 3 * T0)

            def dve_main(eng):
                eng.wait_ge(x_loaded, 16 * B)

                def body(t, u):
                    def low(k):
                        if not L.split_out or not live(t, 5, NT):
                            return
                        T, i = t - 5, 1 - u
                        eng.wait_ge(s["pT_taken"], 3 * (T0 + T) + k + 1)
                        if k == 0 and has_before(T, 2):
                            eng.wait_ge(s["out_ready"], T0 + T - 1)
                        o = (3 + (i + k) % 2) * BANK
                        full = [r for r in PGROUPS[k] if r < NR - 1]
                        sl = slice(full[0], full[-1] + 1)
                        flat = lambda a: a.rearrange("p a n -> p (a n)")
                        ins = eng.tensor_tensor(flat(pT_lo[i][:, sl, :]), psum[:, o:o + len(full) * P], flat(pT[i][:, sl, :]).bitcast(F32), ALU.subtract)
                        if k == 2:
                            ins = eng.tensor_tensor(pT_lo[i][0:lastrows, NR - 1, :], psum[0:lastrows, o + P:o + 2 * P],
                                                    pT[i][0:lastrows, NR - 1, :].bitcast(F32), ALU.subtract)
                        ins.then_inc(s["pT_lo_taken"], 1)
                    def of_scores(g):
                        if not live(t, 3, NT):
                            return
                        T, i = t - 3, 1 - u
                        v = sc[i][:].rearrange("p (h k) -> p h k", k=S2)
                        if L.mask_value is None:
                            if g == 2:
                                eng.wait_ge(s["sc_freed"], 3 * (T0 + T) + 3)
                                eng.tensor_reduce(mx[:, i, :], v, AX, ALU.max).then_inc(s["sc_steps"], 1)
                            return
                        o, h0, h1 = BANKS[g]
                        if g == 0:
                            if has_before(T, 2):
                                eng.wait_ge(s["exp_done"], T0 + T - 1)
                            if L.fside:
                                eng.wait_ge(s["side_loaded"], 16 * (T // FT + 1))
                        eng.wait_ge(s["sc_ready"], 3 * (T0 + T) + g + 1)
                        if L.fside:
                            ins = eng.tensor_tensor(v[:, h0:h1, :], of_bank(g), of_tile(fs, T, h0, h1, FT), ALU.mult)
                        elif L.mask_value is not None:
                            ins = eng.tensor_tensor(v[:, h0:h1, :], of_bank(g), ma3[:, bass.ds(T, 1), :].broadcast_to([P, h1 - h0, S2]), ALU.add)
                        ins.then_inc(s["sc_freed"], 1)
                        if g == 2:
                            eng.wait_ge(s["sc_freed"], 3 * (T0 + T) + 3)
                            if L.fside:
                                eng.wait_ge(s["masks_loaded"], 16 * (T // CT + 1))
                                eng.scalar_tensor_tensor(out=v, in0=of_tile(mk, T, 0, H, CT), scalar=L.mask_value, in1=v,
                                                         op0=ALU.mult, op1=ALU.add).then_inc(s["sc_steps"], 1)
                                eng.wait_ge(s["sc_steps"], SC0 + NSC * T + 1)
                            eng.tensor_reduce(mx[:, i, :], v, AX, ALU.max).then_inc(s["sc_steps"], 1)

                    of_scores(0)
                    low(0)
                    low(1)
                    of_scores(1)
                    if live(t, 2, NT):
                        T, i = t - 2, u
                        eng.wait_ge(s["lnT_taken"], T0 + T + 1)
                        if has_before(T, 2):
                            eng.wait_ge(s["sc_ready"], 3 * (T0 + T - 1))
                        eng.tensor_tensor(lnT_lo[i][:].rearrange("p a n -> p (a n)"), bank(7, 0, KT * P),
                                          lnT[i][:].rearrange("p a n -> p (a n)").bitcast(F32), ALU.subtract).then_inc(s["lnT_lo_taken"], 1)
                    if live(t, 4, NT):
                        T, i = t - 4, u
                        eng.wait_ge(s["exp_done"], T0 + T + 1)
                        eng.tensor_reduce(sm[:, i, :], pr[i][:, 0:HK].rearrange("p (h k) -> p h k", k=S2), AX, ALU.add).then_inc(s["sum_steps"], 1)
                        eng.wait_ge(s["sum_steps"], 2 * (T0 + T) + 1)
                        if has_before(T, 2):
                            eng.wait_ge(s["probs_done"], T0 + T - 1)
                        eng.reciprocal(rs[:, i, :], sm[:, i, :]).then_inc(s["sum_steps"], 1)
                    low(2)
                    of_scores(2)
                    if live(t, 6, NT):
                        T, i = t - 6, u
                        eng.wait_ge(s["out_ready"], T0 + T + 1)
                        xt = x[:, bass.ds(T, 1), :].rearrange("p a n -> p (a n)")
                        eng.tensor_tensor(xt, xt, bank(5 + i, 0, D), ALU.add).then_inc(s["x_added"], 1)
                        if statistics_wanted(n):
                            eng.wait_ge(s["x_added"], T0 + T + 1)
                            statistics(eng, T)
                    if live(t, 1, NT):
                        T, i = t - 1, 1 - u
                        eng.wait_ge(s["ln_rstd"], T0 + T + 1)
                        if has_before(T, 2):
                            eng.wait_ge(s["lnT_ready"], T0 + T - 1)
                        f0 = 1 if L.biased else 0
                        eng.tensor_scalar(lnx[i][:, f0:], x[:, bass.ds(T, 1), f0:].rearrange("p a n -> p (a n)"), mv[:, i, 0:1], rstd[:, i:i + 1],
                                          ALU.subtract, ALU.mult).then_inc(s["ln_done"], 1)
                    if live(t, 0, NT):
                        T, i = t, u
                        if has_before(T, 2):
                            eng.wait_ge(s["ln_rstd"], T0 + T - 1)
                        eng.bn_stats(tile_stats[:, i, :], x[:, bass.ds(T, 1), :].rearrange("p a n -> p (a n)")).then_inc(s["ln_stats"], 1)
                        eng.wait_ge(s["ln_stats"], 3 * (T0 + T) + 1)
                        eng.memset(spare[:], 0.0)
                        eng.bn_aggr(mv[:, i, :], tile_stats[:, i, :]).then_inc(s["ln_stats"], 1)
                        eng.wait_ge(s["ln_stats"], 3 * (T0 + T) + 2)
                        eng.tensor_scalar(ve[:, i:i + 1], mv[:, i, 1:2], EPS, None, ALU.add).then_inc(s["ln_stats"], 1)
                if not L.fside and L.mask_value:
                    eng.wait_ge(s["mask_added"], 1)
                pipeline(eng, NT, 6, 2, body)
            parts["vector"].append(dve_main)

            def act_main(eng):
                def body(t, u):
                    def take_pT(k):
                        if not live(t, 3, NT):
                            return
                        T, i = t - 3, 1 - u
                        if k == 0 and has_before(T, 2):
                            eng.wait_ge(s["out_ready"], T0 + T - 1)
                        eng.wait_ge(s["pT_ready"], 3 * (T0 + T) + k + 1)
                        o = (3 + (i + k) % 2) * BANK
                        full = [r for r in PGROUPS[k] if r < NR - 1]
                        ins = eng.activation(pT[i][:, full[0]:full[-1] + 1, :].rearrange("p a n -> p (a n)"), psum[:, o:o + len(full) * P], ACT.Copy)
                        if k == 2:
                            ins = eng.activation(pT[i][0:lastrows, NR - 1, :], psum[0:lastrows, o + P:o + 2 * P], ACT.Copy)
                        ins.then_inc(s["pT_taken"], 1)
                    def take_scores(g):
                        if L.mask_value is not None or not live(t, 1, NT):
                            return
                        T, i = t - 1, 1 - u
                        o, h0, h1 = BANKS[g]
                        if g == 0 and has_before(T, 2):
                            eng.wait_ge(s["exp_done"], T0 + T - 1)
                        eng.wait_ge(s["sc_ready"], 3 * (T0 + T) + g + 1)
                        eng.activation(sc[i][:, h0 * S2:h1 * S2], psum[:, o:o + (h1 - h0) * S2], ACT.Copy).then_inc(s["sc_freed"], 1)
                    take_scores(0)
                    take_pT(0)
                    take_pT(1)
                    take_scores(1)
                    if live(t, 0, NT):
                        T, i = t, u
                        eng.wait_ge(s["lnT_ready"], T0 + T + 1)
                        if has_before(T, 2):
                            eng.wait_ge(s["sc_ready"], 3 * (T0 + T - 1))
                        eng.activation(lnT[i][:].rearrange("p a n -> p (a n)"), bank(7, 0, KT * P), ACT.Copy).then_inc(s["lnT_taken"], 1)
                    if live(t, 2, NT):
                        T, i = t - 2, u
                        eng.wait_ge(s["shifted"], T0 + T + 1)
                        if has_before(T, 2):
                            eng.wait_ge(s["pT_ready"], 3 * (T0 + T - 1))
                        eng.activation(pr[i][:, 0:HK], sc[i][:], ACT.Exp).then_inc(s["exp_done"], 1)
                    take_pT(2)
                    take_scores(2)
                pipeline(eng, NT, 6, 2, body)
            parts["scalar"].append(act_main)

            def pool_main(eng):
                for i in range(2):
                    eng.memset(pr[i][:, HK:HK + 1], 1.0)
                    if L.biased:
                        eng.memset(lnx[i][:, 0:1], 1.0).then_inc(s["lnx_ones"], 1)
                if not L.fside and L.mask_value:
                    eng.wait_ge(s["side_loaded"], 32)
                    eng.tensor_scalar(ma3[:], mk3[:], L.mask_value, 1.0, ALU.mult, ALU.mult).then_inc(s["mask_added"], 1)

                def body(t, u):
                    if live(t, 4, NT):
                        T, i = t - 4, u
                        v = pr[i][:, 0:HK].rearrange("p (h k) -> p h k", k=S2)
                        eng.wait_ge(s["sum_steps"], 2 * (T0 + T) + 2)
                        eng.tensor_tensor(v, v, rs[:, i, :].unsqueeze(2).broadcast_to([P, H, S2]), ALU.mult).then_inc(s["probs_done"], 1)
                    if live(t, 3, NT):
                        T, i = t - 3, 1 - u
                        v = sc[i][:].rearrange("p (h k) -> p h k", k=S2)
                        eng.wait_ge(s["sc_steps"], SC0 + NSC * (T + 1))
                        eng.tensor_tensor(v, v, mx[:, i, :].unsqueeze(2).broadcast_to([P, H, S2]), ALU.subtract).then_inc(s["shifted"], 1)
                    if live(t, 0, NT):
                        T, i = t, u
                        eng.wait_ge(s["ln_stats"], 3 * (T0 + T) + 3)
                        if has_before(T, 2):
                            eng.wait_ge(s["ln_done"], T0 + T - 1)
                        eng.tensor_tensor(rstd[:, i:i + 1], ve[:, i:i + 1], mhalf[:, 0:1], ALU.pow).then_inc(s["ln_rstd"], 1)
                pipeline(eng, NT, 6, 2, body)
            parts["gpsimd"].append(pool_main)
            attention_tiles["tiles"] += NT
            attention_tiles["split"] += NT if L.split_out else 0
            attention_tiles["sc_steps"] += NSC * NT
            barrier()

        ln_stats = sem("ln_stats")
        ln_rstd = sem("ln_rstd")
        ln_done = sem("ln_done")
        lnT_ready = sem("lnT_ready")
        lnT_taken = sem("lnT_taken")
        lnT_lo_taken = sem("lnT_lo_taken")
        EACH = NT + 1
        calls = {"ln": 0, "lo": 0}

        def normalise(n, lnx, lnT=None, lnT_lo=None, logits=None, dve_meanwhile=None, act_meanwhile=None):
            n0 = calls["ln"]
            c0 = NC * n0
            l0 = NC * calls["lo"]
            calls["ln"] += 1
            if lnT_lo is not None:
                calls["lo"] += 1

            def dve_ln(eng):
                eng.wait_ge(x_loaded, 16 * B)
                if order_of_layers[0] == n:
                    with eng.Fori(0, NC) as c:
                        for q in range(CT):
                            statistics(eng, CT * c + q)
                eng.wait_ge(x_stats, NT * (n0 + 1))
                eng.memset(spare[:], 0.0)
                for T in range(NT):
                    eng.bn_aggr(mv[:, T, :], stats[:, T, :]).then_inc(ln_stats, 1)
                eng.wait_ge(ln_stats, EACH * n0 + NT)
                eng.tensor_scalar(ve[:], mv[:, :, 1], EPS, None, ALU.add).then_inc(ln_stats, 1)
                if dve_meanwhile:
                    dve_meanwhile(eng)
                def low(c):
                    for kt in range(KT):
                        eng.wait_ge(lnT_taken, 2 * (c0 + c) + kt + 1)
                        eng.tensor_tensor(lnT_lo[:, kt, CN * c:CN * (c + 1)], bank(2 * c + kt), lnT[:, kt, CN * c:CN * (c + 1)].bitcast(F32),
                                          ALU.subtract).then_inc(lnT_lo_taken, 1)
                for c in range(NC):
                    eng.wait_ge(ln_rstd, c0 + c + 1)
                    for T in range(CT * c, CT * c + CT):
                        ins = eng.tensor_scalar(lnx[:, T, :], x[:, T, :], mv[:, T, 0:1], rstd[:, T:T + 1], ALU.subtract, ALU.mult)
                    ins.then_inc(ln_done, 1)
                    if lnT_lo is not None and c >= 1:
                        low(c - 1)
                if lnT_lo is not None:
                    low(NC - 1)
            parts["vector"].append(dve_ln)

            def pool_ln(eng):
                eng.wait_ge(ln_stats, EACH * (n0 + 1))
                for c in range(NC):
                    tiles = slice(CT * c, CT * (c + 1))
                    eng.tensor_tensor(rstd[:, tiles], ve[:, tiles], mhalf[:, tiles], ALU.pow).then_inc(ln_rstd, 1)
            parts["gpsimd"].append(pool_ln)
            if lnT is None:
                return c0

            multiply, turn, take, take_turned = logits or (None,) * 4

            def pe_ln(eng):
                for c in range(NC + 2):
                    if c < NC:
                        eng.wait_ge(ln_done, c0 + c + 1)
                        for kt in range(KT):
                            for q in range(CT):
                                ins = eng.transpose(bank(2 * c + kt, P * q, P), lnx[:, CT * c + q, P * kt:P * kt + P], ident[:])
                            ins.then_inc(lnT_ready, 1)
                    if 1 <= c <= NC and lnT_lo is not None:
                        eng.wait_ge(lnT_lo_taken, 2 * (l0 + c))
                        if logits:
                            multiply(eng, c - 1)
                    if c >= 2 and logits:
                        turn(eng, c - 2)
                eng.wait_ge(lnT_taken, 2 * (c0 + NC))
            parts["tensor"].append(pe_ln)

            def act_ln(eng):
                for c in range(NC + 2):
                    for kt in range(KT if c < NC else 0):
                        eng.wait_ge(lnT_ready, 2 * (c0 + c) + kt + 1)
                        eng.activation(lnT[:, kt, CN * c:CN * (c + 1)], bank(2 * c + kt), ACT.Copy).then_inc(lnT_taken, 1)
                    if logits and c >= 2:
                        take_turned(eng, c - 2)
                    if logits and 1 <= c <= NC:
                        take(eng, c - 1)
                    if act_meanwhile:
                        act_meanwhile(eng, c + 1)
            parts["scalar"].append(act_ln)
            return c0

        def feed_forward(n, nf, first_routed=None, per_weight=1, experts=0, route=None, gated=True, biased=False):
            W = Region(*weights_at[n])
            wg = W(n + "wg", [P, KT, nf * P])
            wu = W(n + "wu", [P, KT, nf * P]) if gated else None
            wd = W(n + "wd", [P, nf, D])
            R = Region(start, region_end(n))
            lnT = R(n + "lnT", [P, KT, NC * CN], F32R)
            lnT_lo = R(n + "lnT_lo", [P, KT, NC * CN], F32R)
            wg_hi = R(n + "wg_hi", [P, KT, nf * P], F32R)
            wu_hi = R(n + "wu_hi", [P, KT, nf * P], F32R) if gated else None
            wd_hi = R(n + "wd_hi", [P, nf, D], F32R)
            W_lo = Region(*weights_at[n])
            wg_lo = W_lo(n + "wg_lo", [P, KT, nf * P], F32R)
            wu_lo = W_lo(n + "wu_lo", [P, KT, nf * P], F32R) if gated else None
            wd_lo = W_lo(n + "wd_lo", [P, nf, D], F32R)
            I = Region(R.at, region_end(n))
            lnx = R(n + "lnx", [P, NT, D])
            h = [I(n + f"h{i}", [P, CN]) for i in range(2)]
            h_hi = [I(n + f"h_hi{i}", [P, CN], F32R) for i in range(4)]
            h_lo = [I(n + f"h_lo{i}", [P, CN], F32R) for i in range(4)]
            R.at = max(R.at, I.at)
            before_th = Region(R.at, region_end(n))
            th = [R(n + f"th{i}", [P, CN]) for i in range(2)]
            WG = 4
            NG = nf // WG
            pairs = [(wg[:], d[n + "wg"]), (wd[:], d[n + "wd"])] + ([(wu[:], d[n + "wu"])] if gated else [])
            if experts:
                ns = (nf - first_routed) // per_weight
                wr = W(n + "wr", [P, KT, P])
                wr_hi = before_th(n + "wr_hi", [P, KT, P], F32R)
                wr_lo = before_th(n + "wr_lo", [P, KT, P], F32R)
                tlT = before_th(n + "tlT", [experts, CN])
                sel = W(n + "sel", [experts, ns, P])
                cw = R(n + "cw", [P, CT, experts])
                tl = R(n + "tl", [P, NT, experts])
                cwT = R(n + "cwT", [experts, CN], F32R)
                cwT_lo = R(n + "cwT_lo", [experts, CN], F32R)
                sel_r = R(n + "sel_r", [experts, ns, P], F32R)
                pairs += [(wr[:], d[n + "wr"]), (sel[:], d[n + "sel"])]
            if biased:
                b1 = W(n + "b1", [P, nf])
                b2 = W(n + "b2", [P, D])
                pairs += [(b1[:], d[n + "b1"]), (b2[:], d[n + "b2"])]
            more = route(n, R, W, pairs, tl, cw) if experts else None
            loads(n, pairs)
            parts["sync"].append(lambda eng: load_weights_after(n, eng))

            w_hi_done = sem(n + "w_hi_done")
            w_lo_done = sem(n + "w_lo_done")
            g_ready = sem(n + "g_ready")
            h_full = sem(n + "h_full")
            hi_done = sem(n + "hi_done")
            lo_done = sem(n + "lo_done")
            out_ready = sem(n + "out_ready")
            x_added = sem(n + "x_added")
            h_steps = sem(n + "h_steps")
            if gated:
                u_ready = sem(n + "u_ready")
                th_done = sem(n + "th_done")
            if experts:
                wr_done = sem(n + "wr_done")
                logits_ready = sem(n + "logits_ready")
                tlT_done = sem(n + "tlT_done")
                tl_ready = sem(n + "tl_ready")
                tl_done = sem(n + "tl_done")
                c_ready = sem(n + "c_ready")
                cw_done = sem(n + "cw_done")
                cwT_ready = sem(n + "cwT_ready")
                cwT_taken = sem(n + "cwT_taken")
                cwT_lo_taken = sem(n + "cwT_lo_taken")
                sel_done = sem(n + "sel_done")

            def logits(eng, c):
                eng.wait_ge(wr_done, 2)
                for kt in range(KT):
                    cols = slice(CN * c, CN * (c + 1))
                    ins = matmul_split(eng, bank(2 * c), wr_hi[:, kt, :], wr_lo[:, kt, :], lnT[:, kt, cols], lnT_lo[:, kt, cols], kt == 0, kt == KT - 1)
                ins.then_inc(logits_ready, 1)

            def turn_logits(eng, c):
                eng.wait_ge(tlT_done, c + 1)
                for q in range(CT):
                    ins = eng.transpose(bank(2 * c + 1, experts * q, experts), tlT[:, P * q:P * q + P], ident[0:experts, 0:experts])
                ins.then_inc(tl_ready, 1)

            def take_logits(eng, c):
                eng.wait_ge(logits_ready, c + 1)
                eng.activation(tlT[:], bank(2 * c)[0:experts], ACT.Tanh, scale=more.scale).then_inc(tlT_done, 1)

            def take_turned(eng, c):
                eng.wait_ge(tl_ready, c + 1)
                eng.activation(tl[:, CT * c:CT * (c + 1), :].rearrange("p q e -> p (q e)"), bank(2 * c + 1, 0, CT * experts), ACT.Copy).then_inc(tl_done, 1)
            await_weights(n)

            def of_group(k):
                a, b = WG * k, WG * (k + 1)
                up = [(w[:, :, P * a:P * b], hi[:, :, P * a:P * b], lo[:, :, P * a:P * b])
                      for w, hi, lo in ((wg, wg_hi, wg_lo),) + (((wu, wu_hi, wu_lo),) if gated else ())]
                return up + [(wd[:, a:b, :], wd_hi[:, a:b, :], wd_lo[:, a:b, :])]

            PIECES = 3 if gated else 2
            IN_LN = 2

            def upper_part(eng, k, j):
                whole, upper, lower = of_group(k)[j]
                eng.activation(upper, whole, ACT.Copy).then_inc(w_hi_done, 1)

            def lower_part(eng, k, j):
                whole, upper, lower = of_group(k)[j]
                eng.wait_ge(w_hi_done, PIECES * k + j + 1)
                ins = eng.tensor_tensor(lower, whole, upper.bitcast(F32), ALU.subtract)
                if j == PIECES - 1:
                    ins.then_inc(w_lo_done, 1)

            def piece_at(m, lead):
                k, j = IN_LN + (m - lead) // WG, (m - lead) % WG
                return (k, j) if m >= lead and k < NG and j < PIECES else None

            def act_weights(eng, c):
                if c == 2:
                    for j in range(PIECES):
                        upper_part(eng, 1, j)
                if experts and c == 3:
                    eng.activation(sel_r[:], sel[:], ACT.Copy).then_inc(sel_done, 1)
            parts["scalar"].append(lambda eng: [upper_part(eng, 0, j) for j in range(PIECES)])

            def dve_weights(eng):
                if experts:
                    eng.tensor_copy(wr_hi[:], wr[:]).then_inc(wr_done, 1)
                if experts:
                    eng.wait_ge(wr_done, 1)
                    eng.tensor_tensor(wr_lo[:], wr[:], wr_hi[:].bitcast(F32), ALU.subtract).then_inc(wr_done, 1)

            if experts:
                more.first()
            normalise(n, lnx, lnT, lnT_lo, (logits, turn_logits, take_logits, take_turned) if experts else None, dve_weights, act_weights)

            def pool_weights(eng):
                for k in range(IN_LN):
                    for j in range(PIECES):
                        lower_part(eng, k, j)
            parts["gpsimd"].append(pool_weights)
            if experts:
                more.then(tl_done, cw_done)

            routed = [m for m in range(nf) if experts and m >= first_routed]
            nr = len(routed)
            n_sel = nr // per_weight
            LAG = 2

            def pe_ff(eng):
                if experts:
                    eng.wait_ge(tl_done, NC)

                def down(c, m):
                    eng.wait_ge(lo_done, nf * c + m + 1)
                    if m == 0 and not first(c):
                        eng.wait_ge(x_added, c)
                    for q in range(CT):
                        cols = slice(P * q, P * q + P)
                        ins = matmul_split(eng, bank(5 + q // 2, D * (q % 2), D), h_hi[m % 4][:, cols], h_lo[m % 4][:, cols],
                                           wd_hi[:, m, :], wd_lo[:, m, :], m == 0 and q % 2 == 0, m == nf - 1)
                    if m == nf - 1:
                        ins.then_inc(out_ready, 1)

                def turn_weights(c):
                    eng.wait_ge(cw_done, c + 1)
                    for q in range(CT):
                        ins = eng.transpose(bank(4, P * q, P)[0:experts], cw[:, q, :], ident[:])
                    ins.then_inc(cwT_ready, 1)

                def body(c):
                    for m in range(nf):
                        if first(c) and m % WG == 0:
                            eng.wait_ge(w_lo_done, m // WG + 1)
                        if not first(c) or m >= 2:
                            eng.wait_ge(h_full, nf * c + m - 1)
                        late = experts and first(c) and first_routed == 0
                        if experts and m == first_routed and not late:
                            turn_weights(c)
                        for ready, b0, hi, lo in ((g_ready, 0, wg_hi, wg_lo),) + (((u_ready, 2, wu_hi, wu_lo),) if gated else ()):
                            for kt in range(KT):
                                ins = matmul_split(eng, bank(b0 + m % 2), hi[:, kt, P * m:P * m + P], lo[:, kt, P * m:P * m + P],
                                                   lnT[:, kt, bass.ds(CN * c, CN)], lnT_lo[:, kt, bass.ds(CN * c, CN)], kt == 0, kt == KT - 1)
                            ins.then_inc(ready, 1)
                        if m >= LAG:
                            down(c, m - LAG)
                        elif not first(c):
                            down(c - 1, nf + m - LAG)
                        if late and m == 1:
                            turn_weights(c)
                        if m in routed and (m == 1 if late and m < 2 else routed.index(m) % per_weight == 0):
                            r = routed.index(m) // per_weight
                            if r == 0:
                                eng.wait_ge(cwT_lo_taken, c + 1)
                                if first(c):
                                    eng.wait_ge(sel_done, 1)
                            eng.matmul(bank((4, 7)[r % 2]), sel_r[:, r, :], cwT[:], start=True, stop=False)
                            eng.matmul(bank((4, 7)[r % 2]), sel_r[:, r, :], cwT_lo[:], start=False, stop=True).then_inc(c_ready, 1)
                chunks(eng, body)
                for m in range(nf - LAG, nf):
                    down(NC - 1, m)
            parts["tensor"].append(pe_ff)

            def act_ff(eng):
                def high(c, m):
                    eng.wait_ge(h_full, nf * c + m + 1)
                    eng.activation(h_hi[m % 4][:], h[m % 2][:], ACT.Copy).then_inc(hi_done, 1)

                def body(c):
                    for m in range(nf):
                        if experts and m == routed[0]:
                            eng.wait_ge(cwT_ready, c + 1)
                            eng.activation(cwT[:], bank(4)[0:experts], ACT.Copy).then_inc(cwT_taken, 1)
                        eng.wait_ge(g_ready, nf * c + m + 1)
                        if gated:
                            if not first(c) or m >= 2:
                                eng.wait_ge(h_full, nf * c + m - 1)
                            eng.activation(th[m % 2][:], bank(m % 2), ACT.Tanh, scale=0.5).then_inc(th_done, 1)
                            if m >= 1:
                                high(c, m - 1)
                            elif not first(c):
                                high(c - 1, nf - 1)
                            if first(c) and piece_at(m, 1):
                                upper_part(eng, *piece_at(m, 1))
                        else:
                            if not first(c) or m >= 2:
                                eng.wait_ge(lo_done, nf * c + m - 1)
                            eng.activation(h[m % 2][:], bank(m % 2), ACT.Relu, bias=b1[:, m:m + 1]).then_inc(h_full, 1)
                chunks(eng, body)
                if gated:
                    high(NC - 1, nf - 1)
            parts["scalar"].append(act_ff)

            def pool_ff(eng):
                def body(c):
                    for m in range(nf):
                        eng.wait_ge(hi_done, nf * c + m + 1)
                        eng.tensor_tensor(h_lo[m % 4][:], h[m % 2][:], h_hi[m % 4][:].bitcast(F32), ALU.subtract).then_inc(lo_done, 1)
                        if first(c) and piece_at(m, 1):
                            lower_part(eng, *piece_at(m, 1))
                chunks(eng, body)
            parts["gpsimd"].append(pool_ff)

            inner = nf + nr if gated else 0

            def dve_ff(eng):
                added = 2 if biased else 0

                def add(c):
                    eng.wait_ge(out_ready, c + 1)
                    for k2 in range(2):
                        xt = x[:, bass.ds(CT * c + 2 * k2, 2), :]
                        ins = eng.tensor_tensor(xt, xt, bank(5 + k2).rearrange("p (a n) -> p a n", a=2), ALU.add)
                        if biased:
                            ins.then_inc(h_steps, 1)
                            eng.wait_ge(h_steps, 2 * c + k2 + 1)
                            ins = eng.tensor_tensor(xt, xt, b2[:].unsqueeze(1).broadcast_to([P, 2, D]), ALU.add)
                    ins.then_inc(x_added, 1)
                    if statistics_wanted(n):
                        eng.wait_ge(x_added, c + 1)
                        for q in range(CT):
                            statistics(eng, CT * c + q)

                def body(c):
                    k = 0

                    def step(ins):
                        nonlocal k
                        k += 1
                        ins.then_inc(h_steps, 1)
                        eng.wait_ge(h_steps, c * inner + k)
                    if experts:
                        more.after(eng, c, -1)
                    for m in range(nf):
                        if m == LAG and not first(c):
                            add(c - 1)
                        if not gated:
                            eng.wait_ge(h_full, nf * c + m + 1)
                            eng.tensor_copy(h_hi[m % 4][:], h[m % 2][:]).then_inc(hi_done, 1)
                            continue
                        hm = h[m % 2][:]
                        if experts and m == first_routed:
                            eng.wait_ge(cwT_taken, c + 1)
                            eng.tensor_tensor(cwT_lo[:], bank(4)[0:experts], cwT[:].bitcast(F32), ALU.subtract).then_inc(cwT_lo_taken, 1)
                        eng.wait_ge(u_ready, nf * c + m + 1)
                        eng.wait_ge(th_done, nf * c + m + 1)
                        if not first(c) or m >= 2:
                            eng.wait_ge(lo_done, nf * c + m - 1)
                        step(eng.scalar_tensor_tensor(out=hm, in0=th[m % 2][:], scalar=1.0, in1=bank(2 + m % 2), op0=ALU.add, op1=ALU.mult))
                        last = eng.scalar_tensor_tensor(out=hm, in0=hm, scalar=0.5, in1=bank(m % 2), op0=ALU.mult, op1=ALU.mult)
                        if m in routed:
                            r = routed.index(m) // per_weight
                            step(last)
                            eng.wait_ge(c_ready, n_sel * c + r + 1)
                            last = eng.tensor_tensor(hm, hm, bank((4, 7)[r % 2]), ALU.mult)
                        last.then_inc(h_full, 1)
                        if experts:
                            more.after(eng, c, m)
                chunks(eng, body)
                add(NC - 1)
            parts["vector"].append(dve_ff)
            barrier()

        def rank_below(step, eng, v, gt, eq, tri, cnt, sel, rows, n, k):
            a = v.unsqueeze(2).broadcast_to([P, rows, n, n])
            b = v.unsqueeze(3).broadcast_to([P, rows, n, n])
            yield from step(eng.tensor_tensor(gt, a, b, ALU.is_gt))
            yield from step(eng.tensor_tensor(eq, a, b, ALU.is_equal))
            yield from step(eng.tensor_tensor(eq, eq, tri[:].unsqueeze(1).broadcast_to([P, rows, n, n]), ALU.mult))
            yield from step(eng.tensor_tensor(gt, gt, eq, ALU.add))
            yield from step(eng.tensor_reduce(cnt, gt, AX, ALU.add))
            yield from step(eng.tensor_scalar(sel, cnt, float(k), None, ALU.is_lt))

        class GroupRoute:
            scale = 0.5
            E, G = 16, 4

            def __init__(self, n, R, W, pairs, tl, cw):
                self.n, self.tl, self.cw = n, tl, cw
                E, G = self.E, self.G
                self.bias = W(n + "bias", [P, E])
                self.tri4 = W(n + "tri4", [P, G, G])
                self.tri16 = W(n + "tri16", [P, E, E])
                self.score, self.sb, self.m1, self.sel = (R(n + k, [P, CT, E]) for k in ("score", "sb", "m1", "sel"))
                self.two = R(n + "two", [P, CT * G, 6])
                self.gs, self.gcnt, self.gsel = (R(n + k, [P, CT, G]) for k in ("gs", "gcnt", "gsel"))
                self.g4, self.e4 = (R(n + k, [P, CT, G, G]) for k in ("g4", "e4"))
                self.g16, self.e16 = (R(n + k, [P, CT, E, E]) for k in ("g16", "e16"))
                self.cnt = R(n + "cnt", [P, CT, E])
                self.total = R(n + "total", [P, CT])
                pairs += [(self.bias[:], d[n + "bias"]), (self.tri4[:], d["tri4"]), (self.tri16[:], d["tri16"])]

            def first(self):
                pass

            STEPS = 27

            def then(self, tl_done, cw_done):
                self.tl_done, self.cw_done = tl_done, cw_done
                self.route_steps = sem(self.n + "route_steps")

            def route(self, eng, c):
                E, G = self.E, self.G
                k = 0

                def step(ins):
                    nonlocal k
                    k += 1
                    ins.then_inc(self.route_steps, 1)
                    eng.wait_ge(self.route_steps, c * self.STEPS + k)
                    yield
                every = lambda t: t.unsqueeze(3).broadcast_to([P, CT, G, E // G])
                yield from step(eng.tensor_scalar(self.score[:], self.tl[:, bass.ds(CT * (c % NC), CT), :], 0.5, 0.5, ALU.mult, ALU.add))
                yield from step(eng.tensor_tensor(self.sb[:], self.score[:], self.bias[:].unsqueeze(1).broadcast_to([P, CT, E]), ALU.add))
                v = self.sb[:].rearrange("p q (g k) -> p (q g) k", g=G)
                two = self.two[:]
                yield from step(eng.tensor_tensor(two[:, :, 0:2], v[:, :, 0:2], v[:, :, 2:4], ALU.add))
                yield from step(eng.tensor_tensor(two[:, :, 2:4], v[:, :, 0:4:2], v[:, :, 1:4:2], ALU.add))
                yield from step(eng.tensor_tensor(two[:, :, 4:5], v[:, :, 0:1], v[:, :, 3:4], ALU.add))
                yield from step(eng.tensor_tensor(two[:, :, 5:6], v[:, :, 1:2], v[:, :, 2:3], ALU.add))
                yield from step(eng.tensor_reduce(self.gs[:].rearrange("p q g -> p (q g)"), two, AX, ALU.max))
                yield from rank_below(step, eng, self.gs[:], self.g4[:], self.e4[:], self.tri4, self.gcnt[:], self.gsel[:], CT, G, 2)
                yield from step(eng.tensor_tensor(self.m1[:].rearrange("p q (g k) -> p q g k", g=G), self.sb[:].rearrange("p q (g k) -> p q g k", g=G),
                                       every(self.gsel[:]), ALU.mult))
                yield from step(eng.tensor_scalar(self.gcnt[:], self.gsel[:], -1.0, 1e30, ALU.add, ALU.mult))
                yield from step(eng.tensor_tensor(self.m1[:].rearrange("p q (g k) -> p q g k", g=G), self.m1[:].rearrange("p q (g k) -> p q g k", g=G),
                                       every(self.gcnt[:]), ALU.add))
                yield from rank_below(step, eng, self.m1[:], self.g16[:], self.e16[:], self.tri16, self.cnt[:], self.sel[:], CT, E, 4)
                yield from step(eng.tensor_tensor(self.sel[:], self.sel[:], self.score[:], ALU.mult))
                yield from step(eng.tensor_reduce(self.total[:], self.sel[:], AX, ALU.add))
                yield from step(eng.tensor_scalar(self.total[:], self.total[:], 1e-20, None, ALU.add))
                yield from step(eng.reciprocal(self.total[:], self.total[:]))
                yield from step(eng.tensor_tensor(self.cw[:], self.sel[:], self.total[:].unsqueeze(2).broadcast_to([P, CT, E]), ALU.mult))
                eng.memset(spare[:], 0.0).then_inc(self.cw_done, 1)
                assert k == self.STEPS

            def after(self, eng, c, m):
                if m == -1:
                    if isinstance(c, int) and c == 0:
                        eng.wait_ge(self.tl_done, 1)
                        for _ in self.route(eng, 0):
                            pass
                        eng.wait_ge(self.tl_done, NC)
                    self.next = self.route(eng, c + 1)
                if m > 4:
                    for _ in range(5):
                        next(self.next, None)

        class ZoneRoute:
            E = 8
            CENTER = math.exp(-1.0)
            LOWER, UPPER = 0.5 - math.log(4.0 / 3.0), 0.5
            STEPS = 23

            def __init__(self, n, R, W, pairs, tl, cw):
                self.n, self.tl, self.cw = n, tl, cw
                E = self.E
                self.temp = W(n + "temp", [P, 1])
                self.half = R(n + "half", [P, 1])
                self.scale = self.half[0:E, 0:1]
                self.tri8 = W(n + "tri8", [P, E, E])
                self.inh, self.zone, self.low, self.dist, self.w, self.fb = (R(n + k, [P, NT, E]) for k in ("inh", "zone", "low", "dist", "w", "fb"))
                self.g8, self.e8 = (R(n + k, [P, CT, E, E]) for k in ("g8", "e8"))
                self.cnt, self.sel, self.dif, self.wc, self.fbc = (R(n + k, [P, CT, E]) for k in ("cnt", "sel", "dif", "wc", "fbc"))
                self.total, self.none = R(n + "total", [P, CT]), R(n + "none", [P, CT])
                pairs += [(self.temp[:], d[n + "temp"]), (self.tri8[:], d["tri8"])]
                self.half_done = sem(n + "half_done")

            def first(self):
                def dve_half(eng):
                    eng.reciprocal(self.half[:], self.temp[:]).then_inc(self.half_done, 1)
                    eng.wait_ge(self.half_done, 1)
                    eng.tensor_scalar(self.half[:], self.half[:], 0.5, None, ALU.mult).then_inc(self.half_done, 1)
                parts["vector"].append(dve_half)
                parts["scalar"].append(lambda eng: eng.wait_ge(self.half_done, 2))

            def then(self, tl_done, cw_done):
                self.cw_done = cw_done
                zone_steps = sem(self.n + "zone_steps")
                exps_done = sem(self.n + "exps_done")
                self.exps_done = exps_done
                self.route_steps = sem(self.n + "route_steps")

                def dve_zone(eng):
                    eng.wait_ge(tl_done, NC)
                    eng.tensor_scalar(self.inh[:], self.tl[:], 0.5, 0.5, ALU.mult, ALU.add).then_inc(zone_steps, 1)
                    eng.wait_ge(zone_steps, 1)
                    eng.tensor_scalar(self.low[:], self.inh[:], self.LOWER, None, ALU.is_ge).then_inc(zone_steps, 1)
                    eng.tensor_scalar(self.dist[:], self.inh[:], self.CENTER, None, ALU.subtract).then_inc(zone_steps, 1)
                    eng.wait_ge(zone_steps, 3)
                    eng.scalar_tensor_tensor(out=self.zone[:], in0=self.inh[:], scalar=self.UPPER, in1=self.low[:], op0=ALU.is_le, op1=ALU.mult).then_inc(zone_steps, 1)
                    eng.scalar_tensor_tensor(out=self.dist[:], in0=self.dist[:], scalar=-1.0, in1=self.dist[:], op0=ALU.mult, op1=ALU.max).then_inc(zone_steps, 1)
                parts["vector"].append(dve_zone)

                def act_exps(eng):
                    eng.wait_ge(zone_steps, 5)
                    eng.activation(self.w[:], self.dist[:], ACT.Exp, scale=-1 / 0.1).then_inc(exps_done, 1)
                    eng.activation(self.fb[:], self.dist[:], ACT.Exp, scale=-1 / 0.3).then_inc(exps_done, 1)
                parts["scalar"].append(act_exps)

            def route(self, eng, c):
                E = self.E
                k = 0

                def step(ins):
                    nonlocal k
                    k += 1
                    ins.then_inc(self.route_steps, 1)
                    eng.wait_ge(self.route_steps, c * self.STEPS + k)
                    yield
                every = lambda t: t.unsqueeze(2).broadcast_to([P, CT, E])
                tiles = bass.ds(CT * (c % NC), CT)
                w, fb, total, none, sel = self.wc[:], self.fbc[:], self.total[:], self.none[:], self.sel[:]
                yield from step(eng.tensor_copy(fb, self.fb[:, tiles, :]))
                yield from step(eng.tensor_tensor(w, self.w[:, tiles, :], self.zone[:, tiles, :], ALU.mult))
                yield from rank_below(step, eng, fb, self.g8[:], self.e8[:], self.tri8, self.cnt[:], sel, CT, E, 2)
                yield from step(eng.tensor_tensor(sel, sel, fb, ALU.mult))
                yield from step(eng.tensor_reduce(total, sel, AX, ALU.add))
                yield from step(eng.tensor_scalar(total, total, 1e-8, None, ALU.max))
                yield from step(eng.reciprocal(total, total))
                yield from step(eng.tensor_tensor(sel, sel, every(total), ALU.mult))
                yield from step(eng.tensor_reduce(total, w, AX, ALU.add))
                yield from step(eng.tensor_scalar(none, total, 1e-8, None, ALU.is_lt))
                yield from step(eng.tensor_tensor(self.dif[:], sel, every(none), ALU.mult))
                yield from step(eng.tensor_scalar(none, none, -1.0, 1.0, ALU.mult, ALU.add))
                yield from step(eng.tensor_tensor(sel, w, every(none), ALU.mult))
                yield from step(eng.tensor_tensor(sel, sel, self.dif[:], ALU.add))
                yield from step(eng.tensor_reduce(total, sel, AX, ALU.add))
                yield from step(eng.tensor_scalar(total, total, 1e-8, None, ALU.max))
                yield from step(eng.reciprocal(total, total))
                yield from step(eng.tensor_tensor(self.cw[:], sel, every(total), ALU.mult))
                eng.memset(spare[:], 0.0).then_inc(self.cw_done, 1)
                assert k == self.STEPS, k

            def after(self, eng, c, m):
                if m == -1:
                    if isinstance(c, int) and c == 0:
                        eng.wait_ge(self.exps_done, 2)
                        for _ in self.route(eng, 0):
                            pass
                    self.next = self.route(eng, c + 1)
                if m >= 1:
                    for _ in range(2):
                        next(self.next, None)

        def gate_attention(n):
            R = Region(start, region_end(n))
            RW = Region(*weights_at[n])
            lnx = R(n + "lnx", [P, NT, D])
            lnT = R(n + "lnT", [P, KT, NC * CN])
            W = RW(n + "W", [P, KT, D])
            Ws = RW(n + "Ws", [P, KT, D])
            bcol = RW(n + "bcol", [P, KT])
            wide = RW(n + "wide", [P, KT, 63])
            cB = RW(n + "cB", [P, 2, KT, P])
            bc = RW(n + "bc", [P, 2])
            qm = RW(n + "qm", [P, B, S2], I32)
            txt = R(n + "txt", [P, KT, B * S2])
            ctab = R(n + "ctab", [P, 2, B * S2])
            madd = R(n + "madd", [P, B, S2])
            fT = [R(n + f"fT{b}", [P, KT, S]) for b in range(B)]
            RING = 8
            ring = [R(n + f"ring{i}", [P, S]) for i in range(RING)]
            rhoT = R(n + "rhoT", [96, S])
            rho = R(n + "rho", [P, TB, S2])
            prod = R(n + "prod", [P, TB, S2])
            mx, sm, rs = (R(n + k, [P, TB]) for k in ("mx", "sm", "rs"))
            g = R(n + "g", [P, 2, TB])
            loads(n, [(W[:], d[n + "W"]), (Ws[:], d[n + "Ws"]), (bcol[:], d[n + "b"]), (wide[:], d[n + "wide"]),
                      (cB[:], d[n + "cB"]), (bc[:], d[n + "bc"]), (qm[:], d[n + "qm"])])
            parts["sync"].append(lambda eng: load_weights_after(n, eng))
            await_weights(n)
            tab_ready = sem(n + "tab_ready")
            tab_steps = sem(n + "tab_steps")

            def pe_tables(eng):
                for e in range(KT):
                    for kt in range(KT):
                        ins = eng.matmul(bank(e, 0, B * S2), Ws[:, kt, P * e:P * e + P], ctxT[:, kt, :], start=kt == 0, stop=kt == KT - 1)
                    ins.then_inc(tab_ready, 1)
                for e in range(2):
                    for kt in range(KT):
                        ins = eng.matmul(bank(2 + e, 0, B * S2), cB[:, e, kt, :], ctxT[:, kt, :], start=kt == 0, stop=kt == KT - 1)
                    ins.then_inc(tab_ready, 1)
            parts["tensor"].append(pe_tables)

            def dve_tables(eng):
                for e in range(KT):
                    eng.wait_ge(tab_ready, e + 1)
                    eng.tensor_scalar(txt[:, e, :], bank(e, 0, B * S2), bcol[:, e:e + 1], None, ALU.add).then_inc(tab_steps, 1)
                for e in range(2):
                    eng.wait_ge(tab_ready, 3 + e)
                    eng.tensor_copy(ctab[:, e, :], bank(2 + e, 0, B * S2)).then_inc(tab_steps, 1)
                eng.tensor_scalar(madd[:], qm[:], 1.0, 1e30, ALU.subtract, ALU.mult).then_inc(tab_steps, 1)
            normalise(n, lnx, lnT, dve_meanwhile=dve_tables)
            f_ready = sem(n + "f_ready")
            f_taken = sem(n + "f_taken")
            tanh_done = sem(n + "tanh_done")
            rho_added = sem(n + "rho_added")
            rhoT_taken = sem(n + "rhoT_taken")
            rho_ready = sem(n + "rho_ready")
            soft = sem(n + "soft")
            exp_done = sem(n + "exp_done")
            gates_done = sem(n + "gates_done")
            order = [(t, e) for r in range(32) for e in range(KT) for t in (r, r + 32, r + 64) if t < S2]
            n_ord = len(order)

            RHO_BANK = (0, 2)
            NEXT_F = 24
            TURN, EXP, GATES = 16, 24, (36, 44)
            last_of = [31, 63, S2 - 1]
            SOFT = 8

            def pe_gate(eng):
                def features(b):
                    for k in range(4):
                        e, half = k // 2, k % 2
                        for kt in range(KT):
                            c = b * S + half * CN
                            ins = eng.matmul(bank(2 + k), W[:, kt, P * e:P * e + P], lnT[:, kt, c:c + CN], start=kt == 0, stop=kt == KT - 1)
                        ins.then_inc(f_ready, 1)

                def turn(b):
                    eng.wait_ge(rhoT_taken, 2 * b + 2)
                    for j in range(TB):
                        ins = eng.transpose(bank(6 + j // 4, S2 * (j % 4), S2), rhoT[0:S2, P * j:P * j + P], ident[0:S2, 0:S2])
                    ins.then_inc(rho_ready, 1)
                features(0)
                for b in range(B):
                    for k, (t, e) in enumerate(order):
                        if b == 0 and k == NEXT_F:
                            eng.wait_ge(f_taken, 4)
                            features(1)
                        if b == 1 and k == 0:
                            eng.wait_ge(f_taken, 8)
                        if b == 1 and k == TURN:
                            turn(0)
                        eng.wait_ge(tanh_done, n_ord * b + k + 1)
                        q, r = t // 32, t % 32
                        for half in range(2):
                            ins = eng.matmul(bank(RHO_BANK[b] + half)[32 * q:32 * q + 32], wide[:, e, 31 - r:63 - r],
                                             ring[(n_ord * b + k) % RING][:, half * CN:(half + 1) * CN],
                                             start=r == 0 and e == 0, stop=(t, e) == (last_of[q], KT - 1))
                        ins.then_inc(rho_added, 1)
                eng.wait_ge(soft, 1)
                turn(1)
            parts["tensor"].append(pe_gate)

            def act_gate(eng):
                def take_features(b):
                    for k in range(4):
                        eng.wait_ge(f_ready, 4 * b + k + 1)
                        eng.activation(fT[b][:, k // 2, (k % 2) * CN:(k % 2 + 1) * CN], bank(2 + k), ACT.Copy).then_inc(f_taken, 1)

                def exps(b):
                    eng.wait_ge(soft, SOFT * b + 3)
                    eng.activation(rho[:], rho[:], ACT.Exp).then_inc(exp_done, 1)

                def gate(b, i):
                    eng.wait_ge(soft, SOFT * b + 7 + i)
                    eng.activation(g[:, i, :], g[:, i, :], ACT.Tanh, bias=bc[:, i:i + 1]).then_inc(gates_done, 1)
                take_features(0)
                for b in range(B):
                    for k, (t, e) in enumerate(order):
                        if b == 0 and k == NEXT_F + 8:
                            take_features(1)
                        if b == 1 and k == EXP:
                            exps(0)
                        if b == 1 and k in GATES:
                            gate(0, GATES.index(k))
                        if b or k >= RING:
                            eng.wait_ge(rho_added, n_ord * b + k - RING + 1)
                        if k == 0:
                            eng.wait_ge(f_taken, 4 * b + 4)
                            eng.wait_ge(tab_steps, 5)
                        c = b * S2 + t
                        eng.activation(ring[(n_ord * b + k) % RING][:], fT[b][:, e, :], ACT.Tanh, bias=txt[:, e, c:c + 1]).then_inc(tanh_done, 1)
                exps(1)
                for i in range(2):
                    gate(1, i)
            parts["scalar"].append(act_gate)

            def dve_gate(eng):
                for b in range(B):
                    eng.wait_ge(rho_added, n_ord * (b + 1))
                    for half in range(2):
                        if b:
                            eng.wait_ge(rho_ready, b)
                        eng.tensor_copy(rhoT[:, half * CN:(half + 1) * CN], bank(RHO_BANK[b] + half)[0:96]).then_inc(rhoT_taken, 1)
                    eng.wait_ge(rho_ready, b + 1)
                    for k in range(2):
                        ins = eng.tensor_tensor(rho[:, 4 * k:4 * k + 4, :], bank(6 + k, 0, 4 * S2).rearrange("p (j t) -> p j t", t=S2),
                                                madd[:, bass.ds(b, 1), :].broadcast_to([P, 4, S2]), ALU.add)
                    ins.then_inc(soft, 1)
                    eng.wait_ge(soft, SOFT * b + 1)
                    eng.tensor_reduce(mx[:], rho[:], AX, ALU.max).then_inc(soft, 1)
                    eng.wait_ge(soft, SOFT * b + 2)
                    eng.tensor_tensor(rho[:], rho[:], mx[:].unsqueeze(2).broadcast_to([P, TB, S2]), ALU.subtract).then_inc(soft, 1)
                    eng.wait_ge(exp_done, b + 1)
                    eng.tensor_reduce(sm[:], rho[:], AX, ALU.add).then_inc(soft, 1)
                    eng.wait_ge(soft, SOFT * b + 4)
                    eng.reciprocal(rs[:], sm[:]).then_inc(soft, 1)
                    for i in range(2):
                        if i:
                            eng.wait_ge(dots, 4 * b + 2)
                        eng.tensor_tensor(prod[:], rho[:], ctab[:, i, bass.ds(b * S2, S2)].unsqueeze(1).broadcast_to([P, TB, S2]), ALU.mult).then_inc(dots, 1)
                        eng.wait_ge(dots, 4 * b + 2 * i + 1)
                        eng.tensor_reduce(g[:, i, :], prod[:], AX, ALU.add).then_inc(dots, 1)
                    eng.wait_ge(dots, 4 * b + 4)
                    eng.wait_ge(soft, SOFT * b + 5)
                    eng.memset(spare[:], 0.0).then_inc(soft, 1)
                    eng.tensor_tensor(g[:, 0, :], g[:, 0, :], rs[:], ALU.mult).then_inc(soft, 1)
                    eng.tensor_tensor(g[:, 1, :], g[:, 1, :], rs[:], ALU.mult).then_inc(soft, 1)
                    eng.wait_ge(gates_done, 2 * b + 2)
                    for j in range(TB):
                        xt = x[:, bass.ds(TB * b + j, 1), :].rearrange("p a n -> p (a n)")
                        eng.scalar_tensor_tensor(out=xt, in0=lnx[:, bass.ds(TB * b + j, 1), :].rearrange("p a n -> p (a n)"), scalar=g[:, 0, j:j + 1],
                                                 in1=xt, op0=ALU.mult, op1=ALU.add).then_inc(scaled, 1)
                    for j in range(TB):
                        xt = x[:, bass.ds(TB * b + j, 1), :].rearrange("p a n -> p (a n)")
                        eng.wait_ge(scaled, TB * b + j + 1)
                        ins = eng.tensor_scalar(xt, xt, g[:, 1, j:j + 1], None, ALU.add)
                    ins.then_inc(gated, 1)
                    if statistics_wanted(n):
                        eng.wait_ge(gated, b + 1)
                        for j in range(TB):
                            statistics(eng, TB * b + j)
            dots = sem(n + "dots")
            scaled = sem(n + "scaled")
            gated = sem(n + "gated")
            parts["vector"].append(dve_gate)
            barrier()

        def quantised(n):
            NF = NF3
            R = Region(start, region_end(n))
            W = Region(W3.at, weights_at[n][1])
            lnx = R(n + "lnx", [P, NT, D])
            b1 = W(n + "b1", [P, NF])
            b2 = W(n + "b2", [P, KT])
            q1 = R(n + "q1", [P, NF, D], BF16)
            q2 = R(n + "q2", [P, KT, NF * P], BF16)
            q1T = R(n + "q1T", [P, KT, NF * P], BF16)
            q2T = R(n + "q2T", [P, NF, D], BF16)
            qx = [R(n + f"qx{i}", [P, CT, D]) for i in range(3)]
            qxb = R(n + "qxb", [P, NT, D], BF16)
            qxT = R(n + "qxT", [P, KT, NC * CN], BF16)
            h = R(n + "h", [P, NF, NC * CN])
            hq = [R(n + f"hq{i}", [P, 2, CN]) for i in range(2)]
            qh = [R(n + f"qh{i}", [P, 2, CN], BF16) for i in range(4)]
            sc1, bi1, bi2 = R(n + "sc1", [P, NF]), R(n + "bi1", [P, NF]), R(n + "bi2", [P, KT])
            row = R(n + "row", [P, 2, D])
            diag = R(n + "diag", [P, 2, KT, P])
            mxx, mall, sx, ix = (R(n + k, [P, w]) for k, w in (("mxx", 1), ("mall", 2), ("sx", 2), ("ix", 2)))
            mh, mh1 = R(n + "mh", [P, NC * NF]), R(n + "mh1", [P, 1])
            tmp = R(n + "tmp", [P, NF])
            loads(n, [(w1[:], d[n + "w1"]), (w2[:], d[n + "w2"]), (b1[:], d[n + "b1"]), (b2[:], d[n + "b2"])])
            await_weights(n)
            c0 = normalise(n, lnx)
            st = sem(n + "st")
            maxed = sem(n + "maxed")
            wT_ready = sem(n + "wT_ready")
            wT_taken = sem(n + "wT_taken")
            qx_done = sem(n + "qx_done")
            qxT_ready = sem(n + "qxT_ready")
            qxT_taken = sem(n + "qxT_taken")
            p1_ready = sem(n + "p1_ready")
            h_done = sem(n + "h_done")
            h_maxed = sem(n + "h_maxed")
            hq_steps = sem(n + "hq_steps")
            qh_done = sem(n + "qh_done")
            qh_used = sem(n + "qh_used")
            row_ready = sem(n + "row_ready")
            out_ready = sem(n + "out_ready")
            qsteps = sem(n + "qsteps")
            qround = sem(n + "qround")
            w_scaled = sem(n + "w_scaled")
            wq_done = sem(n + "wq_done")
            x_biased = sem(n + "x_biased")
            ot_done = sem(n + "ot_done")
            osteps = sem(n + "osteps")

            def dve_scales(eng):
                k = 0

                def step(ins):
                    nonlocal k
                    k += 1
                    ins.then_inc(st, 1)
                    eng.wait_ge(st, k)
                eng.wait_ge(ln_done, c0 + NC)
                step(eng.tensor_reduce(mxx[:], lnx[:].rearrange("p t n -> p (t n)"), AX, ALU.max))
                for k2, (s, i) in enumerate(((s1, i1), (s2, i2))):
                    if not ahead:
                        extremes(eng, 2 * k2)
                        extremes(eng, 2 * k2 + 1)
                    eng.wait_ge(extremes_taken, 2 * k2 + 2)
                    step(eng.scalar_tensor_tensor(out=s[:], in0=i[:], scalar=-1.0, in1=s[:], op0=ALU.mult, op1=ALU.max))
                    step(eng.tensor_scalar(s[:], s[:], 1e-8, 1.0 / 127.0, ALU.max, ALU.mult))
                    step(eng.reciprocal(i[:], s[:]))
                eng.wait_ge(maxed, 1)
                step(eng.tensor_scalar(sx[:, 0:1], mall[:, 0:1], 1e-8, 1.0 / 255.0, ALU.max, ALU.mult))
                step(eng.reciprocal(ix[:, 0:1], sx[:, 0:1]))
            N_WEIGHT = 3
            N_IX = 1 + 2 * N_WEIGHT + 2
            N_ALL = N_IX + 6
            parts["vector"].append(dve_scales)

            def pool_max(eng):
                eng.wait_ge(st, 1)
                eng.partition_all_reduce(mall[:, 0:1], mxx[:], P, bass.bass_isa.ReduceOp.max).then_inc(maxed, 1)
            parts["gpsimd"].append(pool_max)

            def act_weights(eng):
                for k, (w, i, nt) in enumerate(((w1, i1, NF), (w2, i2, KT))):
                    eng.wait_ge(st, 1 + N_WEIGHT * (k + 1))
                    for t in range(nt):
                        ins = eng.activation(w[:, t, :], w[:, t, :], ACT.Identity, bias=rounder[:], scale=i[:, t:t + 1])
                    ins.then_inc(w_scaled, 1)
            parts["scalar"].append(act_weights)

            def dve_qx(eng):
                for t in range(NC + 2):
                    if t in (2, 3):
                        w, qf = ((w1, q1), (w2, q2))[t - 2]
                        eng.wait_ge(w_scaled, t - 1)
                        eng.tensor_scalar(qf[:], w[:], ROUND, None, ALU.subtract).then_inc(wq_done, 1)
                    if t < NC:
                        if t >= 3:
                            eng.wait_ge(qx_done, t - 2)
                        eng.tensor_scalar(qx[t % 3][:], lnx[:, CT * t:CT * (t + 1), :], ix[:, 0:1], 0.0, ALU.mult, ALU.max).then_inc(qsteps, 1)
                    if 0 <= t - 2:
                        c = t - 2
                        eng.wait_ge(qround, c + 1)
                        eng.tensor_scalar(qxb[:, CT * c:CT * (c + 1), :], qx[c % 3][:], ROUND, None, ALU.subtract).then_inc(qx_done, 1)
                    if 0 <= t - 1 < NC:
                        c = t - 1
                        eng.wait_ge(qsteps, c + 1)
                        eng.tensor_scalar(qx[c % 3][:], qx[c % 3][:], 255.0, ROUND, ALU.min, ALU.add).then_inc(qround, 1)
                k = N_IX

                def step(ins):
                    nonlocal k
                    k += 1
                    ins.then_inc(st, 1)
                    eng.wait_ge(st, k)
                step(eng.tensor_scalar(sc1[:], s1[:], sx[:, 0:1], None, ALU.mult))
                step(eng.reciprocal(tmp[:], sc1[:]))
                step(eng.tensor_tensor(tmp[:], tmp[:], b1[:], ALU.mult))
                step(eng.tensor_scalar(tmp[:], tmp[:], ROUND, None, ALU.add))
                step(eng.tensor_scalar(tmp[:], tmp[:], ROUND, None, ALU.subtract))
                step(eng.tensor_tensor(bi1[:], tmp[:], sc1[:], ALU.mult))
            parts["vector"].append(dve_qx)

            def bankb(i, a, w):
                return bank(i)[:, a // 2:(a + w) // 2].bitcast(BF16)

            def pe_wT(eng):
                eng.wait_ge(wq_done, 1)
                for kt in range(KT):
                    for f in range(NF):
                        ins = eng.transpose(bankb(kt, P * f, P), q1[:, f, P * kt:P * kt + P], identb[:])
                    ins.then_inc(wT_ready, 1)
            parts["tensor"].append(pe_wT)


            def act_wT(eng):
                for i in range(2):
                    eng.wait_ge(wT_ready, i + 1)
                    eng.activation(q1T[:, i, :], bankb(i, 0, 1024), ACT.Copy).then_inc(wT_taken, 1)
            parts["scalar"].append(act_wT)

            def act_wT2(eng):
                for i in range(2):
                    eng.wait_ge(wT_ready, 3 + i)
                    eng.activation(q2T[:, 4 * i:4 * (i + 1), :].rearrange("p f n -> p (f n)"), bankb(2 + i, 0, 1024), ACT.Copy).then_inc(wT_taken, 1)

            def pe_qxT(eng):
                for c in range(NC):
                    eng.wait_ge(qx_done, c + 1)
                    if c >= 2:
                        eng.wait_ge(qxT_taken, 2 * (c - 1))
                    for kt in range(KT):
                        for q in range(CT):
                            ins = eng.transpose(bankb(4 + 2 * (c % 2) + kt, P * q, P), qxb[:, CT * c + q, P * kt:P * kt + P], identb[:])
                        ins.then_inc(qxT_ready, 1)
            parts["tensor"].append(pe_qxT)

            def pe_wT2(eng):
                eng.wait_ge(wq_done, 2)
                for half in range(2):
                    for f4 in range(4):
                        f = 4 * half + f4
                        for kt in range(KT):
                            ins = eng.transpose(bankb(2 + half, D * f4 + P * kt, P), q2[:, kt, P * f:P * f + P], identb[:])
                    ins.then_inc(wT_ready, 1)
                eng.wait_ge(qxT_taken, 2 * NC)
                eng.wait_ge(wT_taken, 4)
            parts["tensor"].append(pe_wT2)

            def act_qxT(eng):
                for c in range(NC):
                    for kt in range(KT):
                        eng.wait_ge(qxT_ready, 2 * c + kt + 1)
                        eng.activation(qxT[:, kt, CN * c:CN * (c + 1)], bankb(4 + 2 * (c % 2) + kt, 0, CN), ACT.Copy).then_inc(qxT_taken, 1)
            parts["scalar"].append(act_qxT)
            parts["scalar"].append(act_wT2)

            def dve_open(eng):
                eng.memset(spare[:], 0.0).then_inc(qh_done, 2)
            parts["vector"].append(dve_open)

            def pe_p1(eng):
                def body(c):
                    for f in range(NF):
                        if not first(c):
                            eng.wait_ge(h_done, NF * (c - 1) + f + 1)
                        for kt in range(KT):
                            ins = eng.matmul(bank(f), q1T[:, kt, P * f:P * f + P], qxT[:, kt, bass.ds(CN * c, CN)], start=kt == 0, stop=kt == KT - 1)
                        ins.then_inc(p1_ready, 1)
                chunks(eng, body)
            parts["tensor"].append(pe_p1)

            def act_p1(eng):
                eng.wait_ge(st, N_ALL)
                with eng.Fori(0, NC) as c:
                    for f in range(NF):
                        eng.wait_ge(p1_ready, NF * c + f + 1)
                        eng.activation(h[:, f, bass.ds(CN * c, CN)], bank(f), ACT.Relu, bias=bi1[:, f:f + 1], scale=sc1[:, f:f + 1]).then_inc(h_done, 1)
            parts["scalar"].append(act_p1)

            def dve_p1(eng):
                with eng.Fori(0, NC) as c:
                    for f in range(NF):
                        eng.wait_ge(h_done, NF * c + f + 1)
                        eng.tensor_reduce(mh[:, bass.ds(NF * c + f, 1)], h[:, f, bass.ds(CN * c, CN)], AX, ALU.max).then_inc(h_maxed, 1)
                k = N_ALL

                def step(ins):
                    nonlocal k
                    k += 1
                    ins.then_inc(st, 1)
                    eng.wait_ge(st, k)
                eng.wait_ge(h_maxed, NF * NC)
                step(eng.tensor_reduce(mh1[:], mh[:], AX, ALU.max))
                eng.wait_ge(maxed, 2)
                step(eng.tensor_scalar(sx[:, 1:2], mall[:, 1:2], 1e-8, 1.0 / 255.0, ALU.max, ALU.mult))
                step(eng.reciprocal(ix[:, 1:2], sx[:, 1:2]))
                step(eng.tensor_scalar(s2[:], s2[:], sx[:, 1:2], None, ALU.mult))
                step(eng.reciprocal(i2[:], s2[:]))
                step(eng.tensor_tensor(bi2[:], i2[:], b2[:], ALU.mult))
                step(eng.tensor_scalar(bi2[:], bi2[:], ROUND, None, ALU.add))
                step(eng.tensor_scalar(bi2[:], bi2[:], ROUND, None, ALU.subtract))
                step(eng.tensor_tensor(bi2[:], bi2[:], s2[:], ALU.mult))
                for kt in range(KT):
                    eng.tensor_scalar(diag[:, 0, kt, :], ident[:], s2[:, kt:kt + 1], None, ALU.mult)
                    ins = eng.tensor_scalar(diag[:, 1, kt, :], ident[:], bi2[:, kt:kt + 1], None, ALU.mult)
                step(ins)
            parts["vector"].append(dve_p1)

            def pool_max2(eng):
                eng.wait_ge(st, N_ALL + 1)
                eng.partition_all_reduce(mall[:, 1:2], mh1[:], P, bass.bass_isa.ReduceOp.max).then_inc(maxed, 1)
            parts["gpsimd"].append(pool_max2)

            def pe_row(eng):
                eng.wait_ge(st, N_ALL + 10)
                eng.wait_ge(h_done, NF * NC)
                for i in range(2):
                    for kt in range(KT):
                        ins = eng.matmul(bank(6, D * i + P * kt, P), ones[:], diag[:, i, kt, :], start=True, stop=True)
                ins.then_inc(row_ready, 1)
            parts["tensor"].append(pe_row)
            parts["scalar"].append(lambda eng: (eng.wait_ge(row_ready, 1), eng.activation(row[:].rearrange("p i n -> p (i n)"), bank(6), ACT.Copy).then_inc(row_ready, 1)))

            NP = NF // 2

            def act_p2(eng):
                eng.wait_ge(st, N_ALL + 3)
                with eng.Fori(0, NC) as c:
                    for f2 in range(NP):
                        eng.wait_ge(qh_done, NP * c + f2 + 1)
                        eng.activation(hq[f2 % 2][:], h[:, 2 * f2:2 * f2 + 2, bass.ds(CN * c, CN)], ACT.Identity, bias=rounder[:], scale=ix[:, 1:2]).then_inc(hq_steps, 1)
            parts["scalar"].append(act_p2)

            def pool_p2(eng):
                eng.wait_ge(row_ready, 2)
                for c in range(NC):
                    xt = x[:, CT * c:CT * (c + 1), :]
                    eng.tensor_tensor(xt, xt, row[:, 1:2, :].broadcast_to([P, CT, D]), ALU.add).then_inc(x_biased, 1)
            parts["gpsimd"].append(pool_p2)

            def dve_p2(eng):
                eng.wait_ge(row_ready, 2)

                def add(c):
                    eng.wait_ge(qh_used, NP * (c + 1))
                    for k in range(2):
                        o = bank(2 * k).rearrange("p (a n) -> p a n", a=2)
                        eng.tensor_tensor(ot[:, 2 * k:2 * k + 2, :], o, row[:, 0:1, :].broadcast_to([P, 2, D]), ALU.mult).then_inc(ot_done, 1)
                    eng.wait_ge(ot_done, 2 * c + 2)
                    eng.wait_ge(x_biased, c + 1)
                    xt = x[:, CT * c:CT * (c + 1), :]
                    eng.tensor_tensor(xt, xt, ot[:], ALU.add).then_inc(osteps, 1)
                for c in range(NC):
                    for f2 in range(NP):
                        k = NP * c + f2
                        eng.wait_ge(hq_steps, k + 1)
                        if k >= 4:
                            eng.wait_ge(qh_used, k - 3)
                        eng.tensor_scalar(qh[k % 4][:], hq[k % 2][:], ROUND, None, ALU.subtract).then_inc(qh_done, 1)
                        if f2 == 0 and c >= 1:
                            add(c - 1)
                add(NC - 1)
            ot = R(n + "ot", [P, CT, D])
            parts["vector"].append(dve_p2)

            def sp_store(eng):
                for c in range(NC):
                    b, j = CT * c // TB, CT * c % TB
                    eng.wait_ge(osteps, c + 1)
                    eng.dma_start(d["out"][b].rearrange("(p j) n -> p j n", p=P)[:, j:j + CT, :], x[:, CT * c:CT * (c + 1), :]).then_inc(stored, 16)
            parts["sync"].append(sp_store)

            def pe_p2(eng):
                with eng.Fori(0, NC) as c:
                    for f2 in range(NP):
                        eng.wait_ge(qh_done, NP * c + f2 + 3)
                        for a in range(2):
                            f = 2 * f2 + a
                            for q in range(CT):
                                ins = eng.matmul(bank(2 * (q // 2), D * (q % 2), D), qh[f2 % 4][:, a, P * q:P * q + P], q2T[:, f, :],
                                                 start=f == 0 and q % 2 == 0, stop=f == NF - 1, skip_group_check=True)
                        ins.then_inc(qh_used, 1)
                    eng.wait_ge(ot_done, 2 * c + 2)
            parts["tensor"].append(pe_p2)
            barrier()

        LAYERS = [lambda: attention(Attention("a0_", 1024, True, True, -1e30, False)),
                  lambda: feed_forward("f0_", 12, first_routed=4, experts=16, route=GroupRoute),
                  lambda: attention(Attention("a1_", 1024, False, False, None, True)),
                  lambda: feed_forward("f1_", 8, gated=False, biased=True),
                  lambda: gate_attention("a2_"),
                  lambda: feed_forward("f2_", 16, first_routed=0, per_weight=2, experts=8, route=ZoneRoute),
                  lambda: attention(Attention("a3_", 256, True, False, -1e15, True)),
                  lambda: quantised("f3_")]
        for i, make in enumerate(LAYERS):
            if make and i in only:
                make()

        def store_x(eng):
            if order_of_layers[-1] == "f3_":
                eng.wait_ge(stored, 16 * NC)
                return
            for b in range(B):
                eng.dma_start(d["out"][b].rearrange("(p j) n -> p j n", p=P), x[:, TB * b:TB * (b + 1), :]).then_inc(stored, 16)
            eng.wait_ge(stored, 16 * B)
        parts["sync"].append(store_x)

        block = ctx.enter_context(nc.Block())

        @block.sync
        def _(eng):
            for part in parts["sync"]:
                part(eng)

        @block.tensor
        def _(eng):
            for part in parts["tensor"]:
                part(eng)

        @block.scalar
        def _(eng):
            for part in parts["scalar"]:
                part(eng)

        @block.vector
        def _(eng):
            for part in parts["vector"]:
                part(eng)

        @block.gpsimd
        def _(eng):
            for part in parts["gpsimd"]:
                part(eng)


def layouts(v):
    import numpy as np
    v = {k: np.asarray(a) for k, a in v.items()}
    rows = lambda a: np.ascontiguousarray(a.reshape(-1, P, a.shape[-1]).transpose(1, 0, 2))
    col = lambda a: np.ascontiguousarray(a.reshape(-1, P).T)
    every = lambda a: np.ascontiguousarray(np.broadcast_to(a, (P,) + a.shape))
    o = {"x": v["x"], "fside": v["fside_Bx16xSxS2_0"], "mask16": v["mask_Bx16xSxS2_bk1"], "mask1": v["mask_Bx1xSxS2_bk1"],
         "ident": np.eye(P, dtype=np.float32),
         "ctxT": rows(v["ctx_1024"].reshape(B * S2, D).T)}
    for n, l in (("a0_", "L0_xattn_"), ("a1_", "L1_xattn_"), ("a3_", "L3_xattn_")):
        w = {k: v[l + k] for k in ("Wq", "Wk", "Wv", "Wo")}
        dims = w["Wo"].size // D
        o[n + "WqT"] = rows(w["Wq"].reshape(D, dims).T)
        o[n + "Wk"] = rows(w["Wk"].reshape(D, dims))
        o[n + "Wv"] = rows(w["Wv"].reshape(D, dims))
        o[n + "Wo"] = rows(w["Wo"].reshape(dims, D))
        hd = dims // H
        o[n + "group"] = np.kron(np.eye(P // hd), np.ones((hd, 1))).astype(np.float32)
        if l + "bq" in v:
            o[n + "bk"], o[n + "bv"] = col(v[l + "bk"]), col(v[l + "bv"])
            o[n + "bq"] = col(v[l + "bq"])
            o[n + "bo2"] = np.ascontiguousarray(np.broadcast_to(v[l + "bo"], (1, B, D)))
    inner = lambda a: a.transpose(1, 0, 2).reshape(D, -1)
    o["f0_wg"] = rows(np.concatenate([v["L0_ffn_shared_gate_w"].T, inner(v["L0_ffn_gate_w"])], 1))
    o["f0_wu"] = rows(np.concatenate([v["L0_ffn_shared_up_w"].T, inner(v["L0_ffn_up_w"])], 1))
    o["f0_wd"] = rows(np.concatenate([v["L0_ffn_shared_down_w"].T, v["L0_ffn_down_w"].reshape(-1, D)], 0))
    wide_router = lambda a: rows(np.concatenate([a, np.zeros((D, P - a.shape[1]), a.dtype)], 1))
    o["f0_wr"] = wide_router(v["L0_ffn_router_w"].T)
    o["f0_bias"] = every(v["L0_ffn_correction_bias"])
    o["f0_sel"] = np.kron(np.eye(16), np.ones((1, 64))).reshape(16, 8, P).astype(np.float32)
    o["f1_wg"], o["f1_wd"] = rows(v["L1_ffn_W1"]), rows(v["L1_ffn_W2"])
    o["f1_b1"], o["f1_b2"] = col(v["L1_ffn_b1"]), every(v["L1_ffn_b2"])
    o["a2_W"], o["a2_Ws"], o["a2_b"] = rows(v["L2_xattn_W"]), rows(v["L2_xattn_Ws"]), col(v["L2_xattn_b"].reshape(-1))
    wide = np.zeros((P, KT, 63), np.float32)
    wide[:, :, 31] = col(v["L2_xattn_w"].reshape(-1))
    o["a2_wide"] = wide
    o["a2_cB"] = np.ascontiguousarray(np.broadcast_to(
        np.stack([col(v["L2_xattn_Wcw"].reshape(-1)), col(v["L2_xattn_Wcb"].reshape(-1))], 1)[:, :, :, None], (P, 2, KT, P)))
    o["a2_bc"] = every(np.concatenate([v["L2_xattn_bcw"], v["L2_xattn_bcb"]]))
    o["a2_qm"] = every(v["mask_BxS2_ik0"])
    o["f2_wg"], o["f2_wu"] = rows(inner(v["L2_ffn_Wg"])), rows(inner(v["L2_ffn_Wu"]))
    o["f2_wd"], o["f2_wr"] = rows(v["L2_ffn_Wd"].reshape(-1, D)), wide_router(v["L2_ffn_Wr"])
    o["f2_temp"] = every(v["L2_ffn_temperature"])
    o["f2_sel"] = np.kron(np.eye(8), np.ones((1, P))).reshape(8, 8, P).astype(np.float32)
    o["f3_w1"], o["f3_w2"] = rows(v["L3_ffn_w1"]), rows(v["L3_ffn_w2"])
    o["f3_b1"], o["f3_b2"] = col(v["L3_ffn_b1"]), col(v["L3_ffn_b2"])
    for k in (4, 8, 16):
        o[f"tri{k}"] = every(np.tril(np.ones((k, k), np.float32), -1))
    return o


def kernel(**inputs):
    import numpy as np
    import concourse.bacc as bacc
    from concourse.bass_utils import run_bass_kernel_spmd as run

    nc = bacc.Bacc("TRN2", target_bir_lowering=False, num_devices=1)
    arrays, d = {}, {}
    for name, a in layouts(inputs).items():
        arrays[f"in_{name}"] = a
        d[name] = nc.dram_tensor(f"in_{name}", a.shape, mybir.dt.from_np(a.dtype), kind="ExternalInput").ap()
    d["out"] = nc.dram_tensor("out_x", (B, S, D), F32, kind="ExternalOutput").ap()
    build(nc, d)
    return run(nc, [arrays], core_ids=[0]).results[0]["out_x"]
```
